# Optimizing a Trainium2 kernel written in Bass

```python
import numpy as np
import jax
import jax.numpy as jnp

def _softmax(x, axis=-1):
    return jax.nn.softmax(x, axis=axis)

def _gelu(x):
    return jax.nn.gelu(x, approximate=True)

def _silu(x):
    return jax.nn.silu(x)

def _sigmoid(x):
    return jax.nn.sigmoid(x)

def _layernorm(x, axis=-1, eps=1e-05):
    m = jnp.mean(x, axis=axis, keepdims=True)
    v = jnp.var(x, axis=axis, keepdims=True)
    return (x - m) / jnp.sqrt(v + eps)

def _scatter_add(tgt, idx, src, axis=0):
    return tgt.at[idx].add(src)

def _segment_sum(src, seg, n):
    return jax.ops.segment_sum(src, seg, n)
kernel_name = 'mk_decoder_postln_d1_seqx_r4_ea3815'

def setup_inputs(seed: int=0):
    np.random.seed(seed)
    _w = jnp.asarray

    def _rec_inputs():
        import jax
        import jax.numpy as jnp
        _rk = jax.random.key(seed)
        x = 7.22e-05 + 1 * jax.random.normal(jax.random.fold_in(_rk, 1), (32, 128, 256), jnp.float32)
        _lenS = 128 - jax.random.randint(jax.random.fold_in(_rk, 7), (32,), 0, max(1, 128 // 4) + 1, jnp.int32)
        _lenS2 = 128 - jax.random.randint(jax.random.fold_in(_rk, 8), (32,), 0, max(1, 128 // 4) + 1, jnp.int32)
        _ctx_1024P = jax.random.normal(jax.random.fold_in(_rk, 11), (32, 16, 256), jnp.float32)
        _ctx_1024c = jax.random.dirichlet(jax.random.fold_in(_rk, 511), 0.3 * jnp.ones((16,), jnp.float32), (32, 128))
        _ctx_1024t = jnp.einsum('bsk,bkd->bsd', _ctx_1024c, _ctx_1024P)
        _ctx_1024t = _ctx_1024t * jax.lax.rsqrt(jnp.mean(jnp.square(_ctx_1024t)) + 1e-12) * 0.953939
        ctx_1024 = 4.13588e-05 + 0.999923 * (_ctx_1024t + 0.3 * jax.random.normal(jax.random.fold_in(_rk, 611), (32, 128, 256), jnp.float32))
        return (x, ctx_1024)
    x, ctx_1024 = _rec_inputs()

    def _L0_attn_setup():
        import jax, jax.numpy as jnp
        import numpy as np
        B, T, C, NH = (8, 256, 256, 16)
        HD = C // NH
        EPS = 1e-05

        def _decay_mask(nh, t, dtype):
            gamma = 1.0 - 2.0 ** (-5.0 - jnp.arange(nh, dtype=jnp.float32))
            idx = jnp.arange(t)
            diff = idx[:, None] - idx[None, :]
            mask = diff >= 0
            pow_ = gamma[:, None, None] ** jnp.where(mask, diff, 0).astype(jnp.float32)
            return (jnp.where(mask[None], pow_, 0.0).astype(dtype), gamma.astype(dtype))

        def _reference_tuple_inner(x, past_kv, W_qkv, gn_weight, gn_bias):
            b, t, c = x.shape
            nh = gn_weight.shape[0]
            hd = c // nh
            qkv = x @ W_qkv
            q, k, v = jnp.split(qkv, 3, axis=2)
            split_heads = lambda u: u.reshape(b, t, nh, hd).transpose(0, 2, 1, 3)
            q, k, v = (split_heads(q), split_heads(k), split_heads(v))
            decay, gamma = _decay_mask(nh, t, x.dtype)
            ret = jnp.einsum('bhtd,bhsd->bhts', q, k) * decay
            inner = jnp.einsum('bhts,bhsd->bhtd', ret, v)
            inner_decay = float(nh * hd)
            cross = jnp.einsum('bhtd,hde->bhte', q, past_kv) * inner_decay
            r = inner + cross
            current_kv = gamma[:, None, None] * past_kv + jnp.einsum('bhtd,bhte->bhde', k, v)
            current_kv = current_kv.mean(axis=0)
            y = r.transpose(0, 1, 3, 2)
            mu = y.mean(axis=(1, 2, 3), keepdims=True)
            var = y.var(axis=(1, 2, 3), keepdims=True)
            yn = (y - mu) * jax.lax.rsqrt(var + EPS)
            yn = yn * gn_weight[None, :, None, None] + gn_bias[None, :, None, None]
            out = yn.transpose(0, 3, 1, 2).reshape(b, t, c)
            return (out, current_kv)
        key = jax.random.key(seed)
        k1, k2, k3 = jax.random.split(key, 3)
        x = jax.random.normal(k1, (B, T, C), dtype=jnp.float32)
        past_kv = jax.random.normal(k2, (NH, HD, HD), dtype=jnp.float32) * 0.1
        W_qkv = jax.random.normal(k3, (C, 3 * C), dtype=jnp.float32) * 0.02
        gn_weight = jnp.ones((NH,), dtype=jnp.float32)
        gn_bias = jnp.zeros((NH,), dtype=jnp.float32)
        return {'x': x, 'past_kv': past_kv, 'W_qkv': W_qkv, 'gn_weight': gn_weight, 'gn_bias': gn_bias}
    _L0_attn_all = _L0_attn_setup()
    _L0_attn_in = {k: v for k, v in _L0_attn_all.items() if k in ('past_kv', 'W_qkv', 'gn_weight', 'gn_bias')}
    del _L0_attn_all

    def _L0_xattn_setup():
        import jax, jax.numpy as jnp
        import numpy as np
        N_HEAD = 16
        key = jax.random.key(seed)
        ks = jax.random.split(key, 8)
        B, T, D = (4, 512, 256)
        s = 0.02
        return {'querys': jax.random.normal(ks[0], (B, T, D), jnp.float32), 'keys': jax.random.normal(ks[1], (B, T, D), jnp.float32), 'values': jax.random.normal(ks[2], (B, T, D), jnp.float32), 'Wq': jax.random.normal(ks[3], (D, D), jnp.float32) * s, 'Wk': jax.random.normal(ks[4], (D, D), jnp.float32) * s, 'Wv': jax.random.normal(ks[5], (D, D), jnp.float32) * s, 'Wo': jax.random.normal(ks[6], (D, D), jnp.float32) * s, 'bo': jnp.zeros((D,), jnp.float32)}
    _L0_xattn_all = _L0_xattn_setup()
    _L0_xattn_in = {k: v for k, v in _L0_xattn_all.items() if k in ('Wq', 'Wk', 'Wv', 'Wo', 'bo')}
    del _L0_xattn_all

    def _L0_ffn_setup():
        import math
        import jax, jax.numpy as jnp
        import numpy as np
        TOP_K = 2
        _GELU_C = math.sqrt(2.0 / math.pi)

        def gelu_new(x):
            return 0.5 * x * (1.0 + jnp.tanh(_GELU_C * (x + 0.044715 * x * x * x)))
        key = jax.random.key(seed)
        ks = jax.random.split(key, 6)
        B, T, C, E, H = (2, 512, 256, 8, 1024)
        s_in = 1.0 / math.sqrt(C)
        s_hid = 1.0 / math.sqrt(H)
        return {'x': jax.random.normal(ks[0], (B, T, C), dtype=jnp.float32), 'router_w': jax.random.normal(ks[1], (E, C), dtype=jnp.float32) * s_in, 'w_fc': jax.random.normal(ks[2], (E, C, H), dtype=jnp.float32) * s_in, 'b_fc': jax.random.normal(ks[3], (E, H), dtype=jnp.float32) * 0.02, 'w_proj': jax.random.normal(ks[4], (E, H, C), dtype=jnp.float32) * s_hid, 'b_proj': jax.random.normal(ks[5], (E, C), dtype=jnp.float32) * 0.02}
    _L0_ffn_all = _L0_ffn_setup()
    _L0_ffn_in = {k: v for k, v in _L0_ffn_all.items() if k in ('router_w', 'w_fc', 'b_fc', 'w_proj', 'b_proj')}
    del _L0_ffn_all
    return {'x': x, 'ctx_1024': ctx_1024, 'L0_attn_past_kv': _L0_attn_in['past_kv'], 'L0_attn_W_qkv': _L0_attn_in['W_qkv'], 'L0_attn_gn_weight': _L0_attn_in['gn_weight'], 'L0_attn_gn_bias': _L0_attn_in['gn_bias'], 'L0_xattn_Wq': _L0_xattn_in['Wq'], 'L0_xattn_Wk': _L0_xattn_in['Wk'], 'L0_xattn_Wv': _L0_xattn_in['Wv'], 'L0_xattn_Wo': _L0_xattn_in['Wo'], 'L0_xattn_bo': _L0_xattn_in['bo'], 'L0_ffn_router_w': _L0_ffn_in['router_w'], 'L0_ffn_w_fc': _L0_ffn_in['w_fc'], 'L0_ffn_b_fc': _L0_ffn_in['b_fc'], 'L0_ffn_w_proj': _L0_ffn_in['w_proj'], 'L0_ffn_b_proj': _L0_ffn_in['b_proj']}

def reference(x, ctx_1024, L0_attn_past_kv, L0_attn_W_qkv, L0_attn_gn_weight, L0_attn_gn_bias, L0_xattn_Wq, L0_xattn_Wk, L0_xattn_Wv, L0_xattn_Wo, L0_xattn_bo, L0_ffn_router_w, L0_ffn_w_fc, L0_ffn_b_fc, L0_ffn_w_proj, L0_ffn_b_proj):
    import jax
    import jax.numpy as jnp

    def _L0_attn_ref(x, past_kv, W_qkv, gn_weight, gn_bias):
        import jax, jax.numpy as jnp
        import numpy as np
        B, T, C, NH = (8, 256, 256, 16)
        HD = C // NH
        EPS = 1e-05

        def _decay_mask(nh, t, dtype):
            gamma = 1.0 - 2.0 ** (-5.0 - jnp.arange(nh, dtype=jnp.float32))
            idx = jnp.arange(t)
            diff = idx[:, None] - idx[None, :]
            mask = diff >= 0
            pow_ = gamma[:, None, None] ** jnp.where(mask, diff, 0).astype(jnp.float32)
            return (jnp.where(mask[None], pow_, 0.0).astype(dtype), gamma.astype(dtype))

        def _reference_tuple_inner(x, past_kv, W_qkv, gn_weight, gn_bias):
            b, t, c = x.shape
            nh = gn_weight.shape[0]
            hd = c // nh
            qkv = x @ W_qkv
            q, k, v = jnp.split(qkv, 3, axis=2)
            split_heads = lambda u: u.reshape(b, t, nh, hd).transpose(0, 2, 1, 3)
            q, k, v = (split_heads(q), split_heads(k), split_heads(v))
            decay, gamma = _decay_mask(nh, t, x.dtype)
            ret = jnp.einsum('bhtd,bhsd->bhts', q, k) * decay
            inner = jnp.einsum('bhts,bhsd->bhtd', ret, v)
            inner_decay = float(nh * hd)
            cross = jnp.einsum('bhtd,hde->bhte', q, past_kv) * inner_decay
            r = inner + cross
            current_kv = gamma[:, None, None] * past_kv + jnp.einsum('bhtd,bhte->bhde', k, v)
            current_kv = current_kv.mean(axis=0)
            y = r.transpose(0, 1, 3, 2)
            mu = y.mean(axis=(1, 2, 3), keepdims=True)
            var = y.var(axis=(1, 2, 3), keepdims=True)
            yn = (y - mu) * jax.lax.rsqrt(var + EPS)
            yn = yn * gn_weight[None, :, None, None] + gn_bias[None, :, None, None]
            out = yn.transpose(0, 3, 1, 2).reshape(b, t, c)
            return (out, current_kv)
        return _reference_tuple_inner(x, past_kv, W_qkv, gn_weight, gn_bias)[0]

    def _L0_xattn_ref(querys, keys, values, Wq, Wk, Wv, Wo, bo):
        import jax, jax.numpy as jnp
        import numpy as np
        N_HEAD = 16
        B, T, D = querys.shape
        H = N_HEAD
        Hd = D // H

        def split(x, W):
            return (x @ W.T).reshape(B, T, H, Hd).transpose(0, 2, 1, 3)
        q = split(querys, Wq)
        k = split(keys, Wk)
        v = split(values, Wv)
        scale = 1.0 / jnp.sqrt(jnp.array(Hd, jnp.float32))
        scores = jnp.einsum('bhqd,bhkd->bhqk', q, k) * scale
        causal = jnp.tril(jnp.ones((T, T), bool))
        scores = jnp.where(causal[None, None], scores, -jnp.inf)
        weights = jax.nn.softmax(scores, axis=-1)
        attn = jnp.einsum('bhqk,bhkd->bhqd', weights, v)
        out = attn.transpose(0, 2, 1, 3).reshape(B, T, D)
        return out @ Wo.T + bo

    def _L0_ffn_ref(x, router_w, w_fc, b_fc, w_proj, b_proj):
        import math
        import jax, jax.numpy as jnp
        import numpy as np
        TOP_K = 2
        _GELU_C = math.sqrt(2.0 / math.pi)

        def gelu_new(x):
            return 0.5 * x * (1.0 + jnp.tanh(_GELU_C * (x + 0.044715 * x * x * x)))
        B, T, C = x.shape
        E = router_w.shape[0]
        N = B * T
        xf = x.reshape(N, C)
        logits = xf @ router_w.T
        probs = jax.nn.softmax(logits, axis=-1)
        topk_probs, topk_idx = jax.lax.top_k(probs, TOP_K)
        topk_probs = topk_probs / jnp.sum(topk_probs, axis=-1, keepdims=True)
        combine = jnp.zeros((N, E), dtype=x.dtype).at[jnp.arange(N)[:, None], topk_idx].add(topk_probs)
        h = gelu_new(jnp.einsum('nc,ech->neh', xf, w_fc) + b_fc)
        out = jnp.einsum('neh,ehc->nec', h, w_proj) + b_proj
        y = jnp.einsum('nec,ne->nc', out, combine)
        return y.reshape(B, T, C)
    x = _layernorm(x + _L0_attn_ref(x, L0_attn_past_kv, L0_attn_W_qkv, L0_attn_gn_weight, L0_attn_gn_bias), axis=-1)
    x = _layernorm(x + _L0_xattn_ref(x, ctx_1024, ctx_1024, L0_xattn_Wq, L0_xattn_Wk, L0_xattn_Wv, L0_xattn_Wo, L0_xattn_bo), axis=-1)
    x = _layernorm(x + _L0_ffn_ref(x, L0_ffn_router_w, L0_ffn_w_fc, L0_ffn_b_fc, L0_ffn_w_proj, L0_ffn_b_proj), axis=-1)
    return x

_drawn_inputs = setup_inputs


def setup_inputs(seed=0):
    import zlib

    import numpy as np

    out = dict(_drawn_inputs(seed))
    spreads = {'L0_attn_gn_weight': (1.0, 0.2), 'L0_attn_gn_bias': (0.0, 0.1), 'L0_xattn_bo': (0.0, 0.1)}
    factors = {'L0_xattn_Wq': 4.995, 'L0_xattn_Wk': 4.064, 'L0_ffn_b_fc': 6.16, 'L0_ffn_b_proj': 4.087}
    for name, (base, spread) in spreads.items():
        noise = np.random.default_rng([zlib.crc32(name.encode()), seed]).standard_normal(out[name].shape)
        drawn = base * np.exp(spread * noise) if base else spread * noise
        out[name] = jnp.asarray(drawn.astype(out[name].dtype))
    for name, factor in factors.items():
        out[name] = (out[name] * factor).astype(out[name].dtype)
    return out
```

```python
import concourse.bass as bass
from concourse import mybir
from contextlib import ExitStack
import numpy as np

B, T, C = 32, 128, 256
N_TOK = B * T
NH, HD = 16, 16
E, H = 8, 1024
P = 128
NCH = C // P
HPC = P // HD
QH = 4
NQ = NH // QH
HC = H // P
SLOT = 256
HALVES = SLOT // P
ROW = C + 2
CAP = N_TOK + SLOT
EPS = 1e-5
SCALE = 1.0 / float(np.sqrt(HD))
CROSS = float(NH * HD)
NEG = -1.0e30
LEAD = 8
ROUND = 4
DRAIN = 4


class At:

    def __init__(self, loop, k):
        self.n = ROUND * loop + k
        self.r = k % ROUND
        self.g = loop + k // ROUND
        self.fixed = isinstance(loop, int)

    def exists(self):
        return not self.fixed or 0 <= self.n < B


class Chain:

    def __init__(self, eng, sem, base):
        self.eng, self.sem, self.base, self.k = eng, sem, base, 0

    def link(self, ins, then=None):
        ins.then_inc(self.sem, 1)
        self.k += 1
        self.eng.wait_ge(self.sem, self.base + self.k)
        if then:
            then(self.eng)


def decoder_kernel(nc, x, ctx_in, kv_blocks, w_qkv, gn_scale, gn_shift, wq_t, wk_t, wv_t, wo_t, bo,
                   router_t, w_fc, b_fc, w_proj, b_proj, decay_c, small_c, bits_c, out):
    f32, f32r, bf16 = mybir.dt.float32, mybir.dt.float32r, mybir.dt.bfloat16
    i32, u32 = mybir.dt.int32, mybir.dt.uint32
    ALU, ACT, AX = mybir.AluOpType, mybir.ActivationFunctionType, mybir.AxisListType
    ds = bass.ds

    ctx = ExitStack()
    with ctx:
        def sb(name, shape, dt=f32):
            return ctx.enter_context(nc.sbuf_tensor(name, shape, dt))

        attention = ExitStack()

        def ab(name, shape, dt=f32):
            return attention.enter_context(nc.sbuf_tensor(name, shape, dt))

        def sem(name):
            return ctx.enter_context(nc.semaphore(name))

        sent = nc.dram_tensor("sent_rows", [E, CAP, ROW], f32, kind="Internal").ap()
        sent_flat = sent.rearrange("e r c -> (e r) c")
        total = nc.dram_tensor("residual_sum", [N_TOK + P, C], f32, kind="Internal").ap()

        small = sb("small", [P, small_c.shape[1]])
        bits = sb("bits", [P, 4 * P], bf16)
        bfc_s = sb("bfc_s", [P, E, HC])
        bproj_s = sb("bproj_s", [P, E, C])
        x2_row = [[sb(f"x2_row{i}_{k}", [P, ROW]) for k in range(2)] for i in range(2)]
        pos = [sb(f"pos{i}", [P, 2], u32) for i in range(2)]
        filled = sb("filled", [P, E])
        tab_f = sb("tab_f", [1, 4, E])
        tab_i = sb("tab_i", [1, 4, E], i32)

        WROW = NCH * H + HC * C
        w_raw = sb("w_raw", [P, WROW])
        w_hi0 = sb("w_hi0", [P, WROW], f32r)

        decay = ab("decay", [P, NH, T])
        ident, mean_w = small[:, 0:P], small[:, P:2 * P]
        head_mask = small[:, 2 * P:2 * P + HPC]
        region = small[:, 2 * P + 8:2 * P + 16]
        lanes8 = small[:, 2 * P + 16:2 * P + 24]
        lane = small[:, 2 * P + 24:2 * P + 25]
        half_neg = small[:, 2 * P + 25:2 * P + 29]
        pad_row = small[:, 2 * P + 32:2 * P + 32 + ROW]
        ident_b, causal_b, before_b, ones_b = (bits[:, i * P:(i + 1) * P] for i in range(4))
        wqkv_s = ab("wqkv_s", [P, NCH, 3 * C])
        wq_s = ab("wq_s", [P, NCH, C])
        wk_s = ab("wk_s", [P, NCH, C])
        wv_s = ab("wv_s", [P, NCH, C])
        wo_s = ab("wo_s", [P, NCH, C])
        bo_s = ab("bo_s", [P, C])
        rt_s = ab("rt_s", [P, NCH, E])
        kvb_raw = ab("kvb_raw", [P, NCH, P])
        kvb = ab("kvb", [P, NCH, P])
        gnw = ab("gnw", [P, NCH])
        gnb = ab("gnb", [P, NCH])

        bits_f = ab("bits_f", [P, 4 * P])

        x_t = [ab(f"x_t{i}", [P, C]) for i in range(4)]
        c_t = [ab(f"c_t{i}", [P, C]) for i in range(4)]
        xcT = ab("xcT", [P, 2, NCH, T])
        qkT = [ab(f"qkT{i}", [P, 2, NCH, T]) for i in range(2)]
        v_ret = [ab(f"v_ret{i}", [P, NH, P]) for i in range(2)]
        v_att = [ab(f"v_att{i}", [P, NH, P]) for i in range(4)]
        kxT = [ab(f"kxT{i}", [P, NCH, T]) for i in range(4)]
        q_mask = [ab(f"q_mask{i}", [P, NH, T]) for i in range(2)]
        k_mask = [ab(f"k_mask{i}", [P, NH, T]) for i in range(2)]
        ret_p = [ab(f"ret_p{i}", [P, QH, T]) for i in range(2)]
        att_p = [ab(f"att_p{i}", [P, QH, T]) for i in range(2)]
        att_pT = [ab(f"att_pT{i}", [P, QH, T]) for i in range(2)]
        y_raw = ab("y_raw", [P, NCH, T])
        yT = ab("yT", [P, NCH, T])
        gst = ab("gst", [P, 6])
        gmv = ab("gmv", [P, 2])
        gsum = ab("gsum", [P, 2])
        gtot = ab("gtot", [P, 2])
        gsq = ab("gsq", [P, 1])
        gvar = ab("gvar", [P, 1])
        grstd = ab("grstd", [P, 1])
        gmul = ab("gmul", [P, NCH])
        gadd = ab("gadd", [P, NCH])
        x1_pre = ab("x1_pre", [P, C])
        l1st = ab("l1st", [P, 6])
        l1mv = ab("l1mv", [P, 2])
        l1var = ab("l1var", [P, 1])
        l1rstd = ab("l1rstd", [P, 1])
        x1 = ab("x1", [P, C])
        x1_bo = [ab(f"x1_bo{i}", [P, C]) for i in range(4)]
        x1T = ab("x1T", [P, NCH, T])
        qxT = ab("qxT", [P, NCH, T])
        row_max = [ab(f"row_max{i}", [P, NH]) for i in range(2)]
        neg_max = [ab(f"neg_max{i}", [P, NH]) for i in range(2)]
        den = [ab(f"den{i}", [P, NH]) for i in range(2)]
        rden = ab("rden", [P, NH])
        rden_x = ab("rden_x", [P, C])
        rdT = ab("rdT", [P, NCH, T])
        attT = ab("attT", [P, NCH, T])
        x2_pre = ab("x2_pre", [P, C])
        l2st = ab("l2st", [P, 6])
        l2mv = ab("l2mv", [P, 2])
        l2var = ab("l2var", [P, 1])
        l2rstd = ab("l2rstd", [P, 1])
        x2T = ab("x2T", [P, NCH, T])
        lg = ab("lg", [P, E])
        top = ab("top", [P, 8])
        top_i = ab("top_i", [P, 8], u32)
        top_f = ab("top_f", [P, 2])
        hot = ab("hot", [P, 2, E])
        hot_b = ab("hot_b", [P, E], bf16)
        gap = ab("gap", [P, 1])
        gap_e = ab("gap_e", [P, 1])
        gap_s = ab("gap_s", [P, 1])
        place = ab("place", [P, E])
        place2 = ab("place2", [P, 2, E])
        pos_f = ab("pos_f", [P, 2])
        tok = ab("tok", [P, 1])

        attention.close()

        w_hi = [w_hi0, sb("w_hi1", [P, WROW], f32r)]
        w_lo = [sb(f"w_lo{i}", [P, WROW], f32r) for i in range(2)]

        rows = sb("rows", [P, HALVES, ROW])
        meta_next = sb("meta_next", [P, HALVES, 2])
        meta = sb("meta", [P, HALVES, 2])
        meta_i = sb("meta_i", [P, HALVES], u32)
        h_f = [sb(f"h_f{i}", [P, SLOT]) for i in range(2)]
        h_hi = [sb(f"h_hi{i}", [P, SLOT], f32r) for i in range(4)]
        h_lo = [sb(f"h_lo{i}", [P, SLOT], f32r) for i in range(4)]
        xs_hi = sb("xs_hi", [P, NCH, SLOT], f32r)
        xs_lo = sb("xs_lo", [P, NCH, SLOT], f32r)
        y_b = sb("y_b", [P, HALVES, C])
        y_w = sb("y_w", [P, HALVES, C])

        NLAST = N_TOK // (4 * P)
        last_in = [sb(f"last_in{i}", [P, 4, C]) for i in range(2)]
        last_out = [sb(f"last_out{i}", [P, 4, C]) for i in range(2)]
        last_nm = sb("last_nm", [P, 2, 4])
        last_rs = sb("last_rs", [P, 2, 4])
        last_st = sb("last_st", [P, 4, 6])
        last_mv = sb("last_mv", [P, 2, 4, 2])
        last_ve = sb("last_ve", [P, 2, 4])

        bank = [ctx.enter_context(nc.psum_tensor(f"bank{i}", [P, 512], f32)) for i in range(8)]
        ps_ret, ps_att, ps_attT, ps_y, ps_o, ps_prep, bank_g, bank_f = bank
        ps_g, ps_f = bank_g[:, 0:C], bank_f[:, 0:C]
        ps_h = bank[0:4]
        ps_out = bank[4:6]
        ps_xs = bank[6]

        names = """consts kvb_scaled zeroed cleared
            prep_T prep_T_out prep_qk qk_out prep_v v_out prep_kx kx_out
            q_masked k_masked ret_scores ret_decayed ret_done y_out
            gn_chain gn_mean gn_sums gn_var gn_rstd gn_coef gn_applied y_back
            ln1_chain ln1_var ln1_rstd x1_done x1_bo_done x1_T x1_T_out qx qx_out
            att_scores att_max nm_chain att_exp att_turned att_turned_out att_done
            rden_done rden_x_done rden_T rdT_out att_norm att_proj
            ln2_chain ln2_var ln2_rstd x2_done x2_T x2_T_out logits
            top_chain gap_done gap_exp picked ranked placed rows_stored
            tab_chain tab_ready raw_split raw_hi w_ready chain_first
            rows_turned rows_in xs_chain xs_ready fc_done h_done h_chain h_split
            y_done y_chain y_biased y_weighted meta_ready last_chain last_var last_rstd_raw last_rstd last_act last_dve
            pool_small passed""".split()
        s = {k: sem(k) for k in names}
        s_load = [sem(f"loaded{i}") for i in range(4)]
        s_sent = [sem(f"sent{i}") for i in range(2)]
        s_total = [sem(f"total_stored{i}") for i in range(2)]
        s_pad = sem("pad_filled")
        s_wraw = sem("weights_loaded")
        s_rows = sem("rows_loaded")
        s_added = sem("rows_added")
        s_last = [sem(f"last_loaded{i}") for i in range(2)]
        s_stored = [sem(f"out_stored{i}") for i in range(2)]

        CONSTS = 15
        EVER = 1
        GN, LN1, LN2, TOP = 6, 3, 3, 12

        def steps(eng, step):
            for k in range(LEAD):
                step(0, k)
            with eng.Fori(LEAD // ROUND, B // ROUND) as loop:
                for k in range(ROUND):
                    step(loop, k)
            for k in range(B, B + DRAIN):
                step(0, k)

        def experts(eng, body):
            with eng.Fori(0, E // 2 - 1) as pair:
                for k in range(2):
                    body(2 * pair + k, k, True, True)
            body(E - 2, 0, True, False)
            body(E - 1, 1, False, False)

        def first(c, k):
            return c.fixed and c.n < k

        def diagonal(flat):
            wide = flat[:, 0:HPC * P]
            step = P + HD
            head = wide[:, 0:HD]
            return bass.AP(head.tensor, head.offset, [list(head.ap[0]), [step, HPC], [1, HD]])

        def apart(eng):
            eng.sem_inc(s["passed"], 1)

        block = ctx.enter_context(nc.Block())

        @block.sync
        def _(sp):
            def load(c):
                if not first(c, 4):
                    sp.wait_ge(s["ln1_chain"], LN1 * (c.n - 4) + 1)
                    apart(sp)
                    sp.wait_ge(s["prep_T"], c.n - 3)
                    apart(sp)
                sp.dma_start(x_t[c.r][:, :], x[ds(c.n, 1), :, :].rearrange("b t c -> (b t) c"))\
                    .then_inc(s_load[c.r], 16)
                sp.dma_start(c_t[c.r][:, :], ctx_in[ds(c.n, 1), :, :].rearrange("b t c -> (b t) c"))\
                    .then_inc(s_load[c.r], 16)

            def store_total(c):
                sp.wait_ge(s["x2_done"], c.n + 1)
                apart(sp)
                sp.dma_start(total[ds(c.n * T, T), :], x2_row[c.r % 2][0][:, 0:C])\
                    .then_inc(s_total[c.r % 2], 16)

            load(At(0, 0))
            sp.dma_start(small[:, :], small_c).then_inc(s["consts"], 16)
            sp.dma_start(wqkv_s[:, :, :], w_qkv.rearrange("(k p) n -> p k n", p=P)).then_inc(s["consts"], 16)
            sp.dma_start(wv_s[:, :, :], wv_t.rearrange("(k p) n -> p k n", p=P)).then_inc(s["consts"], 16)
            sp.dma_start(wk_s[:, :, :], wk_t.rearrange("(k p) n -> p k n", p=P)).then_inc(s["consts"], 16)
            load(At(0, 1))
            sp.dma_start(bits_f[:, :], bits_c).then_inc(s["consts"], 16)
            sp.dma_start(decay[:, :, :], decay_c).then_inc(s["consts"], 16)
            sp.dma_start(kvb_raw[:, :, :], kv_blocks.rearrange("k p n -> p k n")).then_inc(s["consts"], 16)
            sp.dma_start(gnw[:, :], gn_scale).then_inc(s["consts"], 16)
            sp.dma_start(gnb[:, :], gn_shift).then_inc(s["consts"], 16)
            sp.dma_start(wq_s[:, :, :], wq_t.rearrange("(k p) n -> p k n", p=P)).then_inc(s["consts"], 16)
            sp.dma_start(wo_s[:, :, :], wo_t.rearrange("(k p) n -> p k n", p=P)).then_inc(s["consts"], 16)
            sp.dma_start(bo_s[:, :], bo.partition_broadcast(P)).then_inc(s["consts"], 16)
            sp.dma_start(rt_s[:, :, :], router_t.rearrange("(k p) n -> p k n", p=P)).then_inc(s["consts"], 16)
            sp.dma_start(bfc_s[:, :, :], b_fc).then_inc(s["consts"], 16)
            sp.dma_start(bproj_s[:, :, :].rearrange("p e c -> p (e c)"),
                         b_proj.rearrange("e c -> (e c)").partition_broadcast(P)).then_inc(s["consts"], 16)
            load(At(0, 2))

            def load_weights(e):
                sp.dma_start(w_raw[:, 0:NCH * H].rearrange("p (k n) -> p k n", k=NCH),
                             w_fc[ds(e, 1), :, :].rearrange("e (k p) n -> p (e k) n", p=P))\
                    .then_inc(s_wraw, 16)
                sp.dma_start(w_raw[:, NCH * H:WROW].rearrange("p (k n) -> p k n", k=HC),
                             w_proj[ds(e, 1), :, :].rearrange("e (k p) n -> p (e k) n", p=P))\
                    .then_inc(s_wraw, 16)

            load_weights(0)

            def step(loop, k):
                c = At(loop, k + 3)
                if c.exists():
                    load(c)
                c = At(loop, k - 3)
                if c.exists():
                    store_total(c)

            for k in range(LEAD):
                step(0, k)
            with sp.Fori(LEAD // ROUND, B // ROUND - 1) as loop:
                for k in range(ROUND):
                    step(loop, k)
            for k in range(B - ROUND, B + DRAIN):
                step(0, k)

            sp.wait_ge(s["tab_ready"], 1)
            for e in range(E):
                cnt = sp.value_load(tab_i[0:1, 2, e:e + 1], min_val=0, max_val=N_TOK)
                for half in range(HALVES):
                    sp.dma_start(sent[e, ds(cnt + half * P, P), :], pad_row).then_inc(s_pad, 16)
            sp.wait_ge(s_pad, 16 * E * HALVES)
            sp.wait_ge(s["raw_split"], 1)
            load_weights(1)
            for par in range(2):
                sp.wait_ge(s_sent[par], 16 * B)

            def expert(e, par, has_next, has_after):
                n_slots = sp.value_load(tab_i[0:1, 0, ds(e, 1)], min_val=1, max_val=N_TOK // SLOT)
                before = sp.value_load(tab_i[0:1, 1, ds(e, 1)], min_val=0, max_val=(2 * N_TOK) // SLOT + E)
                with sp.Fori(0, n_slots) as j:
                    sp.wait_ge(s["rows_turned"], before + j + EVER)
                    sp.wait_ge(s["meta_ready"], before + j + EVER)
                    apart(sp)
                    sp.dma_start(rows[:, :, :],
                                 sent[ds(e, 1), ds(j * SLOT, SLOT), :].rearrange("e (h p) c -> p (e h) c", p=P))\
                        .then_inc(s_rows, 16)
                if has_after:
                    sp.wait_ge(s["raw_split"], e + 2)
                    apart(sp)
                    load_weights(e + 2)

            experts(sp, expert)
            n_all = sp.value_load(tab_i[0:1, 3, 0:1], min_val=E, max_val=(2 * N_TOK) // SLOT + E)
            sp.wait_ge(s["rows_turned"], n_all + EVER)
            sp.wait_ge(s["meta_ready"], n_all + EVER)
            sp.dma_start(rows[:, :, :], sent[0, 0:SLOT, :].rearrange("(h p) c -> p h c", p=P)).then_inc(s_rows, 16)

            total_v = total[0:N_TOK, :].rearrange("(b p j) c -> b p j c", p=P, j=4)
            out_v = out.rearrange("b t c -> (b t) c").rearrange("(b p j) c -> b p j c", p=P, j=4)
            n_add = sp.value_load(tab_i[0:1, 3, 1:2], min_val=E, max_val=32 * ((2 * N_TOK) // SLOT + E))
            sp.wait_ge(s_added, n_add + 16 * EVER)
            for b in range(2):
                sp.dma_start(last_in[b][:, :, :], total_v[b]).then_inc(s_last[b], 16)
            for b in range(NLAST):
                sp.wait_ge(s["last_act"], 2 * (b + 1))
                sp.wait_ge(s["last_dve"], 2 * (b + 1))
                sp.dma_start(out_v[b], last_out[b % 2][:, :, :]).then_inc(s_stored[b % 2], 16)
                if b + 2 < NLAST:
                    sp.dma_start(last_in[b % 2][:, :, :], total_v[b + 2]).then_inc(s_last[b % 2], 16)
            for par in range(2):
                sp.wait_ge(s_stored[par], 16 * (NLAST // 2))


        @block.tensor
        def _(pe):
            mm, tr = nc.tensor.matmul, nc.tensor.transpose

            def prep_turn(c):
                pe.wait_ge(s_load[c.r], 32 * (c.g + 1))
                if not first(c, 1):
                    pe.wait_ge(s["kx_out"], c.n)
                for i, src in enumerate((x_t[c.r], c_t[c.r])):
                    for k in range(NCH):
                        at = (i * NCH + k) * P
                        last = tr(ps_prep[:, at:at + P], src[:, k * P:(k + 1) * P], ident)
                last.then_inc(s["prep_T"], 1)

            def prep_qk(c):
                pe.wait_ge(s["prep_T_out"], c.n + 1)
                for m in range(2 * NCH):
                    for k in range(NCH):
                        last = mm(ps_prep[:, m * P:(m + 1) * P], wqkv_s[:, k, m * P:(m + 1) * P],
                                  xcT[:, 0, k, :], start=(k == 0), stop=(k == NCH - 1))
                last.then_inc(s["prep_qk"], 1)

            def prep_v(c):
                pe.wait_ge(s["qk_out"], c.n + 1)
                for i, w in enumerate((wqkv_s[:, :, 2 * C:3 * C], wv_s[:, :, :])):
                    for k in range(NCH):
                        last = mm(ps_prep[:, i * C:(i + 1) * C], xcT[:, i, k, :], w[:, k, :],
                                  start=(k == 0), stop=(k == NCH - 1))
                last.then_inc(s["prep_v"], 1)

            def prep_kx(c):
                pe.wait_ge(s["v_out"], c.n + 1)
                for m in range(NCH):
                    for k in range(NCH):
                        last = mm(ps_prep[:, m * P:(m + 1) * P], wk_s[:, k, m * P:(m + 1) * P],
                                  xcT[:, 1, k, :], start=(k == 0), stop=(k == NCH - 1))
                last.then_inc(s["prep_kx"], 1)

            def ret_scores(c, q):
                if q % 2 == 0:
                    pe.wait_ge(s["q_masked"], 2 * c.n + q // 2 + 1)
                if not (c.fixed and 4 * c.n + q < 1):
                    pe.wait_ge(s["ret_decayed"], 4 * c.n + q)
                mm(ps_ret[:, :], qkT[c.r % 2][:, 1, q // 2, :],
                   q_mask[c.r % 2][:, QH * q:QH * (q + 1), :].rearrange("p h t -> p (h t)"),
                   start=True, stop=True).then_inc(s["ret_scores"], 1)

            def ret_values(c, q):
                pe.wait_ge(s["ret_decayed"], 4 * c.n + q + 1)
                k = q // 2
                o = ps_y[:, k * P:(k + 1) * P]
                if q == 0 and not first(c, 1):
                    pe.wait_ge(s["y_out"], c.n)
                if q % 2 == 0:
                    mm(o, kvb[:, k, :], qkT[c.r % 2][:, 0, k, :], start=True, stop=False)
                for i in range(QH):
                    last = mm(o, v_ret[c.r % 2][:, QH * q + i, :], ret_p[q % 2][:, i, :],
                              start=False, stop=(q % 2 == 1 and i == QH - 1))
                last.then_inc(s["ret_done"], 1)

            def att_scores(c, q):
                if q == 0:
                    pe.wait_ge(s["qx_out"], c.n + 1)
                if q % 2 == 0:
                    pe.wait_ge(s["k_masked"], 2 * c.n + q // 2 + 1)
                if not (c.fixed and c.n == 0 and q == 0):
                    pe.wait_ge(s["att_exp"], 4 * c.n + q)
                mm(ps_att[:, :], qxT[:, q // 2, :],
                   k_mask[c.r % 2][:, QH * q:QH * (q + 1), :].rearrange("p h t -> p (h t)"),
                   start=True, stop=False)
                mm(ps_att[:, :], ident_b, causal_b.unsqueeze(1).to_broadcast([P, QH, T]),
                   start=False, stop=True).then_inc(s["att_scores"], 1)

            def att_turn(c, q):
                pe.wait_ge(s["att_exp"], 4 * c.n + q + 1)
                if not (c.fixed and c.n == 0 and q == 0):
                    pe.wait_ge(s["att_turned_out"], 4 * c.n + q)
                for i in range(QH):
                    last = tr(ps_attT[:, i * P:(i + 1) * P], att_p[q % 2][:, i, :], ident)
                last.then_inc(s["att_turned"], 1)

            def att_values(c, q):
                pe.wait_ge(s["att_turned_out"], 4 * c.n + q + 1)
                k = q // 2
                if q == 0 and not first(c, 1):
                    pe.wait_ge(s["att_norm"], c.n)
                for i in range(QH):
                    last = mm(ps_o[:, k * P:(k + 1) * P], v_att[c.r][:, QH * q + i, :],
                              att_pT[q % 2][:, i, :], start=(q % 2 == 0 and i == 0),
                              stop=(q % 2 == 1 and i == QH - 1))
                last.then_inc(s["att_done"], 1)

            def gn_mean(c):
                pe.wait_ge(s["gn_sums"], c.n + 1)
                if not first(c, 1):
                    pe.wait_ge(s["qx_out"], c.n)
                if not first(c, 2):
                    pe.wait_ge(s["rdT_out"], c.n - 1)
                mm(ps_g[:, 0:2], mean_w, gsum[:, :], start=True, stop=True).then_inc(s["gn_mean"], 1)

            def y_back(c):
                pe.wait_ge(s["gn_applied"], c.n + 1)
                for k in range(NCH):
                    last = tr(ps_g[:, k * P:(k + 1) * P], yT[:, k, :], ident)
                last.then_inc(s["y_back"], 1)

            def x1_turn(c):
                pe.wait_ge(s["x1_done"], c.n + 1)
                for k in range(NCH):
                    last = tr(ps_g[:, k * P:(k + 1) * P], x1[:, k * P:(k + 1) * P], ident)
                last.then_inc(s["x1_T"], 1)

            def qx(c):
                pe.wait_ge(s["x1_T_out"], c.n + 1)
                for m in range(NCH):
                    for k in range(NCH):
                        last = mm(ps_g[:, m * P:(m + 1) * P], wq_s[:, k, m * P:(m + 1) * P], x1T[:, k, :],
                                  start=(k == 0), stop=(k == NCH - 1))
                last.then_inc(s["qx"], 1)

            def rden_turn(c):
                pe.wait_ge(s["rden_x_done"], c.n + 1)
                if not (c.fixed and c.n + 1 >= B):
                    pe.wait_ge(s["qx_out"], c.n + 2)
                else:
                    pe.wait_ge(s["rdT_out"], c.n)
                for k in range(NCH):
                    last = tr(ps_g[:, k * P:(k + 1) * P], rden_x[:, k * P:(k + 1) * P], ident)
                last.then_inc(s["rden_T"], 1)

            def att_proj(c):
                pe.wait_ge(s["att_norm"], c.n + 1)
                if not first(c, 1):
                    pe.wait_ge(s["placed"], c.n)
                for k in range(NCH):
                    last = mm(ps_f, attT[:, k, :], wo_s[:, k, :], start=(k == 0), stop=(k == NCH - 1))
                last.then_inc(s["att_proj"], 1)

            def x2_turn(c):
                pe.wait_ge(s["x2_done"], c.n + 1)
                for k in range(NCH):
                    last = tr(ps_f[:, k * P:(k + 1) * P], x2_row[c.r % 2][0][:, k * P:(k + 1) * P], ident)
                last.then_inc(s["x2_T"], 1)

            def logits(c):
                pe.wait_ge(s["x2_T_out"], c.n + 1)
                for k in range(NCH):
                    last = mm(ps_f[:, 0:E], x2T[:, k, :], rt_s[:, k, :], start=(k == 0), stop=(k == NCH - 1))
                last.then_inc(s["logits"], 1)

            def rank(c):
                pe.wait_ge(s["picked"], c.n + 1)
                mm(ps_f[:, 0:E], before_b, hot_b[:, :], start=True, stop=True)
                mm(ps_f[:, E:2 * E], ones_b, hot_b[:, :], start=True, stop=True).then_inc(s["ranked"], 1)

            def run(stage, c, *more):
                if c.exists():
                    stage(c, *more)

            prep = [prep_turn, prep_qk, prep_v, prep_kx]

            def step(loop, k):
                for q in range(NQ):
                    back = At(loop, k - 1 if q == 0 else k)
                    back_x = At(loop, k - 3 if q == 0 else k - 2)
                    back_v = At(loop, k - 3 if q < 2 else k - 2)
                    if q == 0:
                        run(qx, At(loop, k - 2))
                        run(logits, At(loop, k - 4))
                    run(ret_scores, At(loop, k), q)
                    run(prep[q], At(loop, k + 1))
                    run(att_scores, At(loop, k - 2), q)
                    run(ret_values, back, (q - 1) % NQ)
                    if q == 1:
                        run(gn_mean, At(loop, k - 1))
                        run(rank, At(loop, k - 4))
                    run(att_values, back_v, (q - 2) % NQ)
                    if q == 0:
                        run(rden_turn, At(loop, k - 3))
                    if q == 2:
                        run(y_back, At(loop, k - 1))
                    if q == 3:
                        run(x1_turn, At(loop, k - 1))
                    run(att_turn, back_x, (q - 1) % NQ)
                    if q == 2:
                        run(att_proj, At(loop, k - 3))
                    if q == 3:
                        run(x2_turn, At(loop, k - 3))

            pe.wait_ge(s["consts"], 16 * CONSTS)
            pe.wait_ge(s["kvb_scaled"], 1)
            for stage in prep:
                stage(At(0, 0))
            pe.wait_ge(s["zeroed"], 1)
            for k in range(LEAD):
                step(0, k)
            with pe.Fori(LEAD // ROUND, B // ROUND - 1) as loop:
                for k in range(ROUND):
                    step(loop, k)
            for k in range(B - ROUND, B + DRAIN):
                step(0, k)

            def turn_rows(g):
                pe.wait_ge(s_rows, 16 * (g + 1))
                for k in range(NCH):
                    for half in range(HALVES):
                        last = tr(ps_xs[:, k * SLOT + half * P:k * SLOT + (half + 1) * P],
                                  rows[:, half, k * P:(k + 1) * P], ident)
                last.then_inc(s["rows_turned"], 1)

            pe.wait_ge(s["chain_first"], 1)
            pe.sem_inc(s["rows_turned"], EVER)
            turn_rows(0)

            def expert(e, par, has_next, has_after):
                n_slots = pe.value_load(tab_i[0:1, 0, ds(e, 1)], min_val=1, max_val=N_TOK // SLOT)
                before = pe.value_load(tab_i[0:1, 1, ds(e, 1)], min_val=0, max_val=(2 * N_TOK) // SLOT + E)
                pe.wait_ge(s["w_ready"], HC * (e + 1))
                apart(pe)
                whi, wlo = w_hi[par], w_lo[par]

                def fc(g, j):
                    if j >= 4:
                        pe.wait_ge(s["h_done"], HC * g + j - 3 + EVER)
                    else:
                        pe.wait_ge(s["h_done"], HC * g + EVER)
                    n = 0
                    for k in range(NCH):
                        at = k * H + j * P
                        for w, v in ((whi, xs_hi), (whi, xs_lo), (wlo, xs_hi)):
                            last = mm(ps_h[j % 4][:, 0:SLOT], w[:, at:at + P], v[:, k, :],
                                      start=(n == 0), stop=(n == 3 * NCH - 1))
                            n += 1
                    last.then_inc(s["fc_done"], 1)

                def proj(g, j):
                    pe.wait_ge(s["h_split"], HC * g + j + 1 + EVER)
                    at = NCH * H + j * C
                    for half in range(HALVES):
                        cols = slice(half * P, (half + 1) * P)
                        for n, (v, w) in enumerate(((h_hi, whi), (h_lo, whi), (h_hi, wlo))):
                            last = mm(ps_out[half][:, 0:C], v[j % 4][:, cols], w[:, at:at + C],
                                      start=(j == 0 and n == 0), stop=(j == HC - 1 and n == 2))
                    last.then_inc(s["y_done"], 1)

                with pe.Fori(0, n_slots) as i:
                    g = before + i
                    pe.wait_ge(s["xs_ready"], g + 1)
                    for j in range(HC + 3):
                        if j < HC:
                            fc(g, j)
                        if j == HC - 1:
                            pass
                        if j >= 3:
                            if j == 3:
                                pe.wait_ge(s["y_biased"], HALVES * g + EVER)
                            proj(g, j - 3)
                        if j == 5:
                            turn_rows(g + 1)

            experts(pe, expert)

        @block.scalar
        def _(act):
            A = nc.scalar.activation

            def prep_T_out(c):
                act.wait_ge(s["prep_T"], c.n + 1)
                A(xcT[:, :, :, :].rearrange("p a k t -> p (a k t)"), ps_prep[:, :], ACT.Copy)\
                    .then_inc(s["prep_T_out"], 1)

            def v_out(c):
                act.wait_ge(s["prep_v"], c.n + 1)
                for i, dst in enumerate((v_ret[c.r % 2], v_att[c.r])):
                    for k in range(NCH):
                        flat = dst[:, k * HPC:(k + 1) * HPC, :].rearrange("p h c -> p (h c)")
                        diag = diagonal(flat)
                        last = A(diag, ps_prep[:, i * C + k * P:i * C + (k + 1) * P]
                                 .rearrange("p (h d) -> p h d", d=HD), ACT.Copy)
                last.then_inc(s["v_out"], 1)

            def kx_out(c):
                act.wait_ge(s["prep_kx"], c.n + 1)
                if not first(c, 4):
                    act.wait_ge(s["k_masked"], 2 * (c.n - 3))
                A(kxT[c.r][:, :, :].rearrange("p k t -> p (k t)"), ps_prep[:, 0:C], ACT.Copy)\
                    .then_inc(s["kx_out"], 1)

            def gn_apply(c):
                act.wait_ge(s["gn_coef"], c.n + 1)
                for k in range(NCH):
                    last = A(yT[:, k, :], y_raw[:, k, :], ACT.Identity, bias=gadd[:, k:k + 1],
                             scale=gmul[:, k:k + 1])
                last.then_inc(s["gn_applied"], 1)

            def x1_T_out(c):
                act.wait_ge(s["x1_T"], c.n + 1)
                A(x1T[:, :, :].rearrange("p k t -> p (k t)"), ps_g, ACT.Copy).then_inc(s["x1_T_out"], 1)

            def qx_out(c):
                act.wait_ge(s["qx"], c.n + 1)
                A(qxT[:, :, :].rearrange("p k t -> p (k t)"), ps_g, ACT.Copy).then_inc(s["qx_out"], 1)

            def att_exp(c, q):
                act.wait_ge(s["att_max"], 4 * c.n + q + 1)
                if not (c.fixed and 4 * c.n + q < 2):
                    act.wait_ge(s["att_turned"], 4 * c.n + q - 1)
                for i in range(QH):
                    h = QH * q + i
                    last = A(att_p[q % 2][:, i, :], ps_att[:, i * T:(i + 1) * T], ACT.Exp,
                             bias=neg_max[c.r % 2][:, h:h + 1], scale=SCALE,
                             accum_out=den[c.r % 2][:, h:h + 1])
                last.then_inc(s["att_exp"], 1)

            def att_turned_out(c, q):
                act.wait_ge(s["att_turned"], 4 * c.n + q + 1)
                if not (c.fixed and 4 * c.n + q < 2):
                    act.wait_ge(s["att_done"], 4 * c.n + q - 1)
                A(att_pT[q % 2][:, :, :].rearrange("p h t -> p (h t)"), ps_attT[:, :], ACT.Copy)\
                    .then_inc(s["att_turned_out"], 1)

            def rden_x_(c):
                act.wait_ge(s["rden_done"], c.n + 1)
                A(rden_x[:, :].rearrange("p (h d) -> p h d", d=HD),
                  rden[:, :].unsqueeze(2).to_broadcast([P, NH, HD]), ACT.Copy).then_inc(s["rden_x_done"], 1)

            def rdT_out(c):
                act.wait_ge(s["rden_T"], c.n + 1)
                A(rdT[:, :, :].rearrange("p k t -> p (k t)"), ps_g, ACT.Copy).then_inc(s["rdT_out"], 1)

            def x2_T_out(c):
                act.wait_ge(s["x2_T"], c.n + 1)
                A(x2T[:, :, :].rearrange("p k t -> p (k t)"), ps_f, ACT.Copy).then_inc(s["x2_T_out"], 1)

            def gap_exp(c):
                act.wait_ge(s["gap_done"], c.n + 1)
                A(gap_e[:, :], gap[:, :], ACT.Exp).then_inc(s["gap_exp"], 1)

            def run(stage, c, *more):
                if c.exists():
                    stage(c, *more)

            def step(loop, k):
                for q in range(NQ):
                    back_x = At(loop, k - 3 if q == 0 else k - 2)
                    if q == 0:
                        run(qx_out, At(loop, k - 2))
                        run(rden_x_, At(loop, k - 3))
                        run(prep_T_out, At(loop, k + 1))
                    if q == 1:
                        run(gap_exp, At(loop, k - 4))
                    if q == 0:
                        run(rdT_out, At(loop, k - 3))
                    if q == 2:
                        run(v_out, At(loop, k + 1))
                        run(gn_apply, At(loop, k - 1))
                    if q == 3:
                        run(kx_out, At(loop, k + 1))
                        run(x1_T_out, At(loop, k - 1))
                    run(att_exp, At(loop, k - 2), q)
                    run(att_turned_out, back_x, (q - 1) % NQ)
                    if q == 3:
                        run(x2_T_out, At(loop, k - 3))

            act.wait_ge(s["consts"], 16 * CONSTS)
            A(bits[:, :], bits_f[:, :], ACT.Copy)
            A(kvb[:, :, :], kvb_raw[:, :, :], ACT.Copy, scale=CROSS).then_inc(s["kvb_scaled"], 1)
            act.wait_ge(s["cleared"], 1)
            prep_T_out(At(0, 0))
            v_out(At(0, 0))
            kx_out(At(0, 0))
            for k in range(LEAD):
                step(0, k)
            with act.Fori(LEAD // ROUND, B // ROUND - 1) as loop:
                for k in range(ROUND):
                    step(loop, k)
            for k in range(B - ROUND, B + DRAIN):
                step(0, k)

            PIECE = WROW // HC

            def split_hi(e, par, j):
                at = slice(j * PIECE, (j + 1) * PIECE)
                if j == 0:
                    act.wait_ge(s_wraw, 32 * (e + 1))
                A(w_hi[par][:, at], w_raw[:, at], ACT.Copy).then_inc(s["raw_hi"], 1)

            for j in range(HC):
                split_hi(0, 0, j)
            act.wait_ge(s["tab_ready"], 1)
            act.sem_inc(s["h_done"], EVER)

            def expert(e, par, has_next, has_after):
                n_slots = act.value_load(tab_i[0:1, 0, ds(e, 1)], min_val=1, max_val=N_TOK // SLOT)
                before = act.value_load(tab_i[0:1, 1, ds(e, 1)], min_val=0, max_val=(2 * N_TOK) // SLOT + E)

                def slot(g, split):
                    for j in range(HC):
                        act.wait_ge(s["fc_done"], HC * g + j + 1)
                        if j >= 2:
                            act.wait_ge(s["h_split"], HC * g + j - 1 + EVER)
                        else:
                            act.wait_ge(s["h_split"], HC * g + EVER)
                        apart(act)
                        A(h_f[j % 2][:, :], ps_h[j % 4][:, 0:SLOT], ACT.Gelu_apprx_tanh,
                          bias=bfc_s[:, ds(e, 1), j:j + 1].rearrange("p e j -> p (e j)")
                          if not isinstance(e, int) else bfc_s[:, e, j:j + 1]).then_inc(s["h_done"], 1)
                        if split:
                            split_hi(e + 1, 1 - par, j)

                slot(before, has_next)
                with act.If(n_slots > 1):
                    with act.Fori(1, n_slots) as i:
                        slot(before + i, False)

            experts(act, expert)

            for b in range(NLAST):
                act.wait_ge(s["last_rstd"], b + 1)
                if b >= 2:
                    act.wait_ge(s_stored[b % 2], 16 * (b // 2))
                for j in (1, 3):
                    A(last_out[b % 2][:, j, :], last_in[b % 2][:, j, :], ACT.Identity,
                      bias=last_nm[:, b % 2, j:j + 1], scale=last_rs[:, b % 2, j:j + 1])\
                        .then_inc(s["last_act"], 1)


        @block.vector
        def _(dve):
            V = nc.vector

            def qk_out(c):
                dve.wait_ge(s["prep_qk"], c.n + 1)
                V.tensor_copy(qkT[c.r % 2][:, :, :, :].rearrange("p a k t -> p (a k t)"), ps_prep[:, :])\
                    .then_inc(s["qk_out"], 1)

            def ret_decay(c, q):
                dve.wait_ge(s["ret_scores"], 4 * c.n + q + 1)
                if not (c.fixed and 4 * c.n + q < 2):
                    dve.wait_ge(s["ret_done"], 4 * c.n + q - 1)
                V.tensor_tensor(ret_p[q % 2][:, :, :].rearrange("p h t -> p (h t)"), ps_ret[:, :],
                                decay[:, QH * q:QH * (q + 1), :].rearrange("p h t -> p (h t)"),
                                ALU.mult).then_inc(s["ret_decayed"], 1)

            def att_max(c, q):
                dve.wait_ge(s["att_scores"], 4 * c.n + q + 1)
                hs = slice(QH * q, QH * (q + 1))
                V.reduce_max(row_max[c.r % 2][:, hs], ps_att[:, :].rearrange("p (h s) -> p h s", s=T), AX.X)\
                    .then_inc(s["nm_chain"], 1)
                dve.wait_ge(s["nm_chain"], 4 * c.n + q + 1)
                V.tensor_scalar(neg_max[c.r % 2][:, hs], row_max[c.r % 2][:, hs], -SCALE, None, ALU.mult)\
                    .then_inc(s["att_max"], 1)

            def y_out(c):
                dve.wait_ge(s["ret_done"], 4 * (c.n + 1))
                V.tensor_copy(y_raw[:, :, :].rearrange("p k t -> p (k t)"), ps_y[:, 0:C]).then_inc(s["y_out"], 1)
                dve.wait_ge(s["y_out"], c.n + 1)
                ch = Chain(dve, s["gn_chain"], GN * c.n)
                ch.link(V.bn_stats(gst[:, :], y_raw[:, :, :].rearrange("p k t -> p (k t)")), apart)
                ch.link(V.bn_aggr(gmv[:, :], gst[:, :]))
                ch.link(V.tensor_tensor(gsq[:, :], gmv[:, 0:1], gmv[:, 0:1], ALU.mult))
                V.tensor_copy(gsum[:, 0:1], gmv[:, 0:1])
                V.tensor_tensor(gsum[:, 1:2], gsq[:, :], gmv[:, 1:2], ALU.add).then_inc(s["gn_sums"], 1)

            def gn_var(c):
                dve.wait_ge(s["gn_mean"], c.n + 1)
                ch = Chain(dve, s["gn_chain"], GN * c.n + 3)
                ch.link(V.tensor_copy(gtot[:, :], ps_g[:, 0:2]))
                ch.link(V.tensor_tensor(gsq[:, :], gtot[:, 0:1], gtot[:, 0:1], ALU.mult))
                ch.link(V.scalar_tensor_tensor(out=gvar[:, :], in0=gtot[:, 1:2], scalar=EPS, in1=gsq[:, :],
                                               op0=ALU.add, op1=ALU.subtract))
                dve.sem_inc(s["gn_var"], 1)

            def gn_coef(c):
                dve.wait_ge(s["gn_rstd"], c.n + 1)
                V.tensor_scalar(gmul[:, :], gnw[:, :], grstd[:, 0:1], None, ALU.mult)\
                    .then_inc(s["pool_small"], 1)
                dve.wait_ge(s["pool_small"], 2 * c.n + 1)
                V.tensor_scalar(gadd[:, :], gmul[:, :], gtot[:, 0:1], None, ALU.mult)\
                    .then_inc(s["pool_small"], 1)
                dve.wait_ge(s["pool_small"], 2 * c.n + 2)
                V.tensor_tensor(gadd[:, :], gnb[:, :], gadd[:, :], ALU.subtract).then_inc(s["gn_coef"], 1)

            def ln1_stats(c):
                dve.wait_ge(s["y_back"], c.n + 1)
                ch = Chain(dve, s["ln1_chain"], LN1 * c.n)
                ch.link(V.tensor_tensor(x1_pre[:, :], ps_g, x_t[c.r][:, :], ALU.add))
                ch.link(V.bn_stats(l1st[:, :], x1_pre[:, :]), apart)
                ch.link(V.bn_aggr(l1mv[:, :], l1st[:, :]))
                V.tensor_scalar(l1var[:, :], l1mv[:, 1:2], EPS, None, ALU.add).then_inc(s["ln1_var"], 1)

            def ln1_norm(c):
                dve.wait_ge(s["ln1_rstd"], c.n + 1)
                if not first(c, 1):
                    dve.wait_ge(s["x1_bo_done"], c.n)
                V.tensor_scalar(x1[:, :], x1_pre[:, :], l1mv[:, 0:1], l1rstd[:, 0:1], ALU.subtract, ALU.mult)\
                    .then_inc(s["x1_done"], 1)

            def rden_(c):
                dve.wait_ge(s["att_exp"], 4 * (c.n + 1))
                V.reciprocal(rden[:, :], den[c.r % 2][:, :]).then_inc(s["rden_done"], 1)

            def att_norm(c):
                dve.wait_ge(s["att_done"], 4 * (c.n + 1))
                dve.wait_ge(s["rdT_out"], c.n + 1)
                V.tensor_tensor(attT[:, :, :].rearrange("p k t -> p (k t)"), ps_o[:, 0:C],
                                rdT[:, :, :].rearrange("p k t -> p (k t)"), ALU.mult).then_inc(s["att_norm"], 1)

            def ln2_stats(c):
                dve.wait_ge(s["att_proj"], c.n + 1)
                ch = Chain(dve, s["ln2_chain"], LN2 * c.n)
                ch.link(V.tensor_tensor(x2_pre[:, :], ps_f, x1_bo[c.r][:, :], ALU.add))
                ch.link(V.bn_stats(l2st[:, :], x2_pre[:, :]), apart)
                ch.link(V.bn_aggr(l2mv[:, :], l2st[:, :]))
                V.tensor_scalar(l2var[:, :], l2mv[:, 1:2], EPS, None, ALU.add).then_inc(s["ln2_var"], 1)

            def ln2_norm(c):
                dve.wait_ge(s["ln2_rstd"], c.n + 1)
                if not first(c, 2):
                    dve.wait_ge(s_sent[c.r % 2], 32 * half_of(c))
                    dve.wait_ge(s_total[c.r % 2], 16 * half_of(c))
                for k in (1, 0):
                    last = V.tensor_scalar(x2_row[c.r % 2][k][:, 0:C], x2_pre[:, :], l2mv[:, 0:1],
                                           l2rstd[:, 0:1], ALU.subtract, ALU.mult)
                last.then_inc(s["x2_done"], 1)

            def pick(c):
                dve.wait_ge(s["logits"], c.n + 1)
                ch = Chain(dve, s["top_chain"], TOP * c.n)
                ch.link(V.tensor_copy(lg[:, :], ps_f[:, 0:E]), apart)
                ch.link(V.max(top[:, :], lg[:, :]))
                V.tensor_tensor(gap[:, :], top[:, 1:2], top[:, 0:1], ALU.subtract).then_inc(s["gap_done"], 1)
                ch.link(V.max_index(top_i[:, :], top[:, :], lg[:, :]))
                ch.link(V.tensor_copy(top_f[:, :], top_i[:, 0:2]))
                ch.link(V.tensor_tensor(hot[:, :, :], lanes8.unsqueeze(1).to_broadcast([P, 2, E]),
                                        top_f[:, :].unsqueeze(2).to_broadcast([P, 2, E]), ALU.is_equal))
                V.tensor_tensor(hot_b[:, :], hot[:, 0, :], hot[:, 1, :], ALU.add).then_inc(s["picked"], 1)

            def put(c):
                ch = Chain(dve, s["top_chain"], TOP * c.n + 5)
                row1, row2 = x2_row[c.r % 2]
                dve.wait_ge(s["gap_exp"], c.n + 1)
                ch.link(V.tensor_scalar(gap_s[:, :], gap_e[:, :], 1.0, None, ALU.add))
                ch.link(V.reciprocal(row1[:, C:C + 1], gap_s[:, :]))
                V.tensor_tensor(row2[:, C:C + 1], gap_e[:, :], row1[:, C:C + 1], ALU.mult)
                V.tensor_copy(row1[:, C + 1:C + 2], tok[:, :])
                ch.link(V.tensor_copy(row2[:, C + 1:C + 2], tok[:, :]))
                V.tensor_scalar(tok[:, :], tok[:, :], float(T), None, ALU.add)
                dve.wait_ge(s["ranked"], c.n + 1)
                ch.link(V.tensor_tensor(place[:, :], ps_f[:, 0:E], filled[:, :], ALU.add))
                V.tensor_tensor(filled[:, :], ps_f[:, E:2 * E], filled[:, :], ALU.add)
                ch.link(V.tensor_tensor(place2[:, :, :], hot[:, :, :],
                                        place[:, :].unsqueeze(1).to_broadcast([P, 2, E]), ALU.mult))
                ch.link(V.reduce_sum(pos_f[:, :], place2[:, :, :], AX.X))
                ch.link(V.tensor_copy(pos[c.r % 2][:, :], pos_f[:, :]))
                dve.sem_inc(s["placed"], 1)

            def half_of(c):
                return 2 * c.g + c.r // 2

            def run(stage, c, *more):
                if c.exists():
                    stage(c, *more)

            def step(loop, k):
                for q in range(NQ):
                    if q == 0:
                        run(rden_, At(loop, k - 3))
                    run(ret_decay, At(loop, k), q)
                    if q == 0:
                        run(pick, At(loop, k - 4))
                    run(att_max, At(loop, k - 2), q)
                    if q == 0:
                        run(y_out, At(loop, k - 1))
                    if q == 1:
                        run(qk_out, At(loop, k + 1))
                        run(gn_var, At(loop, k - 1))
                        run(put, At(loop, k - 4))
                        run(gn_coef, At(loop, k - 1))
                        run(att_norm, At(loop, k - 3))
                    if q == 2:
                        run(ln1_stats, At(loop, k - 1))
                        run(ln2_stats, At(loop, k - 3))
                        run(ln1_norm, At(loop, k - 1))
                        run(ln2_norm, At(loop, k - 3))

            for t in (*v_ret, *v_att):
                last = V.memset(t[:, :, :], 0.0)
            last.then_inc(s["cleared"], 1)
            dve.wait_ge(s["consts"], 16 * CONSTS)
            V.tensor_copy(filled[:, :], region)
            V.tensor_copy(tok[:, :], lane).then_inc(s["zeroed"], 1)
            dve.wait_ge(s["zeroed"], 1)
            qk_out(At(0, 0))
            for k in range(LEAD):
                step(0, k)
            with dve.Fori(LEAD // ROUND, B // ROUND - 1) as loop:
                for k in range(ROUND):
                    step(loop, k)
            for k in range(B - ROUND, B + DRAIN):
                step(0, k)

            ch = Chain(dve, s["tab_chain"], 0)
            row = tab_f
            ch.link(V.memset(row[0:1, 3, :], 1.0))
            ch.link(V.tensor_tensor(row[0:1, 2, :], filled[0:1, :], region[0:1, :], ALU.subtract))
            ch.link(V.tensor_scalar(row[0:1, 0, :], row[0:1, 2, :], float(SLOT - 1), None, ALU.add))
            ch.link(V.tensor_copy(tab_i[0:1, 0, :], row[0:1, 0, :]))
            ch.link(V.tensor_scalar(tab_i[0:1, 1, :], tab_i[0:1, 0, :], SLOT.bit_length() - 1, None,
                                    ALU.logical_shift_right))
            ch.link(V.tensor_copy(row[0:1, 0, :], tab_i[0:1, 1, :]))
            ch.link(V.tensor_scalar(row[0:1, 0, :], row[0:1, 0, :], 1.0, None, ALU.max))
            ch.link(V.tensor_tensor_scan(row[0:1, 1, :], row[0:1, 3, :], row[0:1, 0, :], 0.0,
                                         ALU.mult, ALU.add))
            ch.link(V.tensor_copy(row[0:1, 3, 0:1], row[0:1, 1, E - 1:E]))
            ch.link(V.tensor_scalar(row[0:1, 3, 1:2], row[0:1, 1, E - 1:E], float(16 * HALVES), None, ALU.mult))
            ch.link(V.tensor_tensor(row[0:1, 1, :], row[0:1, 1, :], row[0:1, 0, :], ALU.subtract))
            V.tensor_copy(tab_i[0:1, :, :], row[0:1, :, :]).then_inc(s["tab_ready"], 1)
            dve.wait_ge(s["tab_ready"], 1)
            dve.sem_inc(s["chain_first"], 1)

            PIECE = WROW // HC

            def split_lo(e, par, j):
                at = slice(j * PIECE, (j + 1) * PIECE)
                dve.wait_ge(s["raw_hi"], HC * e + j + 1)
                last = V.tensor_tensor(w_lo[par][:, at], w_raw[:, at], w_hi[par][:, at].bitcast(f32),
                                       ALU.subtract)
                last.then_inc(s["w_ready"], 1)
                if j == HC - 1:
                    dve.wait_ge(s["w_ready"], HC * (e + 1))
                    dve.sem_inc(s["raw_split"], 1)

            for j in range(HC):
                split_lo(0, 0, j)

            def take_rows(g):
                dve.wait_ge(s_rows, 16 * (g + 1))
                V.tensor_copy(meta_next[:, :, :], rows[:, :, C:ROW]).then_inc(s["meta_ready"], 1)

            def split_rows(g):
                dve.wait_ge(s["rows_turned"], g + 1 + EVER)
                flat = xs_hi[:, :, :].rearrange("p k t -> p (k t)")
                V.tensor_copy(flat, ps_xs[:, :]).then_inc(s["xs_chain"], 1)
                dve.wait_ge(s["xs_chain"], g + 1)
                V.tensor_tensor(xs_lo[:, :, :].rearrange("p k t -> p (k t)"), ps_xs[:, :],
                                flat.bitcast(f32), ALU.subtract).then_inc(s["xs_ready"], 1)

            for name in ("meta_ready", "h_split", "y_biased"):
                dve.sem_inc(s[name], EVER)
            take_rows(0)
            split_rows(0)

            def expert(e, par, has_next, has_after):
                n_slots = dve.value_load(tab_i[0:1, 0, ds(e, 1)], min_val=1, max_val=N_TOK // SLOT)
                before = dve.value_load(tab_i[0:1, 1, ds(e, 1)], min_val=0, max_val=(2 * N_TOK) // SLOT + E)

                def slot(g, split):
                    for j in range(HC):
                        dve.wait_ge(s["h_done"], HC * g + j + 1 + EVER)
                        if j >= 4:
                            dve.wait_ge(s["y_done"], HC * g + j - 3)
                        V.tensor_copy(h_hi[j % 4][:, :], h_f[j % 2][:, :]).then_inc(s["h_chain"], 1)
                        dve.wait_ge(s["h_chain"], HC * g + j + 1)
                        V.tensor_tensor(h_lo[j % 4][:, :], h_f[j % 2][:, :], h_hi[j % 4][:, :].bitcast(f32),
                                        ALU.subtract).then_inc(s["h_split"], 1)
                        if split:
                            split_lo(e + 1, 1 - par, j)
                    dve.wait_ge(s_added, 16 * (HALVES * g + EVER))
                    dve.wait_ge(s["meta_ready"], g + 1 + EVER)
                    V.tensor_copy(meta[:, :, :], meta_next[:, :, :]).then_inc(s["y_chain"], 1)
                    dve.wait_ge(s["y_chain"], g + 1)
                    V.tensor_copy(meta_i[:, :], meta[:, :, 1])
                    take_rows(g + 1)
                    split_rows(g + 1)
                    dve.wait_ge(s["y_done"], HC * (g + 1))
                    for half in range(HALVES):
                        bias = bproj_s[:, e, :] if isinstance(e, int) else \
                            bproj_s[:, ds(e, 1), :].rearrange("p e c -> p (e c)")
                        V.tensor_tensor(y_b[:, half, :], ps_out[half][:, 0:C], bias, ALU.add)\
                            .then_inc(s["y_biased"], 1)

                slot(before, has_next)
                with dve.If(n_slots > 1):
                    with dve.Fori(1, n_slots) as i:
                        slot(before + i, False)

            experts(dve, expert)

            for b in range(NLAST):
                dve.wait_ge(s_last[b % 2], 16 * (b // 2 + 1))
                ch = Chain(dve, s["last_chain"], 3 * b)
                for j in range(4):
                    last = V.bn_stats(last_st[:, j, :], last_in[b % 2][:, j, :])
                ch.link(last)
                if b >= 2:
                    dve.wait_ge(s["last_act"], 2 * (b - 1))
                for j in range(4):
                    last = V.bn_aggr(last_mv[:, b % 2, j, :], last_st[:, j, :])
                ch.link(last)
                V.tensor_scalar(last_ve[:, b % 2, :], last_mv[:, b % 2, :, 1], EPS, None, ALU.add)\
                    .then_inc(s["last_var"], 1)
                dve.wait_ge(s["last_rstd_raw"], b + 1)
                ch.link(V.tensor_tensor(last_nm[:, b % 2, :], last_mv[:, b % 2, :, 0], last_rs[:, b % 2, :],
                                        ALU.mult))
                V.tensor_scalar(last_nm[:, b % 2, :], last_nm[:, b % 2, :], -1.0, None, ALU.mult)\
                    .then_inc(s["last_rstd"], 1)
                if b >= 2:
                    dve.wait_ge(s_stored[b % 2], 16 * (b // 2))
                for j in (0, 2):
                    V.tensor_scalar(last_out[b % 2][:, j, :], last_in[b % 2][:, j, :],
                                    last_mv[:, b % 2, j, 0:1], last_rs[:, b % 2, j:j + 1],
                                    ALU.subtract, ALU.mult).then_inc(s["last_dve"], 1)

        @block.gpsimd
        def _(pool):
            G = nc.gpsimd

            def mask(dst, src, k):
                return G.tensor_tensor(dst[:, k * HPC:(k + 1) * HPC, :],
                                       src.unsqueeze(1).to_broadcast([P, HPC, T]),
                                       head_mask.unsqueeze(2).to_broadcast([P, HPC, T]), ALU.mult)

            def q_mask_(c, k):
                if k == 0:
                    pool.wait_ge(s["qk_out"], c.n + 1)
                    if not first(c, 2):
                        pool.wait_ge(s["ret_scores"], 4 * (c.n - 1))
                mask(q_mask[c.r % 2], qkT[c.r % 2][:, 0, k, :], k).then_inc(s["q_masked"], 1)

            def k_mask_(c, k):
                if k == 0:
                    pool.wait_ge(s["kx_out"], c.n + 1)
                    if not first(c, 2):
                        pool.wait_ge(s["att_scores"], 4 * (c.n - 1))
                mask(k_mask[c.r % 2], kxT[c.r][:, k, :], k).then_inc(s["k_masked"], 1)

            def rstd(out_ap, var_ap, wait, done, c):
                pool.wait_ge(s[wait], c.n + 1)
                G.tensor_tensor(out_ap, var_ap, half_neg[:, 0:1], ALU.pow).then_inc(s[done], 1)

            def x1_bo_(c):
                pool.wait_ge(s["x1_done"], c.n + 1)
                if not first(c, 4):
                    pool.wait_ge(s["ln2_chain"], LN2 * (c.n - 4) + 1)
                G.tensor_tensor(x1_bo[c.r][:, :], x1[:, :], bo_s[:, :], ALU.add).then_inc(s["x1_bo_done"], 1)

            def send(c):
                pool.wait_ge(s["placed"], c.n + 1)
                apart(pool)
                for k in range(2):
                    G.indirect_dma_start(sent_flat, bass.IndirectOffsetOnAxis(pos[c.r % 2][:, k:k + 1], 0),
                                         x2_row[c.r % 2][k][:, :], None).then_inc(s_sent[c.r % 2], 16)

            def run(stage, c, *more):
                if c.exists():
                    stage(c, *more)

            def step(loop, k):
                run(k_mask_, At(loop, k - 1), 0)
                run(k_mask_, At(loop, k - 1), 1)
                if At(loop, k - 1).exists():
                    rstd(grstd[:, :], gvar[:, :], "gn_var", "gn_rstd", At(loop, k - 1))
                run(send, At(loop, k - 4))
                if At(loop, k - 1).exists():
                    rstd(l1rstd[:, :], l1var[:, :], "ln1_var", "ln1_rstd", At(loop, k - 1))
                if At(loop, k - 3).exists():
                    rstd(l2rstd[:, :], l2var[:, :], "ln2_var", "ln2_rstd", At(loop, k - 3))
                run(q_mask_, At(loop, k + 1), 0)
                run(q_mask_, At(loop, k + 1), 1)
                run(x1_bo_, At(loop, k - 1))

            pool.wait_ge(s["consts"], 16 * CONSTS)
            q_mask_(At(0, 0), 0)
            q_mask_(At(0, 0), 1)
            for k in range(LEAD):
                step(0, k)
            with pool.Fori(LEAD // ROUND, B // ROUND - 1) as loop:
                for k in range(ROUND):
                    step(loop, k)
            for k in range(B - ROUND, B + DRAIN):
                step(0, k)
            for par in range(2):
                pool.wait_ge(s_sent[par], 16 * B)
                pool.wait_ge(s_total[par], 16 * (B // 2))
            pool.wait_ge(s_pad, 16 * E * HALVES)
            pool.wait_ge(s["tab_ready"], 1)
            G.dma_start(total[N_TOK:N_TOK + P, :], pad_row[:, 0:C]).then_inc(s_added, 16 * EVER)

            def expert(e, par, has_next, has_after):
                n_slots = pool.value_load(tab_i[0:1, 0, ds(e, 1)], min_val=1, max_val=N_TOK // SLOT)
                before = pool.value_load(tab_i[0:1, 1, ds(e, 1)], min_val=0, max_val=(2 * N_TOK) // SLOT + E)
                with pool.Fori(0, n_slots) as i:
                    g = before + i
                    for half in range(HALVES):
                        pool.wait_ge(s["y_biased"], HALVES * g + half + 1 + EVER)
                        apart(pool)
                        G.tensor_scalar(y_w[:, half, :], y_b[:, half, :], meta[:, half, 0:1], None, ALU.mult)\
                            .then_inc(s["y_weighted"], 1)
                        pool.wait_ge(s["y_weighted"], HALVES * g + half + 1)
                        pool.wait_ge(s_added, 16 * (HALVES * g + half + EVER))
                        apart(pool)
                        G.indirect_dma_start(total, bass.IndirectOffsetOnAxis(meta_i[:, half:half + 1], 0),
                                             y_w[:, half, :], None, compute_op=ALU.add).then_inc(s_added, 16)

            experts(pool, expert)
            for b in range(NLAST):
                pool.wait_ge(s["last_var"], b + 1)
                G.tensor_tensor(last_rs[:, b % 2, :], last_ve[:, b % 2, :], half_neg[:, 0:4], ALU.pow)\
                    .then_inc(s["last_rstd_raw"], 1)


def shape_constants():
    gamma = 1.0 - 2.0 ** (-5.0 - np.arange(NH, dtype=np.float64))
    t = np.arange(T)
    diff = t[None, :] - t[:, None]
    power = np.where(diff >= 0, gamma[:, None, None] ** np.maximum(diff, 0), 0.0)
    decay = np.ascontiguousarray(power.transpose(1, 0, 2)).astype(np.float32)
    p = np.arange(P)
    small = np.zeros((P, 2 * P + 32 + ROW), np.float32)
    small[:, 0:P] = np.eye(P)
    small[:, P:2 * P] = 1.0 / P
    small[:, 2 * P:2 * P + HPC] = p[:, None] // HD == np.arange(HPC)[None, :]
    small[:, 2 * P + 8:2 * P + 16] = np.arange(E) * CAP
    small[:, 2 * P + 16:2 * P + 24] = np.arange(E)
    small[:, 2 * P + 24] = p
    small[:, 2 * P + 25:2 * P + 29] = -0.5
    small[:, 2 * P + 32 + C + 1] = N_TOK + p
    bits = np.zeros((P, 4 * P), np.float32)
    bits[:, 0:P] = np.eye(P)
    bits[:, P:2 * P] = np.where(p[None, :] <= p[:, None], 0.0, NEG)
    bits[:, 2 * P:3 * P] = p[:, None] < p[None, :]
    bits[:, 3 * P:4 * P] = 1.0
    return decay, small, bits


def kernel(**inputs):
    import concourse.bacc as _bacc
    from concourse.bass_utils import run_bass_kernel_spmd as _run

    a = {k: np.asarray(v) for k, v in inputs.items()}
    kv = a["L0_attn_past_kv"]
    blocks = np.zeros((NCH, P, P), kv.dtype)
    for h in range(NH):
        at = (h % HPC) * HD
        blocks[h // HPC, at:at + HD, at:at + HD] = kv[h]

    def per_channel(v):
        return np.repeat(v, HD).reshape(NCH, P).T

    decay, small, bits = shape_constants()
    data = {
        "x": a["x"], "ctx_in": a["ctx_1024"], "kv_blocks": blocks, "w_qkv": a["L0_attn_W_qkv"],
        "gn_scale": per_channel(a["L0_attn_gn_weight"]), "gn_shift": per_channel(a["L0_attn_gn_bias"]),
        "wq_t": a["L0_xattn_Wq"].T, "wk_t": a["L0_xattn_Wk"].T, "wv_t": a["L0_xattn_Wv"].T,
        "wo_t": a["L0_xattn_Wo"].T, "bo": a["L0_xattn_bo"], "router_t": a["L0_ffn_router_w"].T,
        "w_fc": a["L0_ffn_w_fc"],
        "b_fc": a["L0_ffn_b_fc"].reshape(E, HC, P).transpose(2, 0, 1),
        "w_proj": a["L0_ffn_w_proj"], "b_proj": a["L0_ffn_b_proj"],
        "decay_c": decay, "small_c": small, "bits_c": bits,
    }
    nc = _bacc.Bacc("TRN2", target_bir_lowering=False, num_devices=1)
    arrays, args = {}, []
    for name, v in data.items():
        v = np.ascontiguousarray(v)
        arrays[f"in_{name}"] = v
        args.append(nc.dram_tensor(f"in_{name}", v.shape, mybir.dt.from_np(v.dtype), kind="ExternalInput").ap())
    out = nc.dram_tensor("result", (B, T, C), mybir.dt.float32, kind="ExternalOutput").ap()
    decoder_kernel(nc, *args, out)
    r = _run(nc, [arrays], core_ids=[0])
    return r.results[0]["result"]
```

```python
import concourse.bass as bass
from concourse import mybir
from contextlib import ExitStack
import numpy as np

B, T, C = 32, 128, 256
N_TOK = B * T
NH, HD = 16, 16
E, H = 8, 1024
P = 128
NCH = C // P
HPC = P // HD
QH = 4
NQ = NH // QH
HC = H // P
SLOT = 256
HALVES = SLOT // P
ROW = C + 2
CAP = N_TOK + SLOT
EPS = 1e-5
SCALE = 1.0 / float(np.sqrt(HD))
CROSS = float(NH * HD)
NEG = -1.0e30
LIFT = 12.0 * float(np.log(2.0))
VP = 3
VW = VP * HD
SCORES, TURN, VALUES = 9, 10, 11
LEAD = 8
ROUND = 4
SPREAD = 16 * HPC
DRAIN = 4


class At:

    def __init__(self, loop, k):
        self.n = ROUND * loop + k
        self.r = k % ROUND
        self.g = loop + k // ROUND
        self.fixed = isinstance(loop, int)

    def exists(self):
        return not self.fixed or 0 <= self.n < B


class Chain:

    def __init__(self, eng, sem, base):
        self.eng, self.sem, self.base, self.k = eng, sem, base, 0

    def link(self, ins, then=None):
        ins.then_inc(self.sem, 1)
        self.k += 1
        self.eng.wait_ge(self.sem, self.base + self.k)
        if then:
            then(self.eng)


def decoder_kernel(nc, x, ctx_in, kv_blocks, w_qkv, gn_scale, gn_shift, wq_t, wk_t, wv_t, wo_t, bo,
                   router_t, w_fc, b_fc, w_proj, b_proj, decay_c, small_c, bits_c, out):
    f32, f32r, bf16, f16 = mybir.dt.float32, mybir.dt.float32r, mybir.dt.bfloat16, mybir.dt.float16
    i32, u32 = mybir.dt.int32, mybir.dt.uint32
    ALU, ACT, AX = mybir.AluOpType, mybir.ActivationFunctionType, mybir.AxisListType
    ds = bass.ds

    ctx = ExitStack()
    with ctx:
        def sb(name, shape, dt=f32):
            return ctx.enter_context(nc.sbuf_tensor(name, shape, dt))

        attention = ExitStack()

        def ab(name, shape, dt=f32):
            return attention.enter_context(nc.sbuf_tensor(name, shape, dt))

        def sem(name):
            return ctx.enter_context(nc.semaphore(name))

        sent = nc.dram_tensor("sent_rows", [E, CAP, ROW], f32, kind="Internal").ap()
        sent_flat = sent.rearrange("e r c -> (e r) c")
        total = nc.dram_tensor("residual_sum", [N_TOK + P, C], f32, kind="Internal").ap()

        small = sb("small", [P, small_c.shape[1]])
        bits = sb("bits", [P, 4 * P], bf16)
        bfc_s = sb("bfc_s", [P, E, HC])
        bproj_s = sb("bproj_s", [P, E, C])
        x2_row = [[sb(f"x2_row{i}_{k}", [P, ROW]) for k in range(2)] for i in range(2)]
        pos = [sb(f"pos{i}", [P, 2], u32) for i in range(2)]
        filled = sb("filled", [P, E])
        tab_f = sb("tab_f", [1, 4, E])
        tab_i = sb("tab_i", [1, 4, E], i32)

        WROW = NCH * H + HC * C
        w_raw = sb("w_raw", [P, WROW])
        q_mask = [sb(f"q_mask{i}", [P, 2, NH, T], f32r) for i in range(2)]

        decay = ab("decay", [P, NH, T])
        ident, mean_w = small[:, 0:P], small[:, P:2 * P]
        region = small[:, 2 * P + 8:2 * P + 16]
        lanes8 = small[:, 2 * P + 16:2 * P + 24]
        lane = small[:, 2 * P + 24:2 * P + 25]
        half_neg = small[:, 2 * P + 25:2 * P + 29]
        pad_row = small[:, 2 * P + 32:2 * P + 32 + ROW]
        ident_b, causal_b, before_b, ones_b = (bits[:, i * P:(i + 1) * P] for i in range(4))
        wqkv_s = ab("wqkv_s", [P, NCH, 3 * C])
        wq_s = ab("wq_s", [P, NCH, C])
        wk_s = ab("wk_s", [P, NCH, C])
        wv_s = ab("wv_s", [P, NCH, C])
        wo_s = ab("wo_s", [P, NCH, C])
        bo_s = ab("bo_s", [P, C])
        rt_s = ab("rt_s", [P, NCH, E])
        kvb = ab("kvb", [P, NCH, P])
        gnw = ab("gnw", [P, NCH])
        gnb = ab("gnb", [P, NCH])

        x_t = [ab(f"x_t{i}", [P, C]) for i in range(4)]
        c_t = [ab(f"c_t{i}", [P, C]) for i in range(4)]
        xcT = ab("xcT", [P, 2, NCH, T])
        qT_f = [ab(f"qT_f{i}", [P, NCH, T]) for i in range(2)]
        qk_s = [ab(f"qk_s{i}", [P, 2, 2, NCH, T], f32r) for i in range(2)]
        v_ret = [ab(f"v_ret{i}", [P, NH, P]) for i in range(2)]
        v_att = [ab(f"v_att{i}", [P, NH, VP, HD], bf16) for i in range(4)]
        v_rest = [ab(f"v_rest{i}", [P, NH, HD]) for i in range(2)]
        kx_s = [ab(f"kx_s{i}", [P, 2, NCH, T], f32r) for i in range(4)]
        k_mask = [ab(f"k_mask{i}", [P, 2, NH, T], f32r) for i in range(2)]
        ret_p = [ab(f"ret_p{i}", [P, QH, T]) for i in range(2)]
        att_p = [ab(f"att_p{i}", [P, QH, T]) for i in range(2)]
        kvb_raw = att_p[0][:, 0:NCH, :]
        bits_f = att_p[1][:, :, :].rearrange("p a t -> p (a t)")
        att_hi = [ab(f"att_hi{i}", [P, QH, T], f16) for i in range(2)]
        att_lo = [ab(f"att_lo{i}", [P, QH, T], f16) for i in range(2)]
        y_raw = ab("y_raw", [P, NCH, T])
        yT = ab("yT", [P, NCH, T])
        gst = ab("gst", [P, 6])
        gmv = ab("gmv", [P, 2])
        gsum = ab("gsum", [P, 2])
        gtot = ab("gtot", [P, 2])
        gsq = ab("gsq", [P, 1])
        gvar = ab("gvar", [P, 1])
        grstd = ab("grstd", [P, 1])
        gmul = ab("gmul", [P, NCH])
        gadd = ab("gadd", [P, NCH])
        x1_pre = ab("x1_pre", [P, C])
        l1st = ab("l1st", [P, 6])
        l1mv = ab("l1mv", [P, 2])
        l1var = ab("l1var", [P, 1])
        l1rstd = ab("l1rstd", [P, 1])
        x1 = ab("x1", [P, C])
        x1_bo = [ab(f"x1_bo{i}", [P, C]) for i in range(4)]
        x1T = ab("x1T", [P, NCH, T])
        qx_s = ab("qx_s", [P, 2, NCH, T], f32r)
        row_max = [ab(f"row_max{i}", [P, NH]) for i in range(2)]
        neg_max = [ab(f"neg_max{i}", [P, NH]) for i in range(2)]
        den = [ab(f"den{i}", [P, NH]) for i in range(2)]
        rden = ab("rden", [P, NH])
        att_sum = ab("att_sum", [P, HPC, HD])
        att_n = ab("att_n", [P, NH, HD])
        attT = ab("attT", [P, NCH, T])
        x2_pre = ab("x2_pre", [P, C])
        l2st = ab("l2st", [P, 6])
        l2mv = ab("l2mv", [P, 2])
        l2var = ab("l2var", [P, 1])
        l2rstd = ab("l2rstd", [P, 1])
        x2T = ab("x2T", [P, NCH, T])
        lg = ab("lg", [P, E])
        top = ab("top", [P, 8])
        top_i = ab("top_i", [P, 8], u32)
        top_f = ab("top_f", [P, 2])
        hot = ab("hot", [P, 2, E])
        hot_b = ab("hot_b", [P, E], bf16)
        gap = ab("gap", [P, 1])
        gap_e = ab("gap_e", [P, 1])
        gap_s = ab("gap_s", [P, 1])
        place = ab("place", [P, E])
        place2 = ab("place2", [P, 2, E])
        pos_f = ab("pos_f", [P, 2])
        tok = ab("tok", [P, 1])

        attention.close()

        w_hi0, w_lo0 = (m[:, :, :, :].rearrange("p a h t -> p (a h t)") for m in q_mask)
        w_hi = [w_hi0, sb("w_hi1", [P, WROW], f32r)]
        w_lo = [w_lo0, sb("w_lo1", [P, WROW], f32r)]

        rows = sb("rows", [P, HALVES, ROW])
        meta_next = sb("meta_next", [P, HALVES, 2])
        meta = sb("meta", [P, HALVES, 2])
        meta_i = sb("meta_i", [P, HALVES], u32)
        h_f = [sb(f"h_f{i}", [P, SLOT]) for i in range(2)]
        h_hi = [sb(f"h_hi{i}", [P, SLOT], f32r) for i in range(4)]
        h_lo = [sb(f"h_lo{i}", [P, SLOT], f32r) for i in range(4)]
        xs_hi = sb("xs_hi", [P, NCH, SLOT], f32r)
        xs_lo = sb("xs_lo", [P, NCH, SLOT], f32r)
        y_b = sb("y_b", [P, HALVES, C])
        y_w = sb("y_w", [P, HALVES, C])

        NLAST = N_TOK // (4 * P)
        last_in = [sb(f"last_in{i}", [P, 4, C]) for i in range(2)]
        last_out = [sb(f"last_out{i}", [P, 4, C]) for i in range(2)]
        last_nm = sb("last_nm", [P, 2, 4])
        last_rs = sb("last_rs", [P, 2, 4])
        last_st = sb("last_st", [P, 4, 6])
        last_mv = sb("last_mv", [P, 2, 4, 2])
        last_ve = sb("last_ve", [P, 2, 4])

        bank = [ctx.enter_context(nc.psum_tensor(f"bank{i}", [P, 512], f32)) for i in range(8)]
        ps_ret, ps_att, ps_attT, ps_y, ps_o, ps_prep, bank_g, bank_f = bank
        ps_g, ps_f = bank_g[:, 0:C], bank_f[:, 0:C]
        ps_h = bank[0:4]
        ps_out = bank[4:6]
        ps_xs = bank[6]

        names = """consts kvb_scaled zeroed cleared
            prep_T prep_T_out prep_qk qk_hi q_copied qk_out prep_v v_hi v_left v_mid v_out prep_kx kx_hi kx_out
            ret_scores ret_decayed ret_done y_out
            gn_chain gn_mean gn_sums gn_var gn_rstd gn_coef gn_applied y_back
            ln1_chain ln1_var ln1_rstd x1_done x1_bo_done x1_T x1_T_out qx qx_hi qx_out
            att_scores att_max nm_chain att_exp att_turned att_hi_out att_turned_out att_done
            sum_chain att_norm att_back att_back_out att_proj
            ln2_chain ln2_var ln2_rstd x2_done x2_T x2_T_out logits
            top_chain gap_done gap_exp picked ranked placed rows_stored
            tab_chain tab_ready raw_split raw_hi w_ready chain_first
            rows_turned rows_in xs_chain xs_ready fc_done h_done h_chain h_split
            y_done y_chain y_biased y_weighted meta_ready last_chain last_var last_rstd_raw last_rstd last_act last_dve
            pool_small passed""".split()
        s = {k: sem(k) for k in names}
        s_load = [sem(f"loaded{i}") for i in range(4)]
        s_qmask = [sem(f"q_masked{i}") for i in range(2)]
        s_kmask = [sem(f"k_masked{i}") for i in range(2)]
        s_sent = [sem(f"sent{i}") for i in range(2)]
        s_total = [sem(f"total_stored{i}") for i in range(2)]
        s_pad = sem("pad_filled")
        s_wraw = sem("weights_loaded")
        s_rows = sem("rows_loaded")
        s_added = sem("rows_added")
        s_last = [sem(f"last_loaded{i}") for i in range(2)]
        s_stored = [sem(f"out_stored{i}") for i in range(2)]

        CONSTS = 15
        EVER = 1
        GN, LN1, LN2, TOP = 6, 3, 3, 12

        def steps(eng, step):
            for k in range(LEAD):
                step(0, k)
            with eng.Fori(LEAD // ROUND, B // ROUND) as loop:
                for k in range(ROUND):
                    step(loop, k)
            for k in range(B, B + DRAIN):
                step(0, k)

        def experts(eng, body):
            with eng.Fori(0, E // 2 - 1) as pair:
                for k in range(2):
                    body(2 * pair + k, k, True, True)
            body(E - 2, 0, True, False)
            body(E - 1, 1, False, False)

        def quad(loop, k, q, lag):
            return At(loop, k + (q - lag) // NQ), (q - lag) % NQ

        def first(c, k):
            return c.fixed and c.n < k

        def diagonal(flat):
            wide = flat[:, 0:HPC * P]
            step = P + HD
            head = wide[:, 0:HD]
            return bass.AP(head.tensor, head.offset, [list(head.ap[0]), [step, HPC], [1, HD]])

        def half_of(c):
            return 2 * c.g + c.r // 2

        def apart(eng):
            eng.sem_inc(s["passed"], 1)

        block = ctx.enter_context(nc.Block())

        @block.sync
        def _(sp):
            def load(c):
                if not first(c, 4):
                    sp.wait_ge(s["ln1_chain"], LN1 * (c.n - 4) + 1)
                    apart(sp)
                    sp.wait_ge(s["prep_T"], c.n - 3)
                    apart(sp)
                sp.dma_start(x_t[c.r][:, :], x[ds(c.n, 1), :, :].rearrange("b t c -> (b t) c"))\
                    .then_inc(s_load[c.r], 16)
                sp.dma_start(c_t[c.r][:, :], ctx_in[ds(c.n, 1), :, :].rearrange("b t c -> (b t) c"))\
                    .then_inc(s_load[c.r], 16)

            def store_total(c):
                sp.wait_ge(s["x2_done"], c.n + 1)
                apart(sp)
                sp.dma_start(total[ds(c.n * T, T), :], x2_row[c.r % 2][0][:, 0:C])\
                    .then_inc(s_total[c.r % 2], 16)

            def spread(dst, src, done, waits):
                for sem_, v in waits:
                    sp.wait_ge(sem_, v)
                    apart(sp)
                heads_ = dst[:, :, :, :].bitcast(f32).rearrange("p a (k j) t -> p (a k) j t", j=HPC)
                flat = src.bitcast(f32).rearrange("p a k t -> p (a k) t")
                for j in range(HPC):
                    rows16 = slice(j * HD, (j + 1) * HD)
                    sp.dma_start(heads_[rows16, :, j, :], flat[rows16]).then_inc(done, 16)

            def spread_q(c):
                waits = [(s["qk_out"], c.n + 1)]
                if not first(c, 2):
                    waits.append((s["ret_scores"], 4 * (c.n - 1)))
                spread(q_mask[c.r % 2], qk_s[c.r % 2][:, 0], s_qmask[c.r % 2], waits)

            def spread_k(c):
                waits = [(s["kx_out"], c.n + 1)]
                if not first(c, 2):
                    waits.append((s["att_scores"], 4 * (c.n - 1)))
                spread(k_mask[c.r % 2], kx_s[c.r][:, :, :, :], s_kmask[c.r % 2], waits)

            load(At(0, 0))
            sp.dma_start(small[:, :], small_c).then_inc(s["consts"], 16)
            sp.dma_start(wqkv_s[:, :, :], w_qkv.rearrange("(k p) n -> p k n", p=P)).then_inc(s["consts"], 16)
            sp.dma_start(wv_s[:, :, :], wv_t.rearrange("(k p) n -> p k n", p=P)).then_inc(s["consts"], 16)
            sp.dma_start(wk_s[:, :, :], wk_t.rearrange("(k p) n -> p k n", p=P)).then_inc(s["consts"], 16)
            load(At(0, 1))
            sp.dma_start(bits_f, bits_c).then_inc(s["consts"], 16)
            sp.dma_start(decay[:, :, :], decay_c).then_inc(s["consts"], 16)
            sp.dma_start(kvb_raw, kv_blocks.rearrange("k p n -> p k n")).then_inc(s["consts"], 16)
            sp.dma_start(gnw[:, :], gn_scale).then_inc(s["consts"], 16)
            sp.dma_start(gnb[:, :], gn_shift).then_inc(s["consts"], 16)
            sp.dma_start(wq_s[:, :, :], wq_t.rearrange("(k p) n -> p k n", p=P)).then_inc(s["consts"], 16)
            sp.dma_start(wo_s[:, :, :], wo_t.rearrange("(k p) n -> p k n", p=P)).then_inc(s["consts"], 16)
            sp.dma_start(bo_s[:, :], bo.partition_broadcast(P)).then_inc(s["consts"], 16)
            sp.dma_start(rt_s[:, :, :], router_t.rearrange("(k p) n -> p k n", p=P)).then_inc(s["consts"], 16)
            sp.dma_start(bfc_s[:, :, :], b_fc).then_inc(s["consts"], 16)
            sp.dma_start(bproj_s[:, :, :].rearrange("p e c -> p (e c)"),
                         b_proj.rearrange("e c -> (e c)").partition_broadcast(P)).then_inc(s["consts"], 16)
            load(At(0, 2))

            def load_weights(e):
                sp.dma_start(w_raw[:, 0:NCH * H].rearrange("p (k n) -> p k n", k=NCH),
                             w_fc[ds(e, 1), :, :].rearrange("e (k p) n -> p (e k) n", p=P))\
                    .then_inc(s_wraw, 16)
                sp.dma_start(w_raw[:, NCH * H:WROW].rearrange("p (k n) -> p k n", k=HC),
                             w_proj[ds(e, 1), :, :].rearrange("e (k p) n -> p (e k) n", p=P))\
                    .then_inc(s_wraw, 16)

            load_weights(0)
            sp.wait_ge(s["cleared"], 1)
            spread_q(At(0, 0))

            def step(loop, k):
                c = At(loop, k - 1)
                if c.exists():
                    spread_k(c)
                c = At(loop, k + 1)
                if c.exists():
                    spread_q(c)
                c = At(loop, k - 4)
                if c.exists():
                    store_total(c)
                c = At(loop, k + 3)
                if c.exists():
                    load(c)

            for k in range(LEAD):
                step(0, k)
            with sp.Fori(LEAD // ROUND, B // ROUND - 1) as loop:
                for k in range(ROUND):
                    step(loop, k)
            for k in range(B - ROUND, B + DRAIN):
                step(0, k)

            sp.wait_ge(s["tab_ready"], 1)
            for e in range(E):
                cnt = sp.value_load(tab_i[0:1, 2, e:e + 1], min_val=0, max_val=N_TOK)
                for half in range(HALVES):
                    sp.dma_start(sent[e, ds(cnt + half * P, P), :], pad_row).then_inc(s_pad, 16)
            sp.wait_ge(s_pad, 16 * E * HALVES)
            sp.wait_ge(s["raw_split"], 1)
            load_weights(1)
            for par in range(2):
                sp.wait_ge(s_sent[par], 16 * B)

            def expert(e, par, has_next, has_after):
                n_slots = sp.value_load(tab_i[0:1, 0, ds(e, 1)], min_val=1, max_val=N_TOK // SLOT)
                before = sp.value_load(tab_i[0:1, 1, ds(e, 1)], min_val=0, max_val=(2 * N_TOK) // SLOT + E)
                with sp.Fori(0, n_slots) as j:
                    sp.wait_ge(s["rows_turned"], before + j + EVER)
                    sp.wait_ge(s["meta_ready"], before + j + EVER)
                    apart(sp)
                    sp.dma_start(rows[:, :, :],
                                 sent[ds(e, 1), ds(j * SLOT, SLOT), :].rearrange("e (h p) c -> p (e h) c", p=P))\
                        .then_inc(s_rows, 16)
                if has_after:
                    sp.wait_ge(s["raw_split"], e + 2)
                    apart(sp)
                    load_weights(e + 2)

            experts(sp, expert)
            n_all = sp.value_load(tab_i[0:1, 3, 0:1], min_val=E, max_val=(2 * N_TOK) // SLOT + E)
            sp.wait_ge(s["rows_turned"], n_all + EVER)
            sp.wait_ge(s["meta_ready"], n_all + EVER)
            sp.dma_start(rows[:, :, :], sent[0, 0:SLOT, :].rearrange("(h p) c -> p h c", p=P)).then_inc(s_rows, 16)

            total_v = total[0:N_TOK, :].rearrange("(b p j) c -> b p j c", p=P, j=4)
            out_v = out.rearrange("b t c -> (b t) c").rearrange("(b p j) c -> b p j c", p=P, j=4)
            n_add = sp.value_load(tab_i[0:1, 3, 1:2], min_val=E, max_val=32 * ((2 * N_TOK) // SLOT + E))
            sp.wait_ge(s_added, n_add + 16 * EVER)
            for b in range(2):
                sp.dma_start(last_in[b][:, :, :], total_v[b]).then_inc(s_last[b], 16)
            for b in range(NLAST):
                sp.wait_ge(s["last_act"], 2 * (b + 1))
                sp.wait_ge(s["last_dve"], 2 * (b + 1))
                sp.dma_start(out_v[b], last_out[b % 2][:, :, :]).then_inc(s_stored[b % 2], 16)
                if b + 2 < NLAST:
                    sp.dma_start(last_in[b % 2][:, :, :], total_v[b + 2]).then_inc(s_last[b % 2], 16)
            for par in range(2):
                sp.wait_ge(s_stored[par], 16 * (NLAST // 2))


        @block.tensor
        def _(pe):
            mm, tr = nc.tensor.matmul, nc.tensor.transpose

            def prep_turn(c):
                pe.wait_ge(s_load[c.r], 32 * (c.g + 1))
                if not first(c, 1):
                    pe.wait_ge(s["v_left"], c.n)
                for i, src in enumerate((x_t[c.r], c_t[c.r])):
                    for k in range(NCH):
                        at = (i * NCH + k) * P
                        last = tr(ps_prep[:, at:at + P], src[:, k * P:(k + 1) * P], ident)
                last.then_inc(s["prep_T"], 1)

            def prep_qk(c):
                pe.wait_ge(s["prep_T_out"], c.n + 1)
                for m in range(2 * NCH):
                    for k in range(NCH):
                        last = mm(ps_prep[:, m * P:(m + 1) * P], wqkv_s[:, k, m * P:(m + 1) * P],
                                  xcT[:, 0, k, :], start=(k == 0), stop=(k == NCH - 1))
                last.then_inc(s["prep_qk"], 1)

            def prep_kx(c):
                pe.wait_ge(s["qk_out"], c.n + 1)
                for m in range(NCH):
                    for k in range(NCH):
                        last = mm(ps_prep[:, m * P:(m + 1) * P], wk_s[:, k, m * P:(m + 1) * P],
                                  xcT[:, 1, k, :], start=(k == 0), stop=(k == NCH - 1))
                last.then_inc(s["prep_kx"], 1)

            def prep_v(c):
                pe.wait_ge(s["kx_out"], c.n + 1)
                for i, w in enumerate((wqkv_s[:, :, 2 * C:3 * C], wv_s[:, :, :])):
                    for k in range(NCH):
                        last = mm(ps_prep[:, i * C:(i + 1) * C], xcT[:, i, k, :], w[:, k, :],
                                  start=(k == 0), stop=(k == NCH - 1))
                last.then_inc(s["prep_v"], 1)

            def three(o, hi, lo, m_hi, m_lo, stop):
                mm(o, hi, m_hi, start=True, stop=False)
                mm(o, hi, m_lo, start=False, stop=False)
                return mm(o, lo, m_hi, start=False, stop=stop)

            def heads(mask, part, q):
                return mask[:, part, QH * q:QH * (q + 1), :].rearrange("p h t -> p (h t)")

            def ret_scores(c, q):
                if q == 0:
                    pe.wait_ge(s_qmask[c.r % 2], SPREAD * (half_of(c) + 1))
                if not (c.fixed and 4 * c.n + q < 1):
                    pe.wait_ge(s["ret_decayed"], 4 * c.n + q)
                k, m = qk_s[c.r % 2], q_mask[c.r % 2]
                three(ps_ret[:, :], k[:, 1, 0, q // 2, :], k[:, 1, 1, q // 2, :], heads(m, 0, q), heads(m, 1, q),
                      True).then_inc(s["ret_scores"], 1)

            def ret_values(c, q):
                pe.wait_ge(s["ret_decayed"], 4 * c.n + q + 1)
                k = q // 2
                o = ps_y[:, k * P:(k + 1) * P]
                if q == 0 and not first(c, 1):
                    pe.wait_ge(s["y_out"], c.n)
                if q % 2 == 0:
                    mm(o, kvb[:, k, :], qT_f[c.r % 2][:, k, :], start=True, stop=False)
                for i in range(QH):
                    last = mm(o, v_ret[c.r % 2][:, QH * q + i, :], ret_p[q % 2][:, i, :],
                              start=False, stop=(q % 2 == 1 and i == QH - 1))
                last.then_inc(s["ret_done"], 1)

            def att_scores(c, q):
                if q == 0:
                    pe.wait_ge(s["qx_out"], c.n + 1)
                    pe.wait_ge(s_kmask[c.r % 2], SPREAD * (half_of(c) + 1))
                if not (c.fixed and c.n == 0 and q == 0):
                    pe.wait_ge(s["att_exp"], 4 * c.n + q)
                m = k_mask[c.r % 2]
                three(ps_att[:, :], qx_s[:, 0, q // 2, :], qx_s[:, 1, q // 2, :], heads(m, 0, q), heads(m, 1, q),
                      False)
                mm(ps_att[:, :], ident_b, causal_b.unsqueeze(1).to_broadcast([P, QH, T]),
                   start=False, stop=True).then_inc(s["att_scores"], 1)

            def att_turn(c, q):
                pe.wait_ge(s["att_exp"], 4 * c.n + q + 1)
                if not (c.fixed and c.n == 0 and q == 0):
                    pe.wait_ge(s["att_turned_out"], 4 * c.n + q)
                for i in range(QH):
                    last = tr(ps_attT[:, i * P:(i + 1) * P], att_p[q % 2][:, i, :], ident)
                last.then_inc(s["att_turned"], 1)

            def att_values(c, q):
                pe.wait_ge(s["att_turned_out"], 4 * c.n + q + 1)
                if q == 0:
                    pe.wait_ge(s["v_out"], c.n + 1)
                if q % 2 == 0 and not (c.fixed and c.n == 0 and q == 0):
                    pe.wait_ge(s["att_norm"], 2 * c.n + q // 2)
                for i in range(QH):
                    h = QH * q + i
                    o = ps_o[:, (h % HPC) * VW:(h % HPC + 1) * VW]
                    v = v_att[c.r][:, h, :, :].rearrange("p a d -> p (a d)")
                    mm(o, att_hi[q % 2][:, i, :], v, start=True, stop=False)
                    last = mm(o, att_lo[q % 2][:, i, :], v, start=False, stop=True)
                last.then_inc(s["att_done"], 1)

            def gn_mean(c):
                pe.wait_ge(s["gn_sums"], c.n + 1)
                if not first(c, 1):
                    pe.wait_ge(s["qx_out"], c.n)
                mm(ps_g[:, 0:2], mean_w, gsum[:, :], start=True, stop=True).then_inc(s["gn_mean"], 1)

            def y_back(c):
                pe.wait_ge(s["gn_applied"], c.n + 1)
                for k in range(NCH):
                    last = tr(ps_g[:, k * P:(k + 1) * P], yT[:, k, :], ident)
                last.then_inc(s["y_back"], 1)

            def x1_turn(c):
                pe.wait_ge(s["x1_done"], c.n + 1)
                for k in range(NCH):
                    last = tr(ps_g[:, k * P:(k + 1) * P], x1[:, k * P:(k + 1) * P], ident)
                last.then_inc(s["x1_T"], 1)

            def qx(c):
                pe.wait_ge(s["x1_T_out"], c.n + 1)
                for m in range(NCH):
                    for k in range(NCH):
                        last = mm(ps_g[:, m * P:(m + 1) * P], wq_s[:, k, m * P:(m + 1) * P], x1T[:, k, :],
                                  start=(k == 0), stop=(k == NCH - 1))
                last.then_inc(s["qx"], 1)

            def att_back(c):
                pe.wait_ge(s["att_norm"], 2 * (c.n + 1))
                for k in range(NCH):
                    last = tr(bank_g[:, C + k * P:C + (k + 1) * P],
                              att_n[:, k * HPC:(k + 1) * HPC, :].rearrange("p h d -> p (h d)"), ident)
                last.then_inc(s["att_back"], 1)

            def att_proj(c):
                pe.wait_ge(s["att_back_out"], c.n + 1)
                if not first(c, 1):
                    pe.wait_ge(s["placed"], c.n)
                for k in range(NCH):
                    last = mm(ps_f, attT[:, k, :], wo_s[:, k, :], start=(k == 0), stop=(k == NCH - 1))
                last.then_inc(s["att_proj"], 1)

            def x2_turn(c):
                pe.wait_ge(s["x2_done"], c.n + 1)
                for k in range(NCH):
                    last = tr(ps_f[:, k * P:(k + 1) * P], x2_row[c.r % 2][0][:, k * P:(k + 1) * P], ident)
                last.then_inc(s["x2_T"], 1)

            def logits(c):
                pe.wait_ge(s["x2_T_out"], c.n + 1)
                for k in range(NCH):
                    last = mm(ps_f[:, 0:E], x2T[:, k, :], rt_s[:, k, :], start=(k == 0), stop=(k == NCH - 1))
                last.then_inc(s["logits"], 1)

            def rank(c):
                pe.wait_ge(s["picked"], c.n + 1)
                mm(ps_f[:, 0:E], before_b, hot_b[:, :], start=True, stop=True)
                mm(ps_f[:, E:2 * E], ones_b, hot_b[:, :], start=True, stop=True).then_inc(s["ranked"], 1)

            def run(stage, c, *more):
                if c.exists():
                    stage(c, *more)

            prep = [prep_turn, prep_qk, prep_kx, prep_v]

            def step(loop, k):
                for q in range(NQ):
                    run(ret_scores, At(loop, k), q)
                    run(prep[q], At(loop, k + 1))
                    run(att_scores, *quad(loop, k, q, SCORES))
                    run(ret_values, *quad(loop, k, q, 1))
                    if q == 0:
                        run(att_proj, At(loop, k - 4))
                        run(qx, At(loop, k - 2))
                    if q == 1:
                        run(gn_mean, At(loop, k - 1))
                        run(x2_turn, At(loop, k - 4))
                    if q == 2:
                        run(y_back, At(loop, k - 1))
                        run(logits, At(loop, k - 4))
                    if q == 3:
                        run(x1_turn, At(loop, k - 1))
                        run(att_back, At(loop, k - 3))
                        run(rank, At(loop, k - 4))
                    run(att_values, *quad(loop, k, q, VALUES))
                    run(att_turn, *quad(loop, k, q, TURN))

            pe.wait_ge(s["consts"], 16 * CONSTS)
            pe.wait_ge(s["kvb_scaled"], 1)
            for stage in prep:
                stage(At(0, 0))
            pe.wait_ge(s["zeroed"], 1)
            for k in range(LEAD):
                step(0, k)
            with pe.Fori(LEAD // ROUND, B // ROUND - 1) as loop:
                for k in range(ROUND):
                    step(loop, k)
            for k in range(B - ROUND, B + DRAIN):
                step(0, k)

            def turn_rows(g):
                pe.wait_ge(s_rows, 16 * (g + 1))
                for k in range(NCH):
                    for half in range(HALVES):
                        last = tr(ps_xs[:, k * SLOT + half * P:k * SLOT + (half + 1) * P],
                                  rows[:, half, k * P:(k + 1) * P], ident)
                last.then_inc(s["rows_turned"], 1)

            pe.wait_ge(s["chain_first"], 1)
            pe.sem_inc(s["rows_turned"], EVER)
            turn_rows(0)

            def expert(e, par, has_next, has_after):
                n_slots = pe.value_load(tab_i[0:1, 0, ds(e, 1)], min_val=1, max_val=N_TOK // SLOT)
                before = pe.value_load(tab_i[0:1, 1, ds(e, 1)], min_val=0, max_val=(2 * N_TOK) // SLOT + E)
                pe.wait_ge(s["w_ready"], HC * (e + 1))
                apart(pe)
                whi, wlo = w_hi[par], w_lo[par]

                def fc(g, j):
                    if j >= 4:
                        pe.wait_ge(s["h_done"], HC * g + j - 3 + EVER)
                    else:
                        pe.wait_ge(s["h_done"], HC * g + EVER)
                    n = 0
                    for k in range(NCH):
                        at = k * H + j * P
                        for w, v in ((whi, xs_hi), (whi, xs_lo), (wlo, xs_hi)):
                            last = mm(ps_h[j % 4][:, 0:SLOT], w[:, at:at + P], v[:, k, :],
                                      start=(n == 0), stop=(n == 3 * NCH - 1))
                            n += 1
                    last.then_inc(s["fc_done"], 1)

                def proj(g, j):
                    pe.wait_ge(s["h_split"], HC * g + j + 1 + EVER)
                    at = NCH * H + j * C
                    for half in range(HALVES):
                        cols = slice(half * P, (half + 1) * P)
                        for n, (v, w) in enumerate(((h_hi, whi), (h_lo, whi), (h_hi, wlo))):
                            last = mm(ps_out[half][:, 0:C], v[j % 4][:, cols], w[:, at:at + C],
                                      start=(j == 0 and n == 0), stop=(j == HC - 1 and n == 2))
                    last.then_inc(s["y_done"], 1)

                with pe.Fori(0, n_slots) as i:
                    g = before + i
                    pe.wait_ge(s["xs_ready"], g + 1)
                    for j in range(HC + 3):
                        if j < HC:
                            fc(g, j)
                        if j == HC - 1:
                            pass
                        if j >= 3:
                            if j == 3:
                                pe.wait_ge(s["y_biased"], HALVES * g + EVER)
                            proj(g, j - 3)
                        if j == 5:
                            turn_rows(g + 1)

            experts(pe, expert)

        @block.scalar
        def _(act):
            A = nc.scalar.activation

            def prep_T_out(c):
                act.wait_ge(s["prep_T"], c.n + 1)
                A(xcT[:, :, :, :].rearrange("p a k t -> p (a k t)"), ps_prep[:, :], ACT.Copy)\
                    .then_inc(s["prep_T_out"], 1)

            def qk_hi(c):
                act.wait_ge(s["prep_qk"], c.n + 1)
                if not first(c, 2):
                    act.wait_ge(s_qmask[c.r % 2], SPREAD * half_of(c))
                A(qk_s[c.r % 2][:, :, 0].rearrange("p a k t -> p a (k t)"),
                  ps_prep[:, :].rearrange("p (a n) -> p a n", a=2), ACT.Copy)\
                    .then_inc(s["qk_hi"], 1)
                A(qT_f[c.r % 2][:, :, :].rearrange("p k t -> p (k t)"), ps_prep[:, 0:C], ACT.Copy)\
                    .then_inc(s["q_copied"], 1)

            def v_hi(c):
                act.wait_ge(s["prep_v"], c.n + 1)
                for k in range(NCH):
                    flat = v_ret[c.r % 2][:, k * HPC:(k + 1) * HPC, :].rearrange("p h c -> p (h c)")
                    A(diagonal(flat), ps_prep[:, k * P:(k + 1) * P].rearrange("p (h d) -> p h d", d=HD), ACT.Copy)
                A(v_att[c.r][:, :, 0, :], ps_prep[:, C:2 * C].rearrange("p (h d) -> p h d", d=HD), ACT.Copy)\
                    .then_inc(s["v_hi"], 1)

            def kx_hi(c):
                act.wait_ge(s["prep_kx"], c.n + 1)
                if not first(c, 4):
                    act.wait_ge(s_kmask[c.r % 2], SPREAD * (half_of(c) - 1))
                A(kx_s[c.r][:, 0].rearrange("p k t -> p (k t)"), ps_prep[:, 0:C], ACT.Copy)\
                    .then_inc(s["kx_hi"], 1)

            def gn_apply(c):
                act.wait_ge(s["gn_coef"], c.n + 1)
                for k in range(NCH):
                    last = A(yT[:, k, :], y_raw[:, k, :], ACT.Identity, bias=gadd[:, k:k + 1],
                             scale=gmul[:, k:k + 1])
                last.then_inc(s["gn_applied"], 1)

            def x1_T_out(c):
                act.wait_ge(s["x1_T"], c.n + 1)
                if not first(c, 2):
                    act.wait_ge(s["att_back"], c.n - 1)
                A(x1T[:, :, :].rearrange("p k t -> p (k t)"), ps_g, ACT.Copy).then_inc(s["x1_T_out"], 1)

            def qx_hi(c):
                act.wait_ge(s["qx"], c.n + 1)
                A(qx_s[:, 0].rearrange("p k t -> p (k t)"), ps_g, ACT.Copy).then_inc(s["qx_hi"], 1)

            def att_exp(c, q):
                act.wait_ge(s["att_max"], 4 * c.n + q + 1)
                if not (c.fixed and 4 * c.n + q < 2):
                    act.wait_ge(s["att_turned"], 4 * c.n + q - 1)
                for i in range(QH):
                    h = QH * q + i
                    last = A(att_p[q % 2][:, i, :], ps_att[:, i * T:(i + 1) * T], ACT.Exp,
                             bias=neg_max[c.r % 2][:, h:h + 1], scale=SCALE,
                             accum_out=den[c.r % 2][:, h:h + 1])
                last.then_inc(s["att_exp"], 1)

            def att_hi_out(c, q):
                act.wait_ge(s["att_turned"], 4 * c.n + q + 1)
                if not (c.fixed and 4 * c.n + q < 2):
                    act.wait_ge(s["att_done"], 4 * c.n + q - 1)
                A(att_hi[q % 2][:, :, :].rearrange("p h t -> p (h t)"), ps_attT[:, :], ACT.Copy)\
                    .then_inc(s["att_hi_out"], 1)

            def att_back_out(c):
                act.wait_ge(s["att_back"], c.n + 1)
                A(attT[:, :, :].rearrange("p k t -> p (k t)"), bank_g[:, C:2 * C], ACT.Copy)\
                    .then_inc(s["att_back_out"], 1)

            def x2_T_out(c):
                act.wait_ge(s["x2_T"], c.n + 1)
                A(x2T[:, :, :].rearrange("p k t -> p (k t)"), ps_f, ACT.Copy).then_inc(s["x2_T_out"], 1)

            def gap_exp(c):
                act.wait_ge(s["gap_done"], c.n + 1)
                A(gap_e[:, :], gap[:, :], ACT.Exp).then_inc(s["gap_exp"], 1)

            def run(stage, c, *more):
                if c.exists():
                    stage(c, *more)

            def step(loop, k):
                for q in range(NQ):
                    run(att_hi_out, *quad(loop, k, q, VALUES))
                    if q == 0:
                        run(prep_T_out, At(loop, k + 1))
                    if q == 1:
                        run(qk_hi, At(loop, k + 1))
                    if q == 2:
                        run(gn_apply, At(loop, k - 1))
                        run(kx_hi, At(loop, k + 1))
                    if q == 3:
                        run(gap_exp, At(loop, k - 4))
                        run(v_hi, At(loop, k + 1))
                    run(att_exp, *quad(loop, k, q, SCORES))
                    if q == 0:
                        run(qx_hi, At(loop, k - 2))
                    if q == 1:
                        run(x2_T_out, At(loop, k - 4))
                    if q == 3:
                        run(att_back_out, At(loop, k - 3))
                        run(x1_T_out, At(loop, k - 1))

            act.wait_ge(s["consts"], 16 * CONSTS)
            A(bits[:, :], bits_f, ACT.Copy)
            A(kvb[:, :, :], kvb_raw, ACT.Copy, scale=CROSS).then_inc(s["kvb_scaled"], 1)
            act.wait_ge(s["cleared"], 1)
            prep_T_out(At(0, 0))
            qk_hi(At(0, 0))
            kx_hi(At(0, 0))
            v_hi(At(0, 0))
            for k in range(LEAD):
                step(0, k)
            with act.Fori(LEAD // ROUND, B // ROUND - 1) as loop:
                for k in range(ROUND):
                    step(loop, k)
            for k in range(B - ROUND, B + DRAIN):
                step(0, k)

            act.wait_ge(s["ret_scores"], 4 * B)
            PIECE = WROW // HC

            def split_hi(e, par, j):
                at = slice(j * PIECE, (j + 1) * PIECE)
                if j == 0:
                    act.wait_ge(s_wraw, 32 * (e + 1))
                A(w_hi[par][:, at], w_raw[:, at], ACT.Copy).then_inc(s["raw_hi"], 1)

            for j in range(HC):
                split_hi(0, 0, j)
            act.wait_ge(s["tab_ready"], 1)
            act.sem_inc(s["h_done"], EVER)

            def expert(e, par, has_next, has_after):
                n_slots = act.value_load(tab_i[0:1, 0, ds(e, 1)], min_val=1, max_val=N_TOK // SLOT)
                before = act.value_load(tab_i[0:1, 1, ds(e, 1)], min_val=0, max_val=(2 * N_TOK) // SLOT + E)

                def slot(g, split):
                    for j in range(HC):
                        act.wait_ge(s["fc_done"], HC * g + j + 1)
                        if j >= 2:
                            act.wait_ge(s["h_split"], HC * g + j - 1 + EVER)
                        else:
                            act.wait_ge(s["h_split"], HC * g + EVER)
                        apart(act)
                        A(h_f[j % 2][:, :], ps_h[j % 4][:, 0:SLOT], ACT.Gelu_apprx_tanh,
                          bias=bfc_s[:, ds(e, 1), j:j + 1].rearrange("p e j -> p (e j)")
                          if not isinstance(e, int) else bfc_s[:, e, j:j + 1]).then_inc(s["h_done"], 1)
                        if split:
                            split_hi(e + 1, 1 - par, j)

                slot(before, has_next)
                with act.If(n_slots > 1):
                    with act.Fori(1, n_slots) as i:
                        slot(before + i, False)

            experts(act, expert)

            for b in range(NLAST):
                act.wait_ge(s["last_rstd"], b + 1)
                if b >= 2:
                    act.wait_ge(s_stored[b % 2], 16 * (b // 2))
                for j in (1, 3):
                    A(last_out[b % 2][:, j, :], last_in[b % 2][:, j, :], ACT.Identity,
                      bias=last_nm[:, b % 2, j:j + 1], scale=last_rs[:, b % 2, j:j + 1])\
                        .then_inc(s["last_act"], 1)


        @block.vector
        def _(dve):
            V = nc.vector

            def low(dst, value, hi, wait, done, c, more=()):
                dve.wait_ge(s[wait], c.n + 1)
                for sem_, v in more:
                    dve.wait_ge(sem_, v)
                V.tensor_tensor(dst, value, hi, ALU.subtract).then_inc(s[done], 1)

            def qk_out(c):
                a, flat = qk_s[c.r % 2], "p a k t -> p a (k t)"
                low(a[:, :, 1].rearrange(flat), ps_prep[:, :].rearrange("p (a n) -> p a n", a=2),
                    a[:, :, 0].bitcast(f32).rearrange(flat), "qk_hi", "qk_out", c, [(s["q_copied"], c.n + 1)])

            def v_left(c):
                low(v_rest[c.r % 2][:, :, :], ps_prep[:, C:2 * C].rearrange("p (h d) -> p h d", d=HD),
                    v_att[c.r][:, :, 0, :], "v_hi", "v_left", c, [] if first(c, 2) else [(s["v_out"], c.n - 1)])

            def kx_out(c):
                a, flat = kx_s[c.r], "p k t -> p (k t)"
                low(a[:, 1].rearrange(flat), ps_prep[:, 0:C], a[:, 0].bitcast(f32).rearrange(flat), "kx_hi",
                    "kx_out", c)

            def qx_out(c):
                a, flat = qx_s, "p k t -> p (k t)"
                low(a[:, 1].rearrange(flat), ps_g, a[:, 0].bitcast(f32).rearrange(flat), "qx_hi", "qx_out", c)

            def att_turned_out(c, q):
                dve.wait_ge(s["att_hi_out"], 4 * c.n + q + 1)
                V.tensor_tensor(att_lo[q % 2][:, :, :].rearrange("p h t -> p (h t)"), ps_attT[:, :],
                                att_hi[q % 2][:, :, :].rearrange("p h t -> p (h t)"), ALU.subtract)\
                    .then_inc(s["att_turned_out"], 1)

            def ret_decay(c, q):
                dve.wait_ge(s["ret_scores"], 4 * c.n + q + 1)
                if not (c.fixed and 4 * c.n + q < 2):
                    dve.wait_ge(s["ret_done"], 4 * c.n + q - 1)
                V.tensor_tensor(ret_p[q % 2][:, :, :].rearrange("p h t -> p (h t)"), ps_ret[:, :],
                                decay[:, QH * q:QH * (q + 1), :].rearrange("p h t -> p (h t)"),
                                ALU.mult).then_inc(s["ret_decayed"], 1)

            def att_max(c, q):
                dve.wait_ge(s["att_scores"], 4 * c.n + q + 1)
                hs = slice(QH * q, QH * (q + 1))
                V.reduce_max(row_max[c.r % 2][:, hs], ps_att[:, :].rearrange("p (h s) -> p h s", s=T), AX.X)\
                    .then_inc(s["nm_chain"], 1)
                dve.wait_ge(s["nm_chain"], 4 * c.n + q + 1)
                V.tensor_scalar(neg_max[c.r % 2][:, hs], row_max[c.r % 2][:, hs], -SCALE, LIFT, ALU.mult,
                                ALU.add)\
                    .then_inc(s["att_max"], 1)

            def y_out(c):
                dve.wait_ge(s["ret_done"], 4 * (c.n + 1))
                V.tensor_copy(y_raw[:, :, :].rearrange("p k t -> p (k t)"), ps_y[:, 0:C]).then_inc(s["y_out"], 1)
                dve.wait_ge(s["y_out"], c.n + 1)
                ch = Chain(dve, s["gn_chain"], GN * c.n)
                ch.link(V.bn_stats(gst[:, :], y_raw[:, :, :].rearrange("p k t -> p (k t)")), apart)
                ch.link(V.bn_aggr(gmv[:, :], gst[:, :]))
                ch.link(V.tensor_tensor(gsq[:, :], gmv[:, 0:1], gmv[:, 0:1], ALU.mult))
                V.tensor_copy(gsum[:, 0:1], gmv[:, 0:1])
                V.tensor_tensor(gsum[:, 1:2], gsq[:, :], gmv[:, 1:2], ALU.add).then_inc(s["gn_sums"], 1)

            def gn_var(c):
                dve.wait_ge(s["gn_mean"], c.n + 1)
                ch = Chain(dve, s["gn_chain"], GN * c.n + 3)
                ch.link(V.tensor_copy(gtot[:, :], ps_g[:, 0:2]))
                ch.link(V.tensor_tensor(gsq[:, :], gtot[:, 0:1], gtot[:, 0:1], ALU.mult))
                ch.link(V.scalar_tensor_tensor(out=gvar[:, :], in0=gtot[:, 1:2], scalar=EPS, in1=gsq[:, :],
                                               op0=ALU.add, op1=ALU.subtract))
                dve.sem_inc(s["gn_var"], 1)

            def gn_coef(c):
                dve.wait_ge(s["gn_rstd"], c.n + 1)
                V.tensor_scalar(gmul[:, :], gnw[:, :], grstd[:, 0:1], None, ALU.mult)\
                    .then_inc(s["pool_small"], 1)
                dve.wait_ge(s["pool_small"], 2 * c.n + 1)
                V.tensor_scalar(gadd[:, :], gmul[:, :], gtot[:, 0:1], None, ALU.mult)\
                    .then_inc(s["pool_small"], 1)
                dve.wait_ge(s["pool_small"], 2 * c.n + 2)
                V.tensor_tensor(gadd[:, :], gnb[:, :], gadd[:, :], ALU.subtract).then_inc(s["gn_coef"], 1)

            def ln1_stats(c):
                dve.wait_ge(s["y_back"], c.n + 1)
                ch = Chain(dve, s["ln1_chain"], LN1 * c.n)
                ch.link(V.tensor_tensor(x1_pre[:, :], ps_g, x_t[c.r][:, :], ALU.add))
                ch.link(V.bn_stats(l1st[:, :], x1_pre[:, :]), apart)
                ch.link(V.bn_aggr(l1mv[:, :], l1st[:, :]))
                V.tensor_scalar(l1var[:, :], l1mv[:, 1:2], EPS, None, ALU.add).then_inc(s["ln1_var"], 1)

            def ln1_norm(c):
                dve.wait_ge(s["ln1_rstd"], c.n + 1)
                if not first(c, 1):
                    dve.wait_ge(s["x1_bo_done"], c.n)
                V.tensor_scalar(x1[:, :], x1_pre[:, :], l1mv[:, 0:1], l1rstd[:, 0:1], ALU.subtract, ALU.mult)\
                    .then_inc(s["x1_done"], 1)

            def att_norm(c, half):
                hs = slice(half * HPC, (half + 1) * HPC)
                dve.wait_ge(s["att_exp"], 4 * c.n + 2 * (half + 1))
                V.reciprocal(rden[:, hs], den[c.r % 2][:, hs]).then_inc(s["sum_chain"], 1)
                dve.wait_ge(s["att_done"], 4 * c.n + 2 * (half + 1))
                if half == 0 and not first(c, 1):
                    dve.wait_ge(s["att_back"], c.n)
                V.reduce_sum(att_sum[:, :, :],
                             ps_o[:, 0:HPC * VW].rearrange("p (h a d) -> p h d a", h=HPC, a=VP), AX.X)\
                    .then_inc(s["sum_chain"], 1)
                dve.wait_ge(s["sum_chain"], 4 * c.n + 2 * (half + 1))
                V.tensor_tensor(att_n[:, hs, :], att_sum[:, :, :],
                                rden[:, hs].unsqueeze(2).to_broadcast([P, HPC, HD]), ALU.mult)\
                    .then_inc(s["att_norm"], 1)

            def ln2_stats(c):
                dve.wait_ge(s["att_proj"], c.n + 1)
                ch = Chain(dve, s["ln2_chain"], LN2 * c.n)
                ch.link(V.tensor_tensor(x2_pre[:, :], ps_f, x1_bo[c.r][:, :], ALU.add))
                ch.link(V.bn_stats(l2st[:, :], x2_pre[:, :]), apart)
                ch.link(V.bn_aggr(l2mv[:, :], l2st[:, :]))
                V.tensor_scalar(l2var[:, :], l2mv[:, 1:2], EPS, None, ALU.add).then_inc(s["ln2_var"], 1)

            def ln2_norm(c):
                dve.wait_ge(s["ln2_rstd"], c.n + 1)
                if not first(c, 2):
                    dve.wait_ge(s_sent[c.r % 2], 32 * half_of(c))
                    dve.wait_ge(s_total[c.r % 2], 16 * half_of(c))
                for k in (1, 0):
                    last = V.tensor_scalar(x2_row[c.r % 2][k][:, 0:C], x2_pre[:, :], l2mv[:, 0:1],
                                           l2rstd[:, 0:1], ALU.subtract, ALU.mult)
                last.then_inc(s["x2_done"], 1)

            def pick(c):
                dve.wait_ge(s["logits"], c.n + 1)
                ch = Chain(dve, s["top_chain"], TOP * c.n)
                ch.link(V.tensor_copy(lg[:, :], ps_f[:, 0:E]), apart)
                ch.link(V.max(top[:, :], lg[:, :]))
                V.tensor_tensor(gap[:, :], top[:, 1:2], top[:, 0:1], ALU.subtract).then_inc(s["gap_done"], 1)
                ch.link(V.max_index(top_i[:, :], top[:, :], lg[:, :]))
                ch.link(V.tensor_copy(top_f[:, :], top_i[:, 0:2]))
                ch.link(V.tensor_tensor(hot[:, :, :], lanes8.unsqueeze(1).to_broadcast([P, 2, E]),
                                        top_f[:, :].unsqueeze(2).to_broadcast([P, 2, E]), ALU.is_equal))
                V.tensor_tensor(hot_b[:, :], hot[:, 0, :], hot[:, 1, :], ALU.add).then_inc(s["picked"], 1)

            def put(c):
                ch = Chain(dve, s["top_chain"], TOP * c.n + 5)
                row1, row2 = x2_row[c.r % 2]
                dve.wait_ge(s["gap_exp"], c.n + 1)
                ch.link(V.tensor_scalar(gap_s[:, :], gap_e[:, :], 1.0, None, ALU.add))
                ch.link(V.reciprocal(row1[:, C:C + 1], gap_s[:, :]))
                V.tensor_tensor(row2[:, C:C + 1], gap_e[:, :], row1[:, C:C + 1], ALU.mult)
                V.tensor_copy(row1[:, C + 1:C + 2], tok[:, :])
                ch.link(V.tensor_copy(row2[:, C + 1:C + 2], tok[:, :]))
                V.tensor_scalar(tok[:, :], tok[:, :], float(T), None, ALU.add)
                dve.wait_ge(s["ranked"], c.n + 1)
                ch.link(V.tensor_tensor(place[:, :], ps_f[:, 0:E], filled[:, :], ALU.add))
                V.tensor_tensor(filled[:, :], ps_f[:, E:2 * E], filled[:, :], ALU.add)
                ch.link(V.tensor_tensor(place2[:, :, :], hot[:, :, :],
                                        place[:, :].unsqueeze(1).to_broadcast([P, 2, E]), ALU.mult))
                ch.link(V.reduce_sum(pos_f[:, :], place2[:, :, :], AX.X))
                ch.link(V.tensor_copy(pos[c.r % 2][:, :], pos_f[:, :]))
                dve.sem_inc(s["placed"], 1)

            def run(stage, c, *more):
                if c.exists():
                    stage(c, *more)

            def step(loop, k):
                for q in range(NQ):
                    run(ret_decay, At(loop, k), q)
                    run(att_turned_out, *quad(loop, k, q, VALUES))
                    if q == 1:
                        run(ln2_norm, At(loop, k - 4))
                    if q == 2:
                        run(gn_coef, At(loop, k - 1))
                    if q == 3:
                        run(ln1_norm, At(loop, k - 1))
                    run(att_max, *quad(loop, k, q, SCORES))
                    if q == 0:
                        run(y_out, At(loop, k - 1))
                        run(ln2_stats, At(loop, k - 4))
                        run(qx_out, At(loop, k - 2))
                        run(att_norm, At(loop, k - 3), 0)
                    if q == 1:
                        run(qk_out, At(loop, k + 1))
                        run(gn_var, At(loop, k - 1))
                    if q == 2:
                        run(kx_out, At(loop, k + 1))
                        run(ln1_stats, At(loop, k - 1))
                        run(pick, At(loop, k - 4))
                        run(att_norm, At(loop, k - 3), 1)
                    if q == 3:
                        run(v_left, At(loop, k + 1))
                        run(put, At(loop, k - 4))

            for t in v_ret:
                V.memset(t[:, :, :], 0.0)
            for t in (q_mask[0], q_mask[1], k_mask[0], k_mask[1]):
                last = V.memset(t[:, :, :, :].bitcast(f32), 0.0)
            last.then_inc(s["cleared"], 1)
            dve.wait_ge(s["consts"], 16 * CONSTS)
            V.tensor_copy(filled[:, :], region)
            V.tensor_copy(tok[:, :], lane).then_inc(s["zeroed"], 1)
            dve.wait_ge(s["zeroed"], 1)
            qk_out(At(0, 0))
            kx_out(At(0, 0))
            v_left(At(0, 0))
            for k in range(LEAD):
                step(0, k)
            with dve.Fori(LEAD // ROUND, B // ROUND - 1) as loop:
                for k in range(ROUND):
                    step(loop, k)
            for k in range(B - ROUND, B + DRAIN):
                step(0, k)

            ch = Chain(dve, s["tab_chain"], 0)
            row = tab_f
            ch.link(V.memset(row[0:1, 3, :], 1.0))
            ch.link(V.tensor_tensor(row[0:1, 2, :], filled[0:1, :], region[0:1, :], ALU.subtract))
            ch.link(V.tensor_scalar(row[0:1, 0, :], row[0:1, 2, :], float(SLOT - 1), None, ALU.add))
            ch.link(V.tensor_copy(tab_i[0:1, 0, :], row[0:1, 0, :]))
            ch.link(V.tensor_scalar(tab_i[0:1, 1, :], tab_i[0:1, 0, :], SLOT.bit_length() - 1, None,
                                    ALU.logical_shift_right))
            ch.link(V.tensor_copy(row[0:1, 0, :], tab_i[0:1, 1, :]))
            ch.link(V.tensor_scalar(row[0:1, 0, :], row[0:1, 0, :], 1.0, None, ALU.max))
            ch.link(V.tensor_tensor_scan(row[0:1, 1, :], row[0:1, 3, :], row[0:1, 0, :], 0.0,
                                         ALU.mult, ALU.add))
            ch.link(V.tensor_copy(row[0:1, 3, 0:1], row[0:1, 1, E - 1:E]))
            ch.link(V.tensor_scalar(row[0:1, 3, 1:2], row[0:1, 1, E - 1:E], float(16 * HALVES), None, ALU.mult))
            ch.link(V.tensor_tensor(row[0:1, 1, :], row[0:1, 1, :], row[0:1, 0, :], ALU.subtract))
            V.tensor_copy(tab_i[0:1, :, :], row[0:1, :, :]).then_inc(s["tab_ready"], 1)
            dve.wait_ge(s["tab_ready"], 1)
            dve.sem_inc(s["chain_first"], 1)

            PIECE = WROW // HC

            def split_lo(e, par, j):
                at = slice(j * PIECE, (j + 1) * PIECE)
                dve.wait_ge(s["raw_hi"], HC * e + j + 1)
                last = V.tensor_tensor(w_lo[par][:, at], w_raw[:, at], w_hi[par][:, at].bitcast(f32),
                                       ALU.subtract)
                last.then_inc(s["w_ready"], 1)
                if j == HC - 1:
                    dve.wait_ge(s["w_ready"], HC * (e + 1))
                    dve.sem_inc(s["raw_split"], 1)

            for j in range(HC):
                split_lo(0, 0, j)

            def take_rows(g):
                dve.wait_ge(s_rows, 16 * (g + 1))
                V.tensor_copy(meta_next[:, :, :], rows[:, :, C:ROW]).then_inc(s["meta_ready"], 1)

            def split_rows(g):
                dve.wait_ge(s["rows_turned"], g + 1 + EVER)
                flat = xs_hi[:, :, :].rearrange("p k t -> p (k t)")
                V.tensor_copy(flat, ps_xs[:, :]).then_inc(s["xs_chain"], 1)
                dve.wait_ge(s["xs_chain"], g + 1)
                V.tensor_tensor(xs_lo[:, :, :].rearrange("p k t -> p (k t)"), ps_xs[:, :],
                                flat.bitcast(f32), ALU.subtract).then_inc(s["xs_ready"], 1)

            for name in ("meta_ready", "h_split", "y_biased"):
                dve.sem_inc(s[name], EVER)
            take_rows(0)
            split_rows(0)

            def expert(e, par, has_next, has_after):
                n_slots = dve.value_load(tab_i[0:1, 0, ds(e, 1)], min_val=1, max_val=N_TOK // SLOT)
                before = dve.value_load(tab_i[0:1, 1, ds(e, 1)], min_val=0, max_val=(2 * N_TOK) // SLOT + E)

                def slot(g, split):
                    for j in range(HC):
                        dve.wait_ge(s["h_done"], HC * g + j + 1 + EVER)
                        if j >= 4:
                            dve.wait_ge(s["y_done"], HC * g + j - 3)
                        V.tensor_copy(h_hi[j % 4][:, :], h_f[j % 2][:, :]).then_inc(s["h_chain"], 1)
                        dve.wait_ge(s["h_chain"], HC * g + j + 1)
                        V.tensor_tensor(h_lo[j % 4][:, :], h_f[j % 2][:, :], h_hi[j % 4][:, :].bitcast(f32),
                                        ALU.subtract).then_inc(s["h_split"], 1)
                        if split:
                            split_lo(e + 1, 1 - par, j)
                    dve.wait_ge(s_added, 16 * (HALVES * g + EVER))
                    dve.wait_ge(s["meta_ready"], g + 1 + EVER)
                    V.tensor_copy(meta[:, :, :], meta_next[:, :, :]).then_inc(s["y_chain"], 1)
                    dve.wait_ge(s["y_chain"], g + 1)
                    V.tensor_copy(meta_i[:, :], meta[:, :, 1])
                    take_rows(g + 1)
                    split_rows(g + 1)
                    dve.wait_ge(s["y_done"], HC * (g + 1))
                    for half in range(HALVES):
                        bias = bproj_s[:, e, :] if isinstance(e, int) else \
                            bproj_s[:, ds(e, 1), :].rearrange("p e c -> p (e c)")
                        V.tensor_tensor(y_b[:, half, :], ps_out[half][:, 0:C], bias, ALU.add)\
                            .then_inc(s["y_biased"], 1)

                slot(before, has_next)
                with dve.If(n_slots > 1):
                    with dve.Fori(1, n_slots) as i:
                        slot(before + i, False)

            experts(dve, expert)

            for b in range(NLAST):
                dve.wait_ge(s_last[b % 2], 16 * (b // 2 + 1))
                ch = Chain(dve, s["last_chain"], 3 * b)
                for j in range(4):
                    last = V.bn_stats(last_st[:, j, :], last_in[b % 2][:, j, :])
                ch.link(last)
                if b >= 2:
                    dve.wait_ge(s["last_act"], 2 * (b - 1))
                for j in range(4):
                    last = V.bn_aggr(last_mv[:, b % 2, j, :], last_st[:, j, :])
                ch.link(last)
                V.tensor_scalar(last_ve[:, b % 2, :], last_mv[:, b % 2, :, 1], EPS, None, ALU.add)\
                    .then_inc(s["last_var"], 1)
                dve.wait_ge(s["last_rstd_raw"], b + 1)
                ch.link(V.tensor_tensor(last_nm[:, b % 2, :], last_mv[:, b % 2, :, 0], last_rs[:, b % 2, :],
                                        ALU.mult))
                V.tensor_scalar(last_nm[:, b % 2, :], last_nm[:, b % 2, :], -1.0, None, ALU.mult)\
                    .then_inc(s["last_rstd"], 1)
                if b >= 2:
                    dve.wait_ge(s_stored[b % 2], 16 * (b // 2))
                for j in (0, 2):
                    V.tensor_scalar(last_out[b % 2][:, j, :], last_in[b % 2][:, j, :],
                                    last_mv[:, b % 2, j, 0:1], last_rs[:, b % 2, j:j + 1],
                                    ALU.subtract, ALU.mult).then_inc(s["last_dve"], 1)

        @block.gpsimd
        def _(pool):
            G = nc.gpsimd

            def v_parts(c):
                v = v_att[c.r]
                pool.wait_ge(s["v_left"], c.n + 1)
                apart(pool)
                G.tensor_copy(v[:, :, 1, :], v_rest[c.r % 2][:, :, :]).then_inc(s["v_mid"], 1)
                pool.wait_ge(s["v_mid"], c.n + 1)
                G.tensor_tensor(v[:, :, 2, :], v_rest[c.r % 2][:, :, :], v[:, :, 1, :], ALU.subtract)\
                    .then_inc(s["v_out"], 1)

            def rstd(out_ap, var_ap, wait, done, c):
                pool.wait_ge(s[wait], c.n + 1)
                G.tensor_tensor(out_ap, var_ap, half_neg[:, 0:1], ALU.pow).then_inc(s[done], 1)

            def x1_bo_(c):
                pool.wait_ge(s["x1_done"], c.n + 1)
                if not first(c, 4):
                    pool.wait_ge(s["ln2_chain"], LN2 * (c.n - 4) + 1)
                G.tensor_tensor(x1_bo[c.r][:, :], x1[:, :], bo_s[:, :], ALU.add).then_inc(s["x1_bo_done"], 1)

            def send(c):
                pool.wait_ge(s["placed"], c.n + 1)
                apart(pool)
                for k in range(2):
                    G.indirect_dma_start(sent_flat, bass.IndirectOffsetOnAxis(pos[c.r % 2][:, k:k + 1], 0),
                                         x2_row[c.r % 2][k][:, :], None).then_inc(s_sent[c.r % 2], 16)

            def run(stage, c, *more):
                if c.exists():
                    stage(c, *more)

            def step(loop, k):
                if At(loop, k - 4).exists():
                    rstd(l2rstd[:, :], l2var[:, :], "ln2_var", "ln2_rstd", At(loop, k - 4))
                if At(loop, k - 1).exists():
                    rstd(grstd[:, :], gvar[:, :], "gn_var", "gn_rstd", At(loop, k - 1))
                    rstd(l1rstd[:, :], l1var[:, :], "ln1_var", "ln1_rstd", At(loop, k - 1))
                run(x1_bo_, At(loop, k - 1))
                run(v_parts, At(loop, k + 1))
                run(send, At(loop, k - 4))

            pool.wait_ge(s["consts"], 16 * CONSTS)
            v_parts(At(0, 0))
            for k in range(LEAD):
                step(0, k)
            with pool.Fori(LEAD // ROUND, B // ROUND - 1) as loop:
                for k in range(ROUND):
                    step(loop, k)
            for k in range(B - ROUND, B + DRAIN):
                step(0, k)
            for par in range(2):
                pool.wait_ge(s_sent[par], 16 * B)
                pool.wait_ge(s_total[par], 16 * (B // 2))
            pool.wait_ge(s_pad, 16 * E * HALVES)
            pool.wait_ge(s["tab_ready"], 1)
            G.dma_start(total[N_TOK:N_TOK + P, :], pad_row[:, 0:C]).then_inc(s_added, 16 * EVER)

            def expert(e, par, has_next, has_after):
                n_slots = pool.value_load(tab_i[0:1, 0, ds(e, 1)], min_val=1, max_val=N_TOK // SLOT)
                before = pool.value_load(tab_i[0:1, 1, ds(e, 1)], min_val=0, max_val=(2 * N_TOK) // SLOT + E)
                with pool.Fori(0, n_slots) as i:
                    g = before + i
                    for half in range(HALVES):
                        pool.wait_ge(s["y_biased"], HALVES * g + half + 1 + EVER)
                        apart(pool)
                        G.tensor_scalar(y_w[:, half, :], y_b[:, half, :], meta[:, half, 0:1], None, ALU.mult)\
                            .then_inc(s["y_weighted"], 1)
                        pool.wait_ge(s["y_weighted"], HALVES * g + half + 1)
                        pool.wait_ge(s_added, 16 * (HALVES * g + half + EVER))
                        apart(pool)
                        G.indirect_dma_start(total, bass.IndirectOffsetOnAxis(meta_i[:, half:half + 1], 0),
                                             y_w[:, half, :], None, compute_op=ALU.add).then_inc(s_added, 16)

            experts(pool, expert)
            for b in range(NLAST):
                pool.wait_ge(s["last_var"], b + 1)
                G.tensor_tensor(last_rs[:, b % 2, :], last_ve[:, b % 2, :], half_neg[:, 0:4], ALU.pow)\
                    .then_inc(s["last_rstd_raw"], 1)


def shape_constants():
    gamma = 1.0 - 2.0 ** (-5.0 - np.arange(NH, dtype=np.float64))
    t = np.arange(T)
    diff = t[None, :] - t[:, None]
    power = np.where(diff >= 0, gamma[:, None, None] ** np.maximum(diff, 0), 0.0)
    decay = np.ascontiguousarray(power.transpose(1, 0, 2)).astype(np.float32)
    p = np.arange(P)
    small = np.zeros((P, 2 * P + 32 + ROW), np.float32)
    small[:, 0:P] = np.eye(P)
    small[:, P:2 * P] = 1.0 / P
    small[:, 2 * P:2 * P + HPC] = p[:, None] // HD == np.arange(HPC)[None, :]
    small[:, 2 * P + 8:2 * P + 16] = np.arange(E) * CAP
    small[:, 2 * P + 16:2 * P + 24] = np.arange(E)
    small[:, 2 * P + 24] = p
    small[:, 2 * P + 25:2 * P + 29] = -0.5
    small[:, 2 * P + 32 + C + 1] = N_TOK + p
    bits = np.zeros((P, 4 * P), np.float32)
    bits[:, 0:P] = np.eye(P)
    bits[:, P:2 * P] = np.where(p[None, :] <= p[:, None], 0.0, NEG)
    bits[:, 2 * P:3 * P] = p[:, None] < p[None, :]
    bits[:, 3 * P:4 * P] = 1.0
    return decay, small, bits


def kernel(**inputs):
    import concourse.bacc as _bacc
    from concourse.bass_utils import run_bass_kernel_spmd as _run

    a = {k: np.asarray(v) for k, v in inputs.items()}
    kv = a["L0_attn_past_kv"]
    blocks = np.zeros((NCH, P, P), kv.dtype)
    for h in range(NH):
        at = (h % HPC) * HD
        blocks[h // HPC, at:at + HD, at:at + HD] = kv[h]

    def per_channel(v):
        return np.repeat(v, HD).reshape(NCH, P).T

    decay, small, bits = shape_constants()
    data = {
        "x": a["x"], "ctx_in": a["ctx_1024"], "kv_blocks": blocks, "w_qkv": a["L0_attn_W_qkv"],
        "gn_scale": per_channel(a["L0_attn_gn_weight"]), "gn_shift": per_channel(a["L0_attn_gn_bias"]),
        "wq_t": a["L0_xattn_Wq"].T, "wk_t": a["L0_xattn_Wk"].T, "wv_t": a["L0_xattn_Wv"].T,
        "wo_t": a["L0_xattn_Wo"].T, "bo": a["L0_xattn_bo"], "router_t": a["L0_ffn_router_w"].T,
        "w_fc": a["L0_ffn_w_fc"],
        "b_fc": a["L0_ffn_b_fc"].reshape(E, HC, P).transpose(2, 0, 1),
        "w_proj": a["L0_ffn_w_proj"], "b_proj": a["L0_ffn_b_proj"],
        "decay_c": decay, "small_c": small, "bits_c": bits,
    }
    nc = _bacc.Bacc("TRN2", target_bir_lowering=False, num_devices=1)
    arrays, args = {}, []
    for name, v in data.items():
        v = np.ascontiguousarray(v)
        arrays[f"in_{name}"] = v
        args.append(nc.dram_tensor(f"in_{name}", v.shape, mybir.dt.from_np(v.dtype), kind="ExternalInput").ap())
    out = nc.dram_tensor("result", (B, T, C), mybir.dt.float32, kind="ExternalOutput").ap()
    decoder_kernel(nc, *args, out)
    r = _run(nc, [arrays], core_ids=[0])
    return r.results[0]["result"]
```

```python
import concourse.bass as bass
from concourse import mybir
from contextlib import ExitStack
import numpy as np

B, T, C = 32, 128, 256
N_TOK = B * T
NH, HD = 16, 16
E, H = 8, 1024
P = 128
NCH = C // P
HPC = P // HD
QH = 4
NQ = NH // QH
HC = H // P
SLOT = 256
HALVES = SLOT // P
ROW = C + 2
CAP = N_TOK + SLOT
EPS = 1e-5
SCALE = 1.0 / float(np.sqrt(HD))
CROSS = float(NH * HD)
NEG = -1.0e30
LIFT = 12.0 * float(np.log(2.0))
VP = 3
VW = VP * HD
SCORES, TURN, VALUES = 9, 10, 11
LEAD = 8
ROUND = 4
SPREAD = 16 * HPC
SPLIT = B + 1
DRAIN = 4


class At:

    def __init__(self, loop, k):
        self.n = ROUND * loop + k
        self.r = k % ROUND
        self.g = loop + k // ROUND
        self.fixed = isinstance(loop, int)

    def exists(self):
        return not self.fixed or 0 <= self.n < B


class Chain:

    def __init__(self, eng, sem, base):
        self.eng, self.sem, self.base, self.k = eng, sem, base, 0

    def link(self, ins, then=None):
        ins.then_inc(self.sem, 1)
        self.k += 1
        self.eng.wait_ge(self.sem, self.base + self.k)
        if then:
            then(self.eng)


def decoder_kernel(nc, x, ctx_in, kv_blocks, w_qkv, gn_scale, gn_shift, wq_t, wk_t, wv_t, wo_t, bo,
                   router_t, w_fc, b_fc, w_proj, b_proj, decay_c, small_c, bits_c, out):
    f32, f32r, bf16, f16 = mybir.dt.float32, mybir.dt.float32r, mybir.dt.bfloat16, mybir.dt.float16
    i32, u32 = mybir.dt.int32, mybir.dt.uint32
    ALU, ACT, AX = mybir.AluOpType, mybir.ActivationFunctionType, mybir.AxisListType
    ds = bass.ds

    ctx = ExitStack()
    with ctx:
        def sb(name, shape, dt=f32):
            return ctx.enter_context(nc.sbuf_tensor(name, shape, dt))

        attention = ExitStack()

        def ab(name, shape, dt=f32):
            return attention.enter_context(nc.sbuf_tensor(name, shape, dt))

        def sem(name):
            return ctx.enter_context(nc.semaphore(name))

        sent = nc.dram_tensor("sent_rows", [E, CAP, ROW], f32, kind="Internal").ap()
        sent_flat = sent.rearrange("e r c -> (e r) c")
        total = nc.dram_tensor("residual_sum", [N_TOK + P, C], f32, kind="Internal").ap()

        small = sb("small", [P, small_c.shape[1]])
        bits = sb("bits", [P, 4 * P], bf16)
        bfc_s = sb("bfc_s", [P, E, HC])
        bproj_s = sb("bproj_s", [P, E, C])
        x2_row = [[sb(f"x2_row{i}_{k}", [P, ROW]) for k in range(2)] for i in range(2)]
        pos = [sb(f"pos{i}", [P, 2], u32) for i in range(2)]
        filled = sb("filled", [P, E])
        gelu_warm = sb("gelu_warm", [P, 1])
        tab_f = sb("tab_f", [1, 4, E])
        tab_i = sb("tab_i", [1, 4, E], i32)

        WROW = NCH * H + HC * C
        w_raw = sb("w_raw", [P, WROW])
        q_mask = [sb(f"q_mask{i}", [P, 2, NH, T], f32r) for i in range(2)]

        decay = ab("decay", [P, NH, T])
        ident, mean_w = small[:, 0:P], small[:, P:2 * P]
        eps_c, minus_one, one_c, t_c = (small[:, 2 * P + i:2 * P + i + 1] for i in range(4))
        region = small[:, 2 * P + 8:2 * P + 16]
        lanes8 = small[:, 2 * P + 16:2 * P + 24]
        lane = small[:, 2 * P + 24:2 * P + 25]
        half_neg = small[:, 2 * P + 25:2 * P + 29]
        pad_row = small[:, 2 * P + 32:2 * P + 32 + ROW]
        ident_b, causal_b, before_b, ones_b = (bits[:, i * P:(i + 1) * P] for i in range(4))
        wqk_s = ab("wqk_s", [P, NCH, 2 * C])
        wv_hi = ab("wv_hi", [P, 2, NCH, C], f32r)
        wv_lo = ab("wv_lo", [P, 2, NCH, C], f32r)
        wq_s = ab("wq_s", [P, NCH, C])
        wk_s = ab("wk_s", [P, NCH, C])
        wo_s = ab("wo_s", [P, NCH, C])
        bo_s = ab("bo_s", [P, C])
        rt_s = ab("rt_s", [P, NCH, E])
        kvb = ab("kvb", [P, NCH, P])
        gnw = ab("gnw", [P, NCH])
        gnb = ab("gnb", [P, NCH])

        x_t = [ab(f"x_t{i}", [P, C]) for i in range(4)]
        c_t = [ab(f"c_t{i}", [P, C]) for i in range(4)]
        xcT = ab("xcT", [P, 2, NCH, T])
        xc_hi = ab("xc_hi", [P, 2, NCH, T], f32r)
        xc_lo = ab("xc_lo", [P, 2, NCH, T], f32r)
        qT_f = [ab(f"qT_f{i}", [P, NCH, T]) for i in range(2)]
        qk_s = [ab(f"qk_s{i}", [P, 2, 2, NCH, T], f32r) for i in range(2)]
        v_ret = [ab(f"v_ret{i}", [P, NH, P]) for i in range(2)]
        v_att = [ab(f"v_att{i}", [P, NH, VP, HD], bf16) for i in range(4)]
        v_rest = ab("v_rest", [P, NH, HD])
        kx_s = [ab(f"kx_s{i}", [P, 2, NCH, T], f32r) for i in range(4)]
        k_mask = [ab(f"k_mask{i}", [P, 2, NH, T], f32r) for i in range(2)]
        wv_raw = v_ret[0][:, 0:2 * NCH * C // P, :].rearrange("p (a k j) t -> p a k (j t)", a=2, k=NCH)
        ret_p = [ab(f"ret_p{i}", [P, QH, T]) for i in range(2)]
        att_p = [ab(f"att_p{i}", [P, QH, T]) for i in range(2)]
        kvb_raw = att_p[0][:, 0:NCH, :]
        bits_f = att_p[1][:, :, :].rearrange("p a t -> p (a t)")
        att_hi = [ab(f"att_hi{i}", [P, QH, T], f16) for i in range(2)]
        att_lo = [ab(f"att_lo{i}", [P, QH, T], f16) for i in range(2)]
        y_raw = ab("y_raw", [P, NCH, T])
        yT = ab("yT", [P, NCH, T])
        gst = ab("gst", [P, 6])
        gmv = ab("gmv", [P, 2])
        gsum = ab("gsum", [P, 2])
        gtot = ab("gtot", [P, 2])
        gsq = ab("gsq", [P, 1])
        gmsq = ab("gmsq", [P, 1])
        gshift = ab("gshift", [P, NCH])
        gvar = ab("gvar", [P, 1])
        grstd = ab("grstd", [P, 1])
        gmul = ab("gmul", [P, NCH])
        gadd = ab("gadd", [P, NCH])
        x1_pre = x2_pre = ab("ln_input", [P, C])
        l1st = ab("l1st", [P, 6])
        l1mv = ab("l1mv", [P, 2])
        l1var = ab("l1var", [P, 1])
        l1rstd = ab("l1rstd", [P, 1])
        x1 = ab("x1", [P, C])
        x1_bo = [ab(f"x1_bo{i}", [P, C]) for i in range(4)]
        x1T = ab("x1T", [P, NCH, T])
        qx_s = ab("qx_s", [P, 2, NCH, T], f32r)
        row_max = [ab(f"row_max{i}", [P, NH]) for i in range(2)]
        neg_max = [ab(f"neg_max{i}", [P, NH]) for i in range(2)]
        den = [ab(f"den{i}", [P, NH]) for i in range(2)]
        rden = ab("rden", [P, NH])
        att_sum = ab("att_sum", [P, HPC, HD])
        att_n = ab("att_n", [P, NH, HD])
        attT = ab("attT", [P, NCH, T])
        l2st = ab("l2st", [P, 6])
        l2mv = ab("l2mv", [P, 2])
        l2var = ab("l2var", [P, 1])
        l2rstd = ab("l2rstd", [P, 1])
        x2T = ab("x2T", [P, NCH, T])
        lg = ab("lg", [P, E])
        top = ab("top", [P, 8])
        top_i = ab("top_i", [P, 8], u32)
        top_f = ab("top_f", [P, 2])
        hot = ab("hot", [P, 2, E])
        hot_b = ab("hot_b", [P, E], bf16)
        gap = ab("gap", [P, 1])
        gap_e = ab("gap_e", [P, 1])
        gap_s = ab("gap_s", [P, 1])
        place = ab("place", [P, E])
        place2 = ab("place2", [P, 2, E])
        pos_f = ab("pos_f", [P, 2])
        tok = ab("tok", [P, 1])

        attention.close()

        w_hi0, w_lo0 = (m[:, :, :, :].rearrange("p a h t -> p (a h t)") for m in q_mask)
        w_hi = [w_hi0, sb("w_hi1", [P, WROW], f32r)]
        w_lo = [w_lo0, sb("w_lo1", [P, WROW], f32r)]

        rows = sb("rows", [P, HALVES, ROW])
        meta_next = sb("meta_next", [P, HALVES, 2])
        meta = sb("meta", [P, HALVES, 2])
        meta_i = sb("meta_i", [P, HALVES], u32)
        h_f = [sb(f"h_f{i}", [P, SLOT]) for i in range(2)]
        h_hi = [sb(f"h_hi{i}", [P, SLOT], f32r) for i in range(4)]
        h_lo = [sb(f"h_lo{i}", [P, SLOT], f32r) for i in range(4)]
        xs_hi = sb("xs_hi", [P, NCH, SLOT], f32r)
        xs_lo = sb("xs_lo", [P, NCH, SLOT], f32r)
        y_b = sb("y_b", [P, HALVES, C])
        y_w = sb("y_w", [P, HALVES, C])

        NLAST = N_TOK // (4 * P)
        last_in = [sb(f"last_in{i}", [P, 4, C]) for i in range(NLAST)]
        last_out = [sb(f"last_out{i}", [P, 4, C]) for i in range(NLAST)]
        last_nm = sb("last_nm", [P, NLAST, 4])
        last_rs = sb("last_rs", [P, NLAST, 4])
        last_st = sb("last_st", [P, NLAST, 4, 6])
        last_mv = sb("last_mv", [P, NLAST, 4, 2])
        last_ve = sb("last_ve", [P, NLAST, 4])

        bank = [ctx.enter_context(nc.psum_tensor(f"bank{i}", [P, 512], f32)) for i in range(8)]
        ps_ret, ps_att, ps_attT, ps_y, ps_o, ps_prep, bank_g, bank_f = bank
        ps_g, ps_f = bank_g[:, 0:C], bank_f[:, 0:C]
        ps_h = bank[0:4]
        ps_out = bank[4:6]
        ps_xs = bank[6]

        names = """consts_first consts consts_expert kvb_scaled zeroed cleared masks_cleared
            wv_high wv_split prep_T prep_T_out xc_high xc_low prep_qk qk_hi q_copied qk_out prep_v v_hi v_left v_mid v_out prep_kx kx_hi kx_out
            ret_scores ret_decayed ret_done y_out
            gn_chain gn_mean gn_sums gn_moments gn_coef_chain gn_coef gn_applied y_back
            ln1_chain ln1_var ln1_rstd x1_done x1_bo_done x1_T x1_T_out qx qx_hi qx_out
            att_scores att_max nm_chain att_exp att_turned att_hi_out att_turned_out att_done
            att_summed att_norm att_back att_back_out att_proj
            ln2_chain ln2_var ln2_rstd x2_done x2_again x2_T x2_T_out logits
            top_chain gap_done gap_exp picked ranked placed share_chain shared
            tab_chain counts_ready tab_ready raw_split raw_hi w_ready chain_first
            rows_turned rows_in xs_chain xs_ready fc_done h_done h_chain h_split
            y_done y_chain y_biased y_weighted meta_ready last_chain last_var last_rstd_raw last_rstd last_act last_dve out_stored
            passed""".split()
        s = {k: sem(k) for k in names}
        s_load = [sem(f"loaded{i}") for i in range(4)]
        s_qmask = [sem(f"q_masked{i}") for i in range(2)]
        s_kmask = [sem(f"k_masked{i}") for i in range(2)]
        s_sent = [sem(f"sent{i}") for i in range(2)]
        s_total = [sem(f"total_stored{i}") for i in range(2)]
        s_pad = sem("pad_filled")
        s_wraw = sem("weights_loaded")
        s_rows = sem("rows_loaded")
        s_added = sem("rows_added")
        s_last = [sem(f"last_loaded{b}") for b in range(NLAST)]

        CONSTS_FIRST, CONSTS, CONSTS_EXPERT = 5, 9, 2
        EVER = 1
        GN, GN_COEF, LN1, LN2, TOP, SHARE = 3, 6, 3, 3, 9, 3

        def steps(eng, step):
            for k in range(LEAD):
                step(0, k)
            with eng.Fori(LEAD // ROUND, B // ROUND) as loop:
                for k in range(ROUND):
                    step(loop, k)
            for k in range(B, B + DRAIN):
                step(0, k)

        def experts(eng, body):
            with eng.Fori(0, E // 2 - 1) as pair:
                for k in range(2):
                    body(2 * pair + k, k, True, True)
            body(E - 2, 0, True, False)
            body(E - 1, 1, False, False)

        def quad(loop, k, q, lag):
            return At(loop, k + (q - lag) // NQ), (q - lag) % NQ

        def score_bank(c, q):
            spare = c.fixed and 4 * c.n + q >= 4 * B + 1 - SCORES
            return ps_ret if spare and (4 * c.n + q) % 2 == 0 else ps_att, spare

        def first(c, k):
            return c.fixed and c.n < k

        def diagonal(flat):
            wide = flat[:, 0:HPC * P]
            step = P + HD
            head = wide[:, 0:HD]
            return bass.AP(head.tensor, head.offset, [list(head.ap[0]), [step, HPC], [1, HD]])

        def half_of(c):
            return 2 * c.g + c.r // 2

        def apart(eng):
            eng.sem_inc(s["passed"], 1)

        def pad_rows(eng, some):
            eng.wait_ge(s["counts_ready"], 1)
            for e in some:
                cnt = eng.value_load(tab_i[0:1, 2, e:e + 1], min_val=0, max_val=N_TOK)
                eng.dma_start(sent[e, ds(cnt, SLOT), :].rearrange("(h p) c -> p h c", p=P),
                              pad_row.unsqueeze(1).to_broadcast([P, HALVES, ROW])).then_inc(s_pad, 16)

        block = ctx.enter_context(nc.Block())

        @block.sync
        def _(sp):
            def load(c):
                if not first(c, 4):
                    sp.wait_ge(s["ln1_chain"], LN1 * (c.n - 4) + 1)
                    apart(sp)
                    sp.wait_ge(s["prep_T"], c.n - 3)
                    apart(sp)
                sp.dma_start(x_t[c.r][:, :], x[ds(c.n, 1), :, :].rearrange("b t c -> (b t) c"))\
                    .then_inc(s_load[c.r], 16)
                sp.dma_start(c_t[c.r][:, :], ctx_in[ds(c.n, 1), :, :].rearrange("b t c -> (b t) c"))\
                    .then_inc(s_load[c.r], 16)

            def store_total(c):
                sp.wait_ge(s["x2_done"], c.n + 1)
                apart(sp)
                sp.dma_start(total[ds(c.n * T, T), :], x2_row[c.r % 2][0][:, 0:C])\
                    .then_inc(s_total[c.r % 2], 16)

            def spread(dst, src, done, waits):
                for sem_, v in waits:
                    sp.wait_ge(sem_, v)
                    apart(sp)
                heads_ = dst[:, :, :, :].bitcast(f32).rearrange("p a (k j) t -> p (a k) j t", j=HPC)
                flat = src.bitcast(f32).rearrange("p a k t -> p (a k) t")
                for j in range(HPC):
                    rows16 = slice(j * HD, (j + 1) * HD)
                    sp.dma_start(heads_[rows16, :, j, :], flat[rows16]).then_inc(done, 16)

            def spread_q(c):
                waits = [(s["qk_out"], c.n + 1)]
                if not first(c, 2):
                    waits.append((s["ret_scores"], 4 * (c.n - 1)))
                spread(q_mask[c.r % 2], qk_s[c.r % 2][:, 0], s_qmask[c.r % 2], waits)

            def spread_k(c):
                waits = [(s["kx_out"], c.n + 1)]
                if not first(c, 2):
                    waits.append((s["att_scores"], 4 * (c.n - 1)))
                spread(k_mask[c.r % 2], kx_s[c.r][:, :, :, :], s_kmask[c.r % 2], waits)

            load(At(0, 0))
            for dst, src in ((small[:, :], small_c),
                             (wqk_s[:, :, :], w_qkv[:, 0:2 * C].rearrange("(k p) n -> p k n", p=P)),
                             (wv_raw[:, 0], w_qkv[:, 2 * C:3 * C].rearrange("(k p) n -> p k n", p=P)),
                             (wk_s[:, :, :], wk_t.rearrange("(k p) n -> p k n", p=P)),
                             (wv_raw[:, 1], wv_t.rearrange("(k p) n -> p k n", p=P))):
                sp.dma_start(dst, src).then_inc(s["consts_first"], 16)
            load(At(0, 1))
            for dst, src in ((decay[:, :, :], decay_c), (kvb_raw, kv_blocks.rearrange("k p n -> p k n")),
                             (bits_f, bits_c), (gnw[:, :], gn_scale), (gnb[:, :], gn_shift),
                             (wq_s[:, :, :], wq_t.rearrange("(k p) n -> p k n", p=P)),
                             (wo_s[:, :, :], wo_t.rearrange("(k p) n -> p k n", p=P)),
                             (bo_s[:, :], bo.partition_broadcast(P)),
                             (rt_s[:, :, :], router_t.rearrange("(k p) n -> p k n", p=P))):
                sp.dma_start(dst, src).then_inc(s["consts"], 16)

            def load_weights(e):
                sp.dma_start(w_raw[:, 0:NCH * H].rearrange("p (k n) -> p k n", k=NCH),
                             w_fc[ds(e, 1), :, :].rearrange("e (k p) n -> p (e k) n", p=P))\
                    .then_inc(s_wraw, 16)
                sp.dma_start(w_raw[:, NCH * H:WROW].rearrange("p (k n) -> p k n", k=HC),
                             w_proj[ds(e, 1), :, :].rearrange("e (k p) n -> p (e k) n", p=P))\
                    .then_inc(s_wraw, 16)

            sp.wait_ge(s["cleared"], 1)
            spread_q(At(0, 0))
            load(At(0, 2))

            def step(loop, k):
                c = At(loop, k - 1)
                if c.exists():
                    spread_k(c)
                c = At(loop, k + 1)
                if c.exists():
                    spread_q(c)
                c = At(loop, k - 4)
                if c.exists():
                    store_total(c)
                c = At(loop, k + 3)
                if c.exists():
                    load(c)

            for k in range(LEAD):
                if k < 3:
                    sp.wait_ge(s["masks_cleared"], k + 1)
                if k == LEAD - 1:
                    sp.dma_start(bfc_s[:, :, :], b_fc).then_inc(s["consts_expert"], 16)
                    sp.dma_start(bproj_s[:, :, :].rearrange("p e c -> p (e c)"),
                                 b_proj.rearrange("e c -> (e c)").partition_broadcast(P))\
                        .then_inc(s["consts_expert"], 16)
                    load_weights(0)
                step(0, k)
            with sp.Fori(LEAD // ROUND, B // ROUND - 1) as loop:
                for k in range(ROUND):
                    step(loop, k)
            for k in range(B - ROUND, B + DRAIN):
                if k == SPLIT + HC // NQ:
                    sp.wait_ge(s["raw_split"], 1)
                    load_weights(1)
                step(0, k)

            pad_rows(sp, range(0, E // 2))
            sp.wait_ge(s_pad, 16 * E)
            for par in range(2):
                sp.wait_ge(s_sent[par], 16 * B)
            sp.wait_ge(s["tab_ready"], 1)

            def expert(e, par, has_next, has_after):
                n_slots = sp.value_load(tab_i[0:1, 0, ds(e, 1)], min_val=1, max_val=N_TOK // SLOT)
                before = sp.value_load(tab_i[0:1, 1, ds(e, 1)], min_val=0, max_val=(2 * N_TOK) // SLOT + E)
                with sp.Fori(0, n_slots) as j:
                    sp.wait_ge(s["rows_turned"], before + j + EVER)
                    sp.wait_ge(s["meta_ready"], before + j + EVER)
                    apart(sp)
                    sp.dma_start(rows[:, :, :],
                                 sent[ds(e, 1), ds(j * SLOT, SLOT), :].rearrange("e (h p) c -> p (e h) c", p=P))\
                        .then_inc(s_rows, 16)
                if has_after:
                    sp.wait_ge(s["raw_split"], e + 2)
                    apart(sp)
                    load_weights(e + 2)

            experts(sp, expert)
            n_all = sp.value_load(tab_i[0:1, 3, 0:1], min_val=E, max_val=(2 * N_TOK) // SLOT + E)
            sp.wait_ge(s["rows_turned"], n_all + EVER)
            sp.wait_ge(s["meta_ready"], n_all + EVER)
            sp.dma_start(rows[:, :, :], sent[0, 0:SLOT, :].rearrange("(h p) c -> p h c", p=P)).then_inc(s_rows, 16)

            total_v = total[0:N_TOK, :].rearrange("(b p j) c -> b p j c", p=P, j=4)
            out_v = out.rearrange("b t c -> (b t) c").rearrange("(b p j) c -> b p j c", p=P, j=4)
            n_add = sp.value_load(tab_i[0:1, 3, 1:2], min_val=E, max_val=32 * ((2 * N_TOK) // SLOT + E))
            sp.wait_ge(s_added, n_add + 16 * EVER)
            for b in range(NLAST):
                sp.dma_start(last_in[b][:, :, :], total_v[b]).then_inc(s_last[b], 16)
            for b in range(NLAST):
                sp.wait_ge(s["last_act"], 3 * (b + 1))
                sp.wait_ge(s["last_dve"], b + 1)
                sp.dma_start(out_v[b], last_out[b][:, :, :]).then_inc(s["out_stored"], 16)
            sp.wait_ge(s["out_stored"], 16 * NLAST)

        @block.tensor
        def _(pe):
            mm, tr = nc.tensor.matmul, nc.tensor.transpose

            def prep_turn(c):
                pe.wait_ge(s_load[c.r], 32 * (c.g + 1))
                if not first(c, 1):
                    pe.wait_ge(s["v_left"], c.n)
                for i, src in enumerate((x_t[c.r], c_t[c.r])):
                    for k in range(NCH):
                        at = (i * NCH + k) * P
                        last = tr(ps_prep[:, at:at + P], src[:, k * P:(k + 1) * P], ident)
                last.then_inc(s["prep_T"], 1)

            def prep_qk(c):
                pe.wait_ge(s["prep_T_out"], c.n + 1)
                for m in range(2 * NCH):
                    for k in range(NCH):
                        last = mm(ps_prep[:, m * P:(m + 1) * P], wqk_s[:, k, m * P:(m + 1) * P],
                                  xcT[:, 0, k, :], start=(k == 0), stop=(k == NCH - 1))
                last.then_inc(s["prep_qk"], 1)

            def prep_kx(c):
                pe.wait_ge(s["qk_out"], c.n + 1)
                for m in range(NCH):
                    for k in range(NCH):
                        last = mm(ps_prep[:, m * P:(m + 1) * P], wk_s[:, k, m * P:(m + 1) * P],
                                  xcT[:, 1, k, :], start=(k == 0), stop=(k == NCH - 1))
                last.then_inc(s["prep_kx"], 1)

            def prep_v(c):
                pe.wait_ge(s["kx_out"], c.n + 1)
                pe.wait_ge(s["xc_low"], c.n + 1)
                if first(c, 1):
                    pe.wait_ge(s["wv_split"], 1)
                for i in range(2):
                    o = ps_prep[:, i * C:(i + 1) * C]
                    for k in range(NCH):
                        for n, (v, w) in enumerate(((xc_hi, wv_hi), (xc_hi, wv_lo), (xc_lo, wv_hi))):
                            last = mm(o, v[:, i, k, :], w[:, i, k, :], start=(k == 0 and n == 0),
                                      stop=(k == NCH - 1 and n == 2))
                last.then_inc(s["prep_v"], 1)

            def three(o, hi, lo, m_hi, m_lo, stop):
                mm(o, hi, m_hi, start=True, stop=False)
                mm(o, hi, m_lo, start=False, stop=False)
                return mm(o, lo, m_hi, start=False, stop=stop)

            def heads(mask, part, q):
                return mask[:, part, QH * q:QH * (q + 1), :].rearrange("p h t -> p (h t)")

            def ret_scores(c, q):
                if q == 0:
                    pe.wait_ge(s_qmask[c.r % 2], SPREAD * (half_of(c) + 1))
                if not (c.fixed and 4 * c.n + q < 1):
                    pe.wait_ge(s["ret_decayed"], 4 * c.n + q)
                k, m = qk_s[c.r % 2], q_mask[c.r % 2]
                three(ps_ret[:, :], k[:, 1, 0, q // 2, :], k[:, 1, 1, q // 2, :], heads(m, 0, q), heads(m, 1, q),
                      True).then_inc(s["ret_scores"], 1)

            def ret_values(c, q):
                pe.wait_ge(s["ret_decayed"], 4 * c.n + q + 1)
                k = q // 2
                o = ps_y[:, k * P:(k + 1) * P]
                if q == 0 and not first(c, 1):
                    pe.wait_ge(s["y_out"], c.n)
                if q % 2 == 0:
                    mm(o, kvb[:, k, :], qT_f[c.r % 2][:, k, :], start=True, stop=False)
                for i in range(QH):
                    last = mm(o, v_ret[c.r % 2][:, QH * q + i, :], ret_p[q % 2][:, i, :],
                              start=False, stop=(q % 2 == 1 and i == QH - 1))
                last.then_inc(s["ret_done"], 1)

            def att_scores(c, q):
                if q == 0:
                    pe.wait_ge(s["qx_out"], c.n + 1)
                    pe.wait_ge(s_kmask[c.r % 2], SPREAD * (half_of(c) + 1))
                o, spare = score_bank(c, q)
                if spare:
                    pe.wait_ge(s["ret_decayed"], 4 * B)
                if not (c.fixed and c.n == 0 and q == 0):
                    pe.wait_ge(s["att_exp"], 4 * c.n + q - spare)
                m = k_mask[c.r % 2]
                three(o[:, :], qx_s[:, 0, q // 2, :], qx_s[:, 1, q // 2, :], heads(m, 0, q), heads(m, 1, q),
                      False)
                mm(o[:, :], ident_b, causal_b.unsqueeze(1).to_broadcast([P, QH, T]),
                   start=False, stop=True).then_inc(s["att_scores"], 1)

            def att_turn(c, q):
                pe.wait_ge(s["att_exp"], 4 * c.n + q + 1)
                if not (c.fixed and c.n == 0 and q == 0):
                    pe.wait_ge(s["att_turned_out"], 4 * c.n + q)
                for i in range(QH):
                    last = tr(ps_attT[:, i * P:(i + 1) * P], att_p[q % 2][:, i, :], ident)
                last.then_inc(s["att_turned"], 1)

            def att_values(c, q):
                pe.wait_ge(s["att_turned_out"], 4 * c.n + q + 1)
                if q == 0:
                    pe.wait_ge(s["v_out"], c.n + 1)
                if q % 2 == 0 and not (c.fixed and c.n == 0 and q == 0):
                    pe.wait_ge(s["att_summed"], 2 * c.n + q // 2)
                for i in range(QH):
                    h = QH * q + i
                    o = ps_o[:, (h % HPC) * VW:(h % HPC + 1) * VW]
                    v = v_att[c.r][:, h, :, :].rearrange("p a d -> p (a d)")
                    mm(o, att_hi[q % 2][:, i, :], v, start=True, stop=False)
                    last = mm(o, att_lo[q % 2][:, i, :], v, start=False, stop=True)
                last.then_inc(s["att_done"], 1)

            def gn_mean(c):
                pe.wait_ge(s["gn_sums"], c.n + 1)
                if not first(c, 1):
                    pe.wait_ge(s["qx_out"], c.n)
                mm(ps_g[:, 0:2], mean_w, gsum[:, :], start=True, stop=True).then_inc(s["gn_mean"], 1)

            def y_back(c):
                pe.wait_ge(s["gn_applied"], c.n + 1)
                for k in range(NCH):
                    last = tr(ps_g[:, k * P:(k + 1) * P], yT[:, k, :], ident)
                last.then_inc(s["y_back"], 1)

            def x1_turn(c):
                pe.wait_ge(s["x1_done"], c.n + 1)
                for k in range(NCH):
                    last = tr(ps_g[:, k * P:(k + 1) * P], x1[:, k * P:(k + 1) * P], ident)
                last.then_inc(s["x1_T"], 1)

            def qx(c):
                pe.wait_ge(s["x1_T_out"], c.n + 1)
                for m in range(NCH):
                    for k in range(NCH):
                        last = mm(ps_g[:, m * P:(m + 1) * P], wq_s[:, k, m * P:(m + 1) * P], x1T[:, k, :],
                                  start=(k == 0), stop=(k == NCH - 1))
                last.then_inc(s["qx"], 1)

            def att_back(c):
                pe.wait_ge(s["att_norm"], 2 * (c.n + 1))
                for k in range(NCH):
                    last = tr(bank_g[:, C + k * P:C + (k + 1) * P],
                              att_n[:, k * HPC:(k + 1) * HPC, :].rearrange("p h d -> p (h d)"), ident)
                last.then_inc(s["att_back"], 1)

            def att_proj(c):
                pe.wait_ge(s["att_back_out"], c.n + 1)
                if not first(c, 1):
                    pe.wait_ge(s["placed"], c.n)
                for k in range(NCH):
                    last = mm(ps_f, attT[:, k, :], wo_s[:, k, :], start=(k == 0), stop=(k == NCH - 1))
                last.then_inc(s["att_proj"], 1)

            def x2_turn(c):
                pe.wait_ge(s["x2_done"], c.n + 1)
                for k in range(NCH):
                    last = tr(ps_f[:, k * P:(k + 1) * P], x2_row[c.r % 2][0][:, k * P:(k + 1) * P], ident)
                last.then_inc(s["x2_T"], 1)

            def logits(c):
                pe.wait_ge(s["x2_T_out"], c.n + 1)
                for k in range(NCH):
                    last = mm(ps_f[:, 0:E], x2T[:, k, :], rt_s[:, k, :], start=(k == 0), stop=(k == NCH - 1))
                last.then_inc(s["logits"], 1)

            def rank(c):
                pe.wait_ge(s["picked"], c.n + 1)
                mm(ps_f[:, 0:E], before_b, hot_b[:, :], start=True, stop=True)
                mm(ps_f[:, E:2 * E], ones_b, hot_b[:, :], start=True, stop=True).then_inc(s["ranked"], 1)

            def run(stage, c, *more):
                if c.exists():
                    stage(c, *more)

            prep = [prep_turn, prep_qk, prep_kx, prep_v]

            def step(loop, k):
                for q in range(NQ):
                    run(ret_scores, At(loop, k), q)
                    run(prep[q], At(loop, k + 1))
                    run(att_scores, *quad(loop, k, q, SCORES))
                    run(ret_values, *quad(loop, k, q, 1))
                    run(att_values, *quad(loop, k, q, VALUES))
                    if q == 3:
                        run(rank, At(loop, k - 4))
                    run(att_turn, *quad(loop, k, q, TURN))
                    if q == 0:
                        run(att_proj, At(loop, k - 4))
                        run(qx, At(loop, k - 2))
                    if q == 1:
                        run(gn_mean, At(loop, k - 1))
                        run(x2_turn, At(loop, k - 4))
                    if q == 2:
                        run(y_back, At(loop, k - 1))
                        run(logits, At(loop, k - 4))
                    if q == 3:
                        run(x1_turn, At(loop, k - 1))
                        run(att_back, At(loop, k - 3))

            pe.wait_ge(s["consts_first"], 16 * CONSTS_FIRST)
            for stage in prep:
                stage(At(0, 0))
            pe.wait_ge(s["consts"], 16 * CONSTS)
            pe.wait_ge(s["kvb_scaled"], 1)
            pe.wait_ge(s["zeroed"], 1)
            for k in range(LEAD):
                step(0, k)
            with pe.Fori(LEAD // ROUND, B // ROUND - 1) as loop:
                for k in range(ROUND):
                    step(loop, k)
            for k in range(B - ROUND, B + DRAIN):
                step(0, k)

            def turn_rows(g):
                pe.wait_ge(s_rows, 16 * (g + 1))
                for k in range(NCH):
                    for half in range(HALVES):
                        last = tr(ps_xs[:, k * SLOT + half * P:k * SLOT + (half + 1) * P],
                                  rows[:, half, k * P:(k + 1) * P], ident)
                last.then_inc(s["rows_turned"], 1)

            pe.wait_ge(s["chain_first"], 1)
            pe.sem_inc(s["rows_turned"], EVER)
            turn_rows(0)

            def expert(e, par, has_next, has_after):
                n_slots = pe.value_load(tab_i[0:1, 0, ds(e, 1)], min_val=1, max_val=N_TOK // SLOT)
                before = pe.value_load(tab_i[0:1, 1, ds(e, 1)], min_val=0, max_val=(2 * N_TOK) // SLOT + E)
                pe.wait_ge(s["w_ready"], HC * (e + 1))
                apart(pe)
                whi, wlo = w_hi[par], w_lo[par]

                def fc(g, j):
                    if j >= 4:
                        pe.wait_ge(s["h_done"], HC * g + j - 3 + EVER)
                    else:
                        pe.wait_ge(s["h_done"], HC * g + EVER)
                    n = 0
                    for k in range(NCH):
                        at = k * H + j * P
                        for w, v in ((whi, xs_hi), (whi, xs_lo), (wlo, xs_hi)):
                            last = mm(ps_h[j % 4][:, 0:SLOT], w[:, at:at + P], v[:, k, :],
                                      start=(n == 0), stop=(n == 3 * NCH - 1))
                            n += 1
                    last.then_inc(s["fc_done"], 1)

                def proj(g, j):
                    pe.wait_ge(s["h_split"], HC * g + j + 1 + EVER)
                    at = NCH * H + j * C
                    for half in range(HALVES):
                        cols = slice(half * P, (half + 1) * P)
                        for n, (v, w) in enumerate(((h_hi, whi), (h_lo, whi), (h_hi, wlo))):
                            last = mm(ps_out[half][:, 0:C], v[j % 4][:, cols], w[:, at:at + C],
                                      start=(j == 0 and n == 0), stop=(j == HC - 1 and n == 2))
                    last.then_inc(s["y_done"], 1)

                with pe.Fori(0, n_slots) as i:
                    g = before + i
                    pe.wait_ge(s["xs_ready"], g + 1)
                    for j in range(HC + 3):
                        if j < HC:
                            fc(g, j)
                        if j >= 3:
                            if j == 3:
                                pe.wait_ge(s["y_biased"], HALVES * g + EVER)
                            proj(g, j - 3)
                        if j == 5:
                            turn_rows(g + 1)

            experts(pe, expert)

        @block.scalar
        def _(act):
            A = nc.scalar.activation

            def prep_T_out(c):
                act.wait_ge(s["prep_T"], c.n + 1)
                A(xcT[:, :, :, :].rearrange("p a k t -> p (a k t)"), ps_prep[:, :], ACT.Copy)\
                    .then_inc(s["prep_T_out"], 1)

            def xc_high(c):
                act.wait_ge(s["prep_T_out"], c.n + 1)
                A(xc_hi[:, :, :, :].rearrange("p a k t -> p (a k t)"),
                  xcT[:, :, :, :].rearrange("p a k t -> p (a k t)"), ACT.Copy).then_inc(s["xc_high"], 1)

            def qk_hi(c):
                act.wait_ge(s["prep_qk"], c.n + 1)
                if not first(c, 2):
                    act.wait_ge(s_qmask[c.r % 2], SPREAD * half_of(c))
                A(qk_s[c.r % 2][:, :, 0].rearrange("p a k t -> p a (k t)"),
                  ps_prep[:, :].rearrange("p (a n) -> p a n", a=2), ACT.Copy)\
                    .then_inc(s["qk_hi"], 1)
                A(qT_f[c.r % 2][:, :, :].rearrange("p k t -> p (k t)"), ps_prep[:, 0:C], ACT.Copy)\
                    .then_inc(s["q_copied"], 1)

            def v_hi(c):
                act.wait_ge(s["prep_v"], c.n + 1)
                for k in range(NCH):
                    flat = v_ret[c.r % 2][:, k * HPC:(k + 1) * HPC, :].rearrange("p h c -> p (h c)")
                    A(diagonal(flat), ps_prep[:, k * P:(k + 1) * P].rearrange("p (h d) -> p h d", d=HD), ACT.Copy)
                A(v_att[c.r][:, :, 0, :], ps_prep[:, C:2 * C].rearrange("p (h d) -> p h d", d=HD), ACT.Copy)\
                    .then_inc(s["v_hi"], 1)

            def kx_hi(c):
                act.wait_ge(s["prep_kx"], c.n + 1)
                if not first(c, 4):
                    act.wait_ge(s_kmask[c.r % 2], SPREAD * (half_of(c) - 1))
                A(kx_s[c.r][:, 0].rearrange("p k t -> p (k t)"), ps_prep[:, 0:C], ACT.Copy)\
                    .then_inc(s["kx_hi"], 1)

            def gn_apply(c):
                act.wait_ge(s["gn_coef"], c.n + 1)
                for k in range(NCH):
                    last = A(yT[:, k, :], y_raw[:, k, :], ACT.Identity, bias=gadd[:, k:k + 1],
                             scale=gmul[:, k:k + 1])
                last.then_inc(s["gn_applied"], 1)

            def x1_T_out(c):
                act.wait_ge(s["x1_T"], c.n + 1)
                if not first(c, 2):
                    act.wait_ge(s["att_back"], c.n - 1)
                A(x1T[:, :, :].rearrange("p k t -> p (k t)"), ps_g, ACT.Copy).then_inc(s["x1_T_out"], 1)

            def qx_hi(c):
                act.wait_ge(s["qx"], c.n + 1)
                A(qx_s[:, 0].rearrange("p k t -> p (k t)"), ps_g, ACT.Copy).then_inc(s["qx_hi"], 1)

            def att_exp(c, q):
                act.wait_ge(s["att_max"], 4 * c.n + q + 1)
                if not (c.fixed and 4 * c.n + q < 2):
                    act.wait_ge(s["att_turned"], 4 * c.n + q - 1)
                for i in range(QH):
                    h = QH * q + i
                    last = A(att_p[q % 2][:, i, :], score_bank(c, q)[0][:, i * T:(i + 1) * T], ACT.Exp,
                             bias=neg_max[c.r % 2][:, h:h + 1], scale=SCALE,
                             accum_out=den[c.r % 2][:, h:h + 1])
                last.then_inc(s["att_exp"], 1)

            def att_hi_out(c, q):
                act.wait_ge(s["att_turned"], 4 * c.n + q + 1)
                if not (c.fixed and 4 * c.n + q < 2):
                    act.wait_ge(s["att_done"], 4 * c.n + q - 1)
                A(att_hi[q % 2][:, :, :].rearrange("p h t -> p (h t)"), ps_attT[:, :], ACT.Copy)\
                    .then_inc(s["att_hi_out"], 1)

            def att_back_out(c):
                act.wait_ge(s["att_back"], c.n + 1)
                A(attT[:, :, :].rearrange("p k t -> p (k t)"), bank_g[:, C:2 * C], ACT.Copy)\
                    .then_inc(s["att_back_out"], 1)

            def x2_T_out(c):
                act.wait_ge(s["x2_T"], c.n + 1)
                A(x2T[:, :, :].rearrange("p k t -> p (k t)"), ps_f, ACT.Copy).then_inc(s["x2_T_out"], 1)

            def x2_again(c):
                act.wait_ge(s["x2_done"], c.n + 1)
                A(x2_row[c.r % 2][1][:, 0:C], x2_row[c.r % 2][0][:, 0:C], ACT.Copy).then_inc(s["x2_again"], 1)

            def gap_exp(c):
                act.wait_ge(s["gap_done"], c.n + 1)
                if not first(c, 1):
                    act.wait_ge(s["shared"], c.n)
                A(gap_e[:, :], gap[:, :], ACT.Exp).then_inc(s["gap_exp"], 1)

            def run(stage, c, *more):
                if c.exists():
                    stage(c, *more)

            PIECE = WROW // HC

            def split_hi(e, par, j):
                at = slice(j * PIECE, (j + 1) * PIECE)
                if j == 0:
                    act.wait_ge(s_wraw, 32 * (e + 1))
                    if isinstance(e, int) and e == 0:
                        act.wait_ge(s["ret_scores"], 4 * B)
                A(w_hi[par][:, at], w_raw[:, at], ACT.Copy).then_inc(s["raw_hi"], 1)

            def step(loop, k):
                for q in range(NQ):
                    run(att_hi_out, *quad(loop, k, q, VALUES))
                    if q == 0:
                        run(prep_T_out, At(loop, k + 1))
                        run(xc_high, At(loop, k + 1))
                    if q == 1:
                        run(qk_hi, At(loop, k + 1))
                    if q == 2:
                        run(gn_apply, At(loop, k - 1))
                        run(kx_hi, At(loop, k + 1))
                    if q == 3:
                        run(gap_exp, At(loop, k - 4))
                        run(v_hi, At(loop, k + 1))
                    run(att_exp, *quad(loop, k, q, SCORES))
                    if q == 0:
                        run(qx_hi, At(loop, k - 2))
                    if q == 1:
                        run(x2_T_out, At(loop, k - 4))
                        run(x2_again, At(loop, k - 4))
                    if q == 3:
                        run(att_back_out, At(loop, k - 3))
                        run(x1_T_out, At(loop, k - 1))
                    if SPLIT <= k < SPLIT + HC // NQ:
                        split_hi(0, 0, NQ * (k - SPLIT) + q)

            prep_T_out(At(0, 0))
            xc_high(At(0, 0))
            A(wv_hi[:, :, :, :], wv_raw, ACT.Copy).then_inc(s["wv_high"], 1)
            qk_hi(At(0, 0))
            kx_hi(At(0, 0))
            act.wait_ge(s["cleared"], 1)
            v_hi(At(0, 0))
            act.wait_ge(s["consts"], 16 * CONSTS)
            A(bits[:, :], bits_f, ACT.Copy)
            A(kvb[:, :, :], kvb_raw, ACT.Copy, scale=CROSS).then_inc(s["kvb_scaled"], 1)
            for k in range(LEAD):
                step(0, k)
            with act.Fori(LEAD // ROUND, B // ROUND - 1) as loop:
                for k in range(ROUND):
                    step(loop, k)
            for k in range(B - ROUND, B + DRAIN):
                step(0, k)

            act.wait_ge(s["gap_exp"], B)
            A(gelu_warm[:, :], half_neg[:, 0:1], ACT.Gelu_apprx_tanh)
            pad_rows(act, range(E // 2, E))
            act.wait_ge(s["consts_expert"], 16 * CONSTS_EXPERT)
            act.wait_ge(s["tab_ready"], 1)
            act.sem_inc(s["h_done"], EVER)

            def xs_high(g):
                act.wait_ge(s["rows_turned"], g + 1 + EVER)
                apart(act)
                A(xs_hi[:, :, :].rearrange("p k t -> p (k t)"), ps_xs[:, :], ACT.Copy).then_inc(s["xs_chain"], 1)

            xs_high(0)

            def expert(e, par, has_next, has_after):
                n_slots = act.value_load(tab_i[0:1, 0, ds(e, 1)], min_val=1, max_val=N_TOK // SLOT)
                before = act.value_load(tab_i[0:1, 1, ds(e, 1)], min_val=0, max_val=(2 * N_TOK) // SLOT + E)

                def slot(g, split):
                    for j in range(HC):
                        act.wait_ge(s["fc_done"], HC * g + j + 1)
                        if j >= 2:
                            act.wait_ge(s["h_split"], HC * g + j - 1 + EVER)
                        else:
                            act.wait_ge(s["h_split"], HC * g + EVER)
                        apart(act)
                        A(h_f[j % 2][:, :], ps_h[j % 4][:, 0:SLOT], ACT.Gelu_apprx_tanh,
                          bias=bfc_s[:, ds(e, 1), j:j + 1].rearrange("p e j -> p (e j)")
                          if not isinstance(e, int) else bfc_s[:, e, j:j + 1]).then_inc(s["h_done"], 1)
                        if split:
                            split_hi(e + 1, 1 - par, j)

                    xs_high(g + 1)

                slot(before, has_next)
                with act.If(n_slots > 1):
                    with act.Fori(1, n_slots) as i:
                        slot(before + i, False)

            experts(act, expert)

            for b in range(NLAST):
                act.wait_ge(s["last_rstd"], b + 1)
                for j in range(1, 4):
                    A(last_out[b][:, j, :], last_in[b][:, j, :], ACT.Identity, bias=last_nm[:, b, j:j + 1],
                      scale=last_rs[:, b, j:j + 1]).then_inc(s["last_act"], 1)

        @block.vector
        def _(dve):
            V = nc.vector

            def low(dst, value, hi, wait, done, c, more=()):
                dve.wait_ge(s[wait], c.n + 1)
                for sem_, v in more:
                    dve.wait_ge(sem_, v)
                V.tensor_tensor(dst, value, hi, ALU.subtract).then_inc(s[done], 1)

            def qk_out(c):
                a, flat = qk_s[c.r % 2], "p a k t -> p a (k t)"
                low(a[:, :, 1].rearrange(flat), ps_prep[:, :].rearrange("p (a n) -> p a n", a=2),
                    a[:, :, 0].bitcast(f32).rearrange(flat), "qk_hi", "qk_out", c, [(s["q_copied"], c.n + 1)])

            def v_left(c):
                low(v_rest[:, :, :], ps_prep[:, C:2 * C].rearrange("p (h d) -> p h d", d=HD),
                    v_att[c.r][:, :, 0, :], "v_hi", "v_left", c, [] if first(c, 1) else [(s["v_out"], c.n)])

            def kx_out(c):
                a, flat = kx_s[c.r], "p k t -> p (k t)"
                low(a[:, 1].rearrange(flat), ps_prep[:, 0:C], a[:, 0].bitcast(f32).rearrange(flat), "kx_hi",
                    "kx_out", c)

            def qx_out(c):
                a, flat = qx_s, "p k t -> p (k t)"
                low(a[:, 1].rearrange(flat), ps_g, a[:, 0].bitcast(f32).rearrange(flat), "qx_hi", "qx_out", c)

            def att_turned_out(c, q):
                dve.wait_ge(s["att_hi_out"], 4 * c.n + q + 1)
                V.tensor_tensor(att_lo[q % 2][:, :, :].rearrange("p h t -> p (h t)"), ps_attT[:, :],
                                att_hi[q % 2][:, :, :].rearrange("p h t -> p (h t)"), ALU.subtract)\
                    .then_inc(s["att_turned_out"], 1)

            def ret_decay(c, q):
                dve.wait_ge(s["ret_scores"], 4 * c.n + q + 1)
                if not (c.fixed and 4 * c.n + q < 2):
                    dve.wait_ge(s["ret_done"], 4 * c.n + q - 1)
                V.tensor_tensor(ret_p[q % 2][:, :, :].rearrange("p h t -> p (h t)"), ps_ret[:, :],
                                decay[:, QH * q:QH * (q + 1), :].rearrange("p h t -> p (h t)"),
                                ALU.mult).then_inc(s["ret_decayed"], 1)

            def att_max(c, q):
                dve.wait_ge(s["att_scores"], 4 * c.n + q + 1)
                hs = slice(QH * q, QH * (q + 1))
                V.reduce_max(row_max[c.r % 2][:, hs],
                             score_bank(c, q)[0][:, :].rearrange("p (h s) -> p h s", s=T), AX.X)\
                    .then_inc(s["nm_chain"], 1)
                dve.wait_ge(s["nm_chain"], 4 * c.n + q + 1)
                V.tensor_scalar(neg_max[c.r % 2][:, hs], row_max[c.r % 2][:, hs], -SCALE, LIFT, ALU.mult,
                                ALU.add)\
                    .then_inc(s["att_max"], 1)

            def y_out(c):
                dve.wait_ge(s["ret_done"], 4 * (c.n + 1))
                V.tensor_copy(y_raw[:, :, :].rearrange("p k t -> p (k t)"), ps_y[:, 0:C]).then_inc(s["y_out"], 1)

            def y_stats(c):
                dve.wait_ge(s["y_out"], c.n + 1)
                ch = Chain(dve, s["gn_chain"], GN * c.n)
                ch.link(V.bn_stats(gst[:, :], y_raw[:, :, :].rearrange("p k t -> p (k t)")), apart)
                ch.link(V.bn_aggr(gmv[:, :], gst[:, :]))
                ch.link(V.tensor_tensor(gsq[:, :], gmv[:, 0:1], gmv[:, 0:1], ALU.mult))
                V.tensor_copy(gsum[:, 0:1], gmv[:, 0:1])
                V.tensor_tensor(gsum[:, 1:2], gsq[:, :], gmv[:, 1:2], ALU.add).then_inc(s["gn_sums"], 1)

            def gn_moments(c):
                dve.wait_ge(s["gn_mean"], c.n + 1)
                if not first(c, 1):
                    dve.wait_ge(s["gn_coef"], c.n)
                V.tensor_copy(gtot[:, :], ps_g[:, 0:2]).then_inc(s["gn_moments"], 1)

            def ln1_stats(c):
                dve.wait_ge(s["y_back"], c.n + 1)
                ch = Chain(dve, s["ln1_chain"], LN1 * c.n)
                ch.link(V.tensor_tensor(x1_pre[:, :], ps_g, x_t[c.r][:, :], ALU.add))
                ch.link(V.bn_stats(l1st[:, :], x1_pre[:, :]), apart)
                ch.link(V.bn_aggr(l1mv[:, :], l1st[:, :]))
                V.tensor_scalar(l1var[:, :], l1mv[:, 1:2], EPS, None, ALU.add).then_inc(s["ln1_var"], 1)

            def ln1_norm(c):
                dve.wait_ge(s["ln1_rstd"], c.n + 1)
                if not first(c, 1):
                    dve.wait_ge(s["x1_bo_done"], c.n)
                V.tensor_scalar(x1[:, :], x1_pre[:, :], l1mv[:, 0:1], l1rstd[:, 0:1], ALU.subtract, ALU.mult)\
                    .then_inc(s["x1_done"], 1)

            def att_sums(c, half):
                hs = slice(half * HPC, (half + 1) * HPC)
                dve.wait_ge(s["att_exp"], 4 * c.n + 2 * (half + 1))
                if not (half == 0 and first(c, 1)):
                    dve.wait_ge(s["att_norm"], 2 * c.n + half)
                V.reciprocal(rden[:, hs], den[c.r % 2][:, hs])
                dve.wait_ge(s["att_done"], 4 * c.n + 2 * (half + 1))
                V.reduce_sum(att_sum[:, :, :],
                             ps_o[:, 0:HPC * VW].rearrange("p (h a d) -> p h d a", h=HPC, a=VP), AX.X)\
                    .then_inc(s["att_summed"], 1)

            def ln2_stats(c):
                dve.wait_ge(s["att_proj"], c.n + 1)
                ch = Chain(dve, s["ln2_chain"], LN2 * c.n)
                ch.link(V.tensor_tensor(x2_pre[:, :], ps_f, x1_bo[c.r][:, :], ALU.add))
                ch.link(V.bn_stats(l2st[:, :], x2_pre[:, :]), apart)
                ch.link(V.bn_aggr(l2mv[:, :], l2st[:, :]))
                V.tensor_scalar(l2var[:, :], l2mv[:, 1:2], EPS, None, ALU.add).then_inc(s["ln2_var"], 1)

            def ln2_norm(c):
                dve.wait_ge(s["ln2_rstd"], c.n + 1)
                if not first(c, 2):
                    dve.wait_ge(s_sent[c.r % 2], 32 * half_of(c))
                    dve.wait_ge(s_total[c.r % 2], 16 * half_of(c))
                V.tensor_scalar(x2_row[c.r % 2][0][:, 0:C], x2_pre[:, :], l2mv[:, 0:1], l2rstd[:, 0:1],
                                ALU.subtract, ALU.mult).then_inc(s["x2_done"], 1)

            def pick_top(c):
                dve.wait_ge(s["logits"], c.n + 1)
                ch = Chain(dve, s["top_chain"], TOP * c.n)
                ch.link(V.tensor_copy(lg[:, :], ps_f[:, 0:E]), apart)
                V.max(top[:, :], lg[:, :]).then_inc(s["top_chain"], 1)

            def pick_index(c):
                dve.wait_ge(s["top_chain"], TOP * c.n + 2)
                V.tensor_tensor(gap[:, :], top[:, 1:2], top[:, 0:1], ALU.subtract).then_inc(s["gap_done"], 1)
                V.max_index(top_i[:, :], top[:, :], lg[:, :]).then_inc(s["top_chain"], 1)

            def pick_hot(c):
                ch = Chain(dve, s["top_chain"], TOP * c.n + 3)
                dve.wait_ge(s["top_chain"], TOP * c.n + 3)
                ch.link(V.tensor_copy(top_f[:, :], top_i[:, 0:2]))
                V.tensor_tensor(hot[:, :, :], lanes8.unsqueeze(1).to_broadcast([P, 2, E]),
                                top_f[:, :].unsqueeze(2).to_broadcast([P, 2, E]), ALU.is_equal)\
                    .then_inc(s["top_chain"], 1)

            def picked(c):
                dve.wait_ge(s["top_chain"], TOP * c.n + 5)
                V.tensor_tensor(hot_b[:, :], hot[:, 0, :], hot[:, 1, :], ALU.add).then_inc(s["picked"], 1)

            def put(c):
                ch = Chain(dve, s["top_chain"], TOP * c.n + 5)
                dve.wait_ge(s["ranked"], c.n + 1)
                ch.link(V.tensor_tensor(place[:, :], ps_f[:, 0:E], filled[:, :], ALU.add))
                V.tensor_tensor(filled[:, :], ps_f[:, E:2 * E], filled[:, :], ALU.add)
                ch.link(V.tensor_tensor(place2[:, :, :], hot[:, :, :],
                                        place[:, :].unsqueeze(1).to_broadcast([P, 2, E]), ALU.mult))
                ch.link(V.reduce_sum(pos_f[:, :], place2[:, :, :], AX.X))
                ch.link(V.tensor_copy(pos[c.r % 2][:, :], pos_f[:, :]))
                dve.sem_inc(s["placed"], 1)

            def run(stage, c, *more):
                if c.exists():
                    stage(c, *more)

            PIECE = WROW // HC

            def split_lo(e, par, j):
                at = slice(j * PIECE, (j + 1) * PIECE)
                dve.wait_ge(s["raw_hi"], HC * e + j + 1)
                last = V.tensor_tensor(w_lo[par][:, at], w_raw[:, at], w_hi[par][:, at].bitcast(f32),
                                       ALU.subtract)
                last.then_inc(s["w_ready"], 1)
                if j == HC - 1:
                    dve.wait_ge(s["w_ready"], HC * (e + 1))
                    dve.sem_inc(s["raw_split"], 1)

            def step(loop, k):
                for q in range(NQ):
                    run(ret_decay, At(loop, k), q)
                    if q == 3:
                        run(pick_index, At(loop, k - 4))
                    run(att_turned_out, *quad(loop, k, q, VALUES))
                    if q == 0:
                        run(y_out, At(loop, k - 1))
                    if q == 1:
                        run(ln2_norm, At(loop, k - 4))
                    if q == 3:
                        run(pick_hot, At(loop, k - 4))
                        run(ln1_norm, At(loop, k - 1))
                        run(picked, At(loop, k - 4))
                    run(att_max, *quad(loop, k, q, SCORES))
                    if q == 0:
                        run(y_stats, At(loop, k - 1))
                        run(ln2_stats, At(loop, k - 4))
                        run(qx_out, At(loop, k - 2))
                        run(att_sums, At(loop, k - 3), 0)
                    if q == 1:
                        run(qk_out, At(loop, k + 1))
                        run(gn_moments, At(loop, k - 1))
                    if q == 2:
                        run(kx_out, At(loop, k + 1))
                        run(ln1_stats, At(loop, k - 1))
                        run(att_sums, At(loop, k - 3), 1)
                        run(pick_top, At(loop, k - 4))
                    if q == 3:
                        run(v_left, At(loop, k + 1))
                        run(put, At(loop, k - 4))
                    if SPLIT <= k < SPLIT + HC // NQ:
                        split_lo(0, 0, NQ * (k - SPLIT) + q)

            V.memset(q_mask[0][:, :, :, :].bitcast(f32), 0.0)
            V.memset(v_ret[1][:, :, :], 0.0)
            dve.wait_ge(s["wv_high"], 1)
            V.tensor_tensor(wv_lo[:, :, :, :], wv_raw, wv_hi[:, :, :, :].bitcast(f32), ALU.subtract)\
                .then_inc(s["wv_split"], 1)
            dve.wait_ge(s["wv_split"], 1)
            V.memset(v_ret[0][:, :, :], 0.0).then_inc(s["cleared"], 1)
            qk_out(At(0, 0))
            kx_out(At(0, 0))
            v_left(At(0, 0))
            dve.wait_ge(s["consts"], 16 * CONSTS)
            V.tensor_copy(filled[:, :], region)
            V.tensor_copy(tok[:, :], lane).then_inc(s["zeroed"], 1)
            dve.wait_ge(s["zeroed"], 1)
            for k in range(LEAD):
                step(0, k)
            with dve.Fori(LEAD // ROUND, B // ROUND - 1) as loop:
                for k in range(ROUND):
                    step(loop, k)
            for k in range(B - ROUND, B + DRAIN):
                step(0, k)

            ch = Chain(dve, s["tab_chain"], 0)
            row = tab_f
            V.memset(row[0:1, 3, :], 1.0)
            ch.link(V.tensor_tensor(row[0:1, 2, :], filled[0:1, :], region[0:1, :], ALU.subtract))
            V.tensor_copy(tab_i[0:1, 2, :], row[0:1, 2, :]).then_inc(s["counts_ready"], 1)
            ch.link(V.tensor_scalar(row[0:1, 0, :], row[0:1, 2, :], float(SLOT - 1), None, ALU.add))
            ch.link(V.tensor_copy(tab_i[0:1, 0, :], row[0:1, 0, :]))
            ch.link(V.tensor_scalar(tab_i[0:1, 1, :], tab_i[0:1, 0, :], SLOT.bit_length() - 1, None,
                                    ALU.logical_shift_right))
            ch.link(V.tensor_copy(row[0:1, 0, :], tab_i[0:1, 1, :]))
            ch.link(V.tensor_scalar(row[0:1, 0, :], row[0:1, 0, :], 1.0, None, ALU.max))
            ch.link(V.tensor_tensor_scan(row[0:1, 1, :], row[0:1, 3, :], row[0:1, 0, :], 0.0,
                                         ALU.mult, ALU.add))
            ch.link(V.tensor_copy(row[0:1, 3, 0:1], row[0:1, 1, E - 1:E]))
            ch.link(V.tensor_scalar(row[0:1, 3, 1:2], row[0:1, 1, E - 1:E], float(16 * HALVES), None, ALU.mult))
            ch.link(V.tensor_tensor(row[0:1, 1, :], row[0:1, 1, :], row[0:1, 0, :], ALU.subtract))
            ch.link(V.tensor_copy(tab_i[0:1, 0:2, :], row[0:1, 0:2, :]))
            V.tensor_copy(tab_i[0:1, 3, :], row[0:1, 3, :]).then_inc(s["tab_ready"], 1)
            dve.wait_ge(s["tab_ready"], 1)
            dve.sem_inc(s["chain_first"], 1)

            dve.wait_ge(s["consts_expert"], 16 * CONSTS_EXPERT)

            def take_rows(g):
                dve.wait_ge(s_rows, 16 * (g + 1))
                V.tensor_copy(meta_next[:, :, :], rows[:, :, C:ROW]).then_inc(s["meta_ready"], 1)

            def split_rows(g):
                dve.wait_ge(s["xs_chain"], g + 1)
                V.tensor_tensor(xs_lo[:, :, :].rearrange("p k t -> p (k t)"), ps_xs[:, :],
                                xs_hi[:, :, :].bitcast(f32).rearrange("p k t -> p (k t)"), ALU.subtract)\
                    .then_inc(s["xs_ready"], 1)

            for name in ("meta_ready", "h_split", "y_biased"):
                dve.sem_inc(s[name], EVER)
            take_rows(0)
            split_rows(0)

            def expert(e, par, has_next, has_after):
                n_slots = dve.value_load(tab_i[0:1, 0, ds(e, 1)], min_val=1, max_val=N_TOK // SLOT)
                before = dve.value_load(tab_i[0:1, 1, ds(e, 1)], min_val=0, max_val=(2 * N_TOK) // SLOT + E)

                def slot(g, split):
                    for j in range(HC):
                        dve.wait_ge(s["h_done"], HC * g + j + 1 + EVER)
                        if j >= 4:
                            dve.wait_ge(s["y_done"], HC * g + j - 3)
                        V.tensor_copy(h_hi[j % 4][:, :], h_f[j % 2][:, :]).then_inc(s["h_chain"], 1)
                        dve.wait_ge(s["h_chain"], HC * g + j + 1)
                        V.tensor_tensor(h_lo[j % 4][:, :], h_f[j % 2][:, :], h_hi[j % 4][:, :].bitcast(f32),
                                        ALU.subtract).then_inc(s["h_split"], 1)
                        if split:
                            split_lo(e + 1, 1 - par, j)
                    split_rows(g + 1)
                    dve.wait_ge(s_added, 16 * (HALVES * g + EVER))
                    dve.wait_ge(s["meta_ready"], g + 1 + EVER)
                    V.tensor_copy(meta[:, :, :], meta_next[:, :, :]).then_inc(s["y_chain"], 1)
                    dve.wait_ge(s["y_chain"], g + 1)
                    V.tensor_copy(meta_i[:, :], meta[:, :, 1])
                    take_rows(g + 1)
                    dve.wait_ge(s["y_done"], HC * (g + 1))
                    for half in range(HALVES):
                        bias = bproj_s[:, e, :] if isinstance(e, int) else \
                            bproj_s[:, ds(e, 1), :].rearrange("p e c -> p (e c)")
                        V.tensor_tensor(y_b[:, half, :], ps_out[half][:, 0:C], bias, ALU.add)\
                            .then_inc(s["y_biased"], 1)

                slot(before, has_next)
                with dve.If(n_slots > 1):
                    with dve.Fori(1, n_slots) as i:
                        slot(before + i, False)

            experts(dve, expert)

            def last_stats(b):
                dve.wait_ge(s_last[b], 16)
                ch = Chain(dve, s["last_chain"], 2 * b)
                for j in range(4):
                    last = V.bn_stats(last_st[:, b, j, :], last_in[b][:, j, :])
                ch.link(last)
                for j in range(4):
                    last = V.bn_aggr(last_mv[:, b, j, :], last_st[:, b, j, :])
                ch.link(last)
                V.tensor_scalar(last_ve[:, b, :], last_mv[:, b, :, 1], EPS, None, ALU.add)\
                    .then_inc(s["last_var"], 1)

            def last_norm(b):
                dve.wait_ge(s["last_rstd_raw"], b + 1)
                V.scalar_tensor_tensor(out=last_nm[:, b, :], in0=last_mv[:, b, :, 0], scalar=-1.0,
                                       in1=last_rs[:, b, :], op0=ALU.mult, op1=ALU.mult)\
                    .then_inc(s["last_rstd"], 1)
                V.tensor_scalar(last_out[b][:, 0, :], last_in[b][:, 0, :], last_mv[:, b, 0, 0:1],
                                last_rs[:, b, 0:1], ALU.subtract, ALU.mult).then_inc(s["last_dve"], 1)

            last_stats(0)
            for b in range(NLAST):
                if b + 1 < NLAST:
                    last_stats(b + 1)
                last_norm(b)

        @block.gpsimd
        def _(pool):
            G = nc.gpsimd

            def v_parts(c):
                v = v_att[c.r]
                pool.wait_ge(s["v_left"], c.n + 1)
                apart(pool)
                G.tensor_copy(v[:, :, 1, :], v_rest[:, :, :]).then_inc(s["v_mid"], 1)
                pool.wait_ge(s["v_mid"], c.n + 1)
                G.tensor_tensor(v[:, :, 2, :], v_rest[:, :, :], v[:, :, 1, :], ALU.subtract)\
                    .then_inc(s["v_out"], 1)

            def gn_coef(c):
                pool.wait_ge(s["gn_moments"], c.n + 1)
                if not first(c, 1):
                    pool.wait_ge(s["gn_applied"], c.n)
                ch = Chain(pool, s["gn_coef_chain"], GN_COEF * c.n)
                mean, square = gtot[:, 0:1], gtot[:, 1:2]
                both = [P, NCH]
                ch.link(G.tensor_tensor(gmsq[:, :], mean, mean, ALU.mult))
                ch.link(G.tensor_tensor(gvar[:, :], square, gmsq[:, :], ALU.subtract))
                ch.link(G.tensor_tensor(gvar[:, :], gvar[:, :], eps_c, ALU.add))
                ch.link(G.tensor_tensor(grstd[:, :], gvar[:, :], half_neg[:, 0:1], ALU.pow))
                ch.link(G.tensor_tensor(gmul[:, :], gnw[:, :], grstd[:, :].to_broadcast(both), ALU.mult))
                ch.link(G.tensor_tensor(gshift[:, :], gmul[:, :], mean.to_broadcast(both), ALU.mult))
                G.tensor_tensor(gadd[:, :], gnb[:, :], gshift[:, :], ALU.subtract).then_inc(s["gn_coef"], 1)

            def att_norm(c, half):
                pool.wait_ge(s["att_summed"], 2 * c.n + half + 1)
                if half == 0 and not first(c, 1):
                    pool.wait_ge(s["att_back"], c.n)
                hs = slice(half * HPC, (half + 1) * HPC)
                G.tensor_tensor(att_n[:, hs, :], att_sum[:, :, :],
                                rden[:, hs].unsqueeze(2).to_broadcast([P, HPC, HD]), ALU.mult)\
                    .then_inc(s["att_norm"], 1)

            def shares(c):
                row1, row2 = x2_row[c.r % 2]
                pool.wait_ge(s["gap_exp"], c.n + 1)
                ch = Chain(pool, s["share_chain"], SHARE * c.n)
                ch.link(G.tensor_tensor(gap_s[:, :], gap_e[:, :], one_c, ALU.add))
                ch.link(G.tensor_tensor(row1[:, C:C + 1], gap_s[:, :], minus_one, ALU.pow))
                G.tensor_tensor(row2[:, C:C + 1], gap_e[:, :], row1[:, C:C + 1], ALU.mult)
                G.tensor_tensor(row1[:, C + 1:C + 2], tok[:, :], one_c, ALU.mult)
                ch.link(G.tensor_tensor(row2[:, C + 1:C + 2], tok[:, :], one_c, ALU.mult))
                G.tensor_tensor(tok[:, :], tok[:, :], t_c, ALU.add).then_inc(s["shared"], 1)
                pool.wait_ge(s["shared"], c.n + 1)

            def xc_low(c):
                pool.wait_ge(s["xc_high"], c.n + 1)
                flat = "p a k t -> p (a k t)"
                G.tensor_tensor(xc_lo[:, :, :, :].rearrange(flat), xcT[:, :, :, :].rearrange(flat),
                                xc_hi[:, :, :, :].bitcast(f32).rearrange(flat), ALU.subtract)\
                    .then_inc(s["xc_low"], 1)

            def rstd(out_ap, var_ap, wait, done, c):
                pool.wait_ge(s[wait], c.n + 1)
                G.tensor_tensor(out_ap, var_ap, half_neg[:, 0:1], ALU.pow).then_inc(s[done], 1)

            def x1_bo_(c):
                pool.wait_ge(s["x1_done"], c.n + 1)
                if not first(c, 4):
                    pool.wait_ge(s["ln2_chain"], LN2 * (c.n - 4) + 1)
                G.tensor_tensor(x1_bo[c.r][:, :], x1[:, :], bo_s[:, :], ALU.add).then_inc(s["x1_bo_done"], 1)

            def send(c):
                pool.wait_ge(s["placed"], c.n + 1)
                apart(pool)
                pool.wait_ge(s["x2_again"], c.n + 1)
                apart(pool)
                for k in range(2):
                    G.indirect_dma_start(sent_flat, bass.IndirectOffsetOnAxis(pos[c.r % 2][:, k:k + 1], 0),
                                         x2_row[c.r % 2][k][:, :], None).then_inc(s_sent[c.r % 2], 16)

            def run(stage, c, *more):
                if c.exists():
                    stage(c, *more)

            def step(loop, k):
                run(xc_low, At(loop, k + 1))
                if At(loop, k - 4).exists():
                    rstd(l2rstd[:, :], l2var[:, :], "ln2_var", "ln2_rstd", At(loop, k - 4))
                run(att_norm, At(loop, k - 3), 0)
                run(gn_coef, At(loop, k - 1))
                run(att_norm, At(loop, k - 3), 1)
                if At(loop, k - 1).exists():
                    rstd(l1rstd[:, :], l1var[:, :], "ln1_var", "ln1_rstd", At(loop, k - 1))
                run(shares, At(loop, k - 4))
                run(x1_bo_, At(loop, k - 1))
                run(v_parts, At(loop, k + 1))
                run(send, At(loop, k - 4))

            for m in (q_mask[1], k_mask[0], k_mask[1]):
                if m is k_mask[1]:
                    xc_low(At(0, 0))
                G.memset(m[:, :, :, :].bitcast(f32), 0.0).then_inc(s["masks_cleared"], 1)
            pool.wait_ge(s["consts"], 16 * CONSTS)
            v_parts(At(0, 0))
            for k in range(LEAD):
                step(0, k)
            with pool.Fori(LEAD // ROUND, B // ROUND - 1) as loop:
                for k in range(ROUND):
                    step(loop, k)
            for k in range(B - ROUND, B + DRAIN):
                step(0, k)
            G.dma_start(total[N_TOK:N_TOK + P, :], pad_row[:, 0:C]).then_inc(s_added, 16 * EVER)
            for par in range(2):
                pool.wait_ge(s_sent[par], 16 * B)
                pool.wait_ge(s_total[par], 16 * (B // 2))
            pool.wait_ge(s_pad, 16 * E)
            pool.wait_ge(s["tab_ready"], 1)

            def expert(e, par, has_next, has_after):
                n_slots = pool.value_load(tab_i[0:1, 0, ds(e, 1)], min_val=1, max_val=N_TOK // SLOT)
                before = pool.value_load(tab_i[0:1, 1, ds(e, 1)], min_val=0, max_val=(2 * N_TOK) // SLOT + E)
                with pool.Fori(0, n_slots) as i:
                    g = before + i
                    for half in range(HALVES):
                        pool.wait_ge(s["y_biased"], HALVES * g + half + 1 + EVER)
                        apart(pool)
                        G.tensor_scalar(y_w[:, half, :], y_b[:, half, :], meta[:, half, 0:1], None, ALU.mult)\
                            .then_inc(s["y_weighted"], 1)
                        pool.wait_ge(s["y_weighted"], HALVES * g + half + 1)
                        pool.wait_ge(s_added, 16 * (HALVES * g + half + EVER))
                        apart(pool)
                        G.indirect_dma_start(total, bass.IndirectOffsetOnAxis(meta_i[:, half:half + 1], 0),
                                             y_w[:, half, :], None, compute_op=ALU.add).then_inc(s_added, 16)

            experts(pool, expert)
            for b in range(NLAST):
                pool.wait_ge(s["last_var"], b + 1)
                G.tensor_tensor(last_rs[:, b, :], last_ve[:, b, :], half_neg[:, 0:4], ALU.pow)\
                    .then_inc(s["last_rstd_raw"], 1)


def shape_constants():
    gamma = 1.0 - 2.0 ** (-5.0 - np.arange(NH, dtype=np.float64))
    t = np.arange(T)
    diff = t[None, :] - t[:, None]
    power = np.where(diff >= 0, gamma[:, None, None] ** np.maximum(diff, 0), 0.0)
    decay = np.ascontiguousarray(power.transpose(1, 0, 2)).astype(np.float32)
    p = np.arange(P)
    small = np.zeros((P, 2 * P + 32 + ROW), np.float32)
    small[:, 0:P] = np.eye(P)
    small[:, P:2 * P] = 1.0 / P
    small[:, 2 * P:2 * P + 4] = EPS, -1.0, 1.0, float(T)
    small[:, 2 * P + 8:2 * P + 16] = np.arange(E) * CAP
    small[:, 2 * P + 16:2 * P + 24] = np.arange(E)
    small[:, 2 * P + 24] = p
    small[:, 2 * P + 25:2 * P + 29] = -0.5
    small[:, 2 * P + 32 + C + 1] = N_TOK + p
    bits = np.zeros((P, 4 * P), np.float32)
    bits[:, 0:P] = np.eye(P)
    bits[:, P:2 * P] = np.where(p[None, :] <= p[:, None], 0.0, NEG)
    bits[:, 2 * P:3 * P] = p[:, None] < p[None, :]
    bits[:, 3 * P:4 * P] = 1.0
    return decay, small, bits


def kernel(**inputs):
    import concourse.bacc as _bacc
    from concourse.bass_utils import run_bass_kernel_spmd as _run

    a = {k: np.asarray(v) for k, v in inputs.items()}
    kv = a["L0_attn_past_kv"]
    blocks = np.zeros((NCH, P, P), kv.dtype)
    for h in range(NH):
        at = (h % HPC) * HD
        blocks[h // HPC, at:at + HD, at:at + HD] = kv[h]

    def per_channel(v):
        return np.repeat(v, HD).reshape(NCH, P).T

    decay, small, bits = shape_constants()
    data = {
        "x": a["x"], "ctx_in": a["ctx_1024"], "kv_blocks": blocks, "w_qkv": a["L0_attn_W_qkv"],
        "gn_scale": per_channel(a["L0_attn_gn_weight"]), "gn_shift": per_channel(a["L0_attn_gn_bias"]),
        "wq_t": a["L0_xattn_Wq"].T, "wk_t": a["L0_xattn_Wk"].T, "wv_t": a["L0_xattn_Wv"].T,
        "wo_t": a["L0_xattn_Wo"].T, "bo": a["L0_xattn_bo"], "router_t": a["L0_ffn_router_w"].T,
        "w_fc": a["L0_ffn_w_fc"],
        "b_fc": a["L0_ffn_b_fc"].reshape(E, HC, P).transpose(2, 0, 1),
        "w_proj": a["L0_ffn_w_proj"], "b_proj": a["L0_ffn_b_proj"],
        "decay_c": decay, "small_c": small, "bits_c": bits,
    }
    nc = _bacc.Bacc("TRN2", target_bir_lowering=False, num_devices=1)
    arrays, args = {}, []
    for name, v in data.items():
        v = np.ascontiguousarray(v)
        arrays[f"in_{name}"] = v
        args.append(nc.dram_tensor(f"in_{name}", v.shape, mybir.dt.from_np(v.dtype), kind="ExternalInput").ap())
    out = nc.dram_tensor("result", (B, T, C), mybir.dt.float32, kind="ExternalOutput").ap()
    decoder_kernel(nc, *args, out)
    r = _run(nc, [arrays], core_ids=[0])
    return r.results[0]["result"]
```
